# Optimizing a Trainium2 kernel written in Bass

```python
import numpy as np
import jax
import jax.numpy as jnp

def _softmax(x, axis=-1):
    return jax.nn.softmax(x, axis=axis)

def _gelu(x):
    return jax.nn.gelu(x, approximate=True)

def _silu(x):
    return jax.nn.silu(x)

def _sigmoid(x):
    return jax.nn.sigmoid(x)

def _layernorm(x, axis=-1, eps=1e-05):
    m = jnp.mean(x, axis=axis, keepdims=True)
    v = jnp.var(x, axis=axis, keepdims=True)
    return (x - m) / jnp.sqrt(v + eps)

def _scatter_add(tgt, idx, src, axis=0):
    return tgt.at[idx].add(src)

def _segment_sum(src, seg, n):
    return jax.ops.segment_sum(src, seg, n)
kernel_name = 'mk_early_fusion_embed_d2_tok_img1024_r4_8f9b59'

def setup_inputs(seed: int=0):
    np.random.seed(seed)
    _w = jnp.asarray

    def _rec_inputs():
        import jax
        import jax.numpy as jnp
        _rk = jax.random.key(seed)
        x = -0.000222058 + 0.999998 * jax.random.normal(jax.random.fold_in(_rk, 1), (16, 3, 128, 128), jnp.float32)
        x_txt = jax.random.randint(jax.random.fold_in(_rk, 51), (16, 77), 0, 7999, jnp.int32)
        return (x, x_txt)
    x, x_txt = _rec_inputs()

    def _L0_tok_setup():
        import jax, jax.numpy as jnp
        import numpy as np
        P = 16
        C = 3
        D = 256

        def _patchify(x, p):
            B, Cc, H, W = x.shape
            gh, gw = (H // p, W // p)
            x = x.reshape(B, Cc, gh, p, gw, p)
            x = x.transpose(0, 2, 4, 1, 3, 5)
            return x.reshape(B, gh * gw, Cc * p * p)
        key = jax.random.key(seed)
        k1, k2, k3, k4, k5 = jax.random.split(key, 5)
        patch_dim = C * P * P
        s1 = 1.0 / np.sqrt(patch_dim)
        s2 = 1.0 / np.sqrt(D)
        return {'x': jax.random.normal(k1, (32, C, 128, 128), dtype=jnp.float32), 'W1': jax.random.uniform(k2, (patch_dim, D), jnp.float32, -s1, s1), 'b1': jax.random.uniform(k3, (D,), jnp.float32, -s1, s1), 'W2': jax.random.uniform(k4, (D, D), jnp.float32, -s2, s2), 'b2': jax.random.uniform(k5, (D,), jnp.float32, -s2, s2)}
    _L0_tok_all = _L0_tok_setup()
    _L0_tok_in = {k: v for k, v in _L0_tok_all.items() if k in ('W1', 'b1', 'W2', 'b2')}
    del _L0_tok_all

    def _L0_txt_setup():
        import jax, jax.numpy as jnp
        import numpy as np
        VOCAB = 8000
        DIM = 256
        PADDING_IDX = 0
        key = jax.random.key(seed)
        k_tok, k_w = jax.random.split(key)
        tokens = jax.random.randint(k_tok, (8, 512), 0, VOCAB, dtype=jnp.int64)
        weight = jax.random.normal(k_w, (VOCAB, DIM), dtype=jnp.float32)
        weight = weight.at[PADDING_IDX].set(0.0)
        return {'tokens': tokens, 'weight': weight}
    _L0_txt_all = _L0_txt_setup()
    _L0_txt_in = {k: v for k, v in _L0_txt_all.items() if k in ('weight',)}
    del _L0_txt_all

    def _L0_attn_setup():
        import jax, jax.numpy as jnp
        import numpy as np
        from jax import lax
        B, L, D, K = (4, 1024, 256, 3)
        H = 512

        def _layernorm(h, g, b):
            m = jnp.mean(h, axis=-1, keepdims=True)
            v = jnp.mean((h - m) ** 2, axis=-1, keepdims=True)
            return (h - m) / jnp.sqrt(v + 1e-05) * g + b
        key = jax.random.key(seed)
        ks = jax.random.split(key, 16)
        s = 0.02
        return {'x': jax.random.normal(ks[0], (B, L, D), jnp.float32), 'ln1_g': jnp.ones((D,), jnp.float32), 'ln1_b': jnp.zeros((D,), jnp.float32), 'in_W': jax.random.normal(ks[1], (D, 2 * D), jnp.float32) * s, 'in_b': jnp.zeros((2 * D,), jnp.float32), 'dw_W': jax.random.normal(ks[2], (D, 1, K), jnp.float32) * s, 'dw_b': jnp.zeros((D,), jnp.float32), 'dt_W': jax.random.normal(ks[3], (D, D), jnp.float32) * s, 'dt_b': jnp.zeros((D,), jnp.float32), 'b_W': jax.random.normal(ks[4], (D, D), jnp.float32) * s, 'b_b': jnp.zeros((D,), jnp.float32), 'c_W': jax.random.normal(ks[5], (D, D), jnp.float32) * s, 'c_b': jnp.zeros((D,), jnp.float32), 'a_log': jnp.zeros((D,), jnp.float32), 'd_skip': jnp.ones((D,), jnp.float32), 'out_W': jax.random.normal(ks[6], (D, D), jnp.float32) * s, 'out_b': jnp.zeros((D,), jnp.float32), 'ln2_g': jnp.ones((D,), jnp.float32), 'ln2_b': jnp.zeros((D,), jnp.float32), 'f1_W': jax.random.normal(ks[7], (D, H), jnp.float32) * s, 'f1_b': jnp.zeros((H,), jnp.float32), 'f2_W': jax.random.normal(ks[8], (H, D), jnp.float32) * s, 'f2_b': jnp.zeros((D,), jnp.float32)}
    _L0_attn_all = _L0_attn_setup()
    _L0_attn_in = {k: v for k, v in _L0_attn_all.items() if k in ('ln1_g', 'ln1_b', 'in_W', 'in_b', 'dw_W', 'dw_b', 'dt_W', 'dt_b', 'b_W', 'b_b', 'c_W', 'c_b', 'a_log', 'd_skip', 'out_W', 'out_b', 'ln2_g', 'ln2_b', 'f1_W', 'f1_b', 'f2_W', 'f2_b')}
    del _L0_attn_all

    def _L0_ffn_setup():
        import jax, jax.numpy as jnp
        import numpy as np
        HIDDEN = 256
        INNER = 1024

        def _weight_quant(w):
            scale = 1.0 / jnp.clip(jnp.mean(jnp.abs(w)), 1e-05)
            wq = jnp.clip(jnp.round(w * scale), -1.0, 1.0) / scale
            return w + jax.lax.stop_gradient(wq - w)

        def _act_quant(x):
            scale = 127.0 / jnp.clip(jnp.max(jnp.abs(x), axis=-1, keepdims=True), 1e-05)
            xq = jnp.clip(jnp.round(x * scale), -128.0, 127.0) / scale
            return x + jax.lax.stop_gradient(xq - x)

        def _bitlinear(x, w):
            return jnp.einsum('bsi,oi->bso', _act_quant(x), _weight_quant(w))
        key = jax.random.key(seed)
        k0, k1, k2, k3 = jax.random.split(key, 4)
        x = jax.random.normal(k0, (4, 512, HIDDEN), dtype=jnp.float32)
        w_gate = jax.random.normal(k1, (INNER, HIDDEN), dtype=jnp.float32) / np.sqrt(HIDDEN)
        w_up = jax.random.normal(k2, (INNER, HIDDEN), dtype=jnp.float32) / np.sqrt(HIDDEN)
        w_down = jax.random.normal(k3, (HIDDEN, INNER), dtype=jnp.float32) / np.sqrt(INNER)
        return {'x': x, 'w_gate': w_gate, 'w_up': w_up, 'w_down': w_down}
    _L0_ffn_all = _L0_ffn_setup()
    _L0_ffn_in = {k: v for k, v in _L0_ffn_all.items() if k in ('w_gate', 'w_up', 'w_down')}
    del _L0_ffn_all

    def _L1_attn_setup():
        import jax, jax.numpy as jnp
        import numpy as np
        H = 16
        LN_EPS = 1e-05
        key = jax.random.key(seed)
        ks = jax.random.split(key, 10)
        B, N, D = (2, 512, 256)
        s = 1.0 / np.sqrt(D).astype(np.float32)
        x = jax.random.normal(ks[0], (B, N, D), jnp.float32)
        Wq = jax.random.normal(ks[1], (D, D), jnp.float32) * s
        Wk = jax.random.normal(ks[2], (D, D), jnp.float32) * s
        Wv = jax.random.normal(ks[3], (D, D), jnp.float32) * s
        Wo = jax.random.normal(ks[4], (D, D), jnp.float32) * s
        bq = jnp.zeros((D,), jnp.float32)
        bk = jnp.zeros((D,), jnp.float32)
        bv = jnp.zeros((D,), jnp.float32)
        bo = jnp.zeros((D,), jnp.float32)
        beta = jnp.ones((H,), jnp.float32)
        t = jnp.ones((H,), jnp.float32)
        ln_w = jnp.ones((D,), jnp.float32)
        ln_b = jnp.zeros((D,), jnp.float32)
        return {'x': x, 'Wq': Wq, 'bq': bq, 'Wk': Wk, 'bk': bk, 'Wv': Wv, 'bv': bv, 'Wo': Wo, 'bo': bo, 'beta': beta, 't': t, 'ln_w': ln_w, 'ln_b': ln_b}
    _L1_attn_all = _L1_attn_setup()
    _L1_attn_in = {k: v for k, v in _L1_attn_all.items() if k in ('Wq', 'bq', 'Wk', 'bk', 'Wv', 'bv', 'Wo', 'bo', 'beta', 't', 'ln_w', 'ln_b')}
    del _L1_attn_all

    def _L1_ffn_setup():
        import jax, jax.numpy as jnp
        import numpy as np
        NUM_EXPERTS = 8
        TOP_K = 2
        CAP_RATIO = 1.25
        INIT_STD = 0.02
        key = jax.random.key(seed)
        k1, k2, k3, k4 = jax.random.split(key, 4)
        B, T, H, F = (4, 512, 256, 1024)
        x = jax.random.normal(k1, (B, T, H), jnp.float32)
        router_w = jax.random.normal(k2, (NUM_EXPERTS, H), jnp.float32) * INIT_STD
        w1 = jax.random.normal(k3, (NUM_EXPERTS, H, F), jnp.float32) * INIT_STD
        w2 = jax.random.normal(k4, (NUM_EXPERTS, F, H), jnp.float32) * INIT_STD
        return {'x': x, 'router_w': router_w, 'w1': w1, 'w2': w2}
    _L1_ffn_all = _L1_ffn_setup()
    _L1_ffn_in = {k: v for k, v in _L1_ffn_all.items() if k in ('router_w', 'w1', 'w2')}
    del _L1_ffn_all
    return {'x': x, 'x_txt': x_txt, 'L0_tok_W1': _L0_tok_in['W1'], 'L0_tok_b1': _L0_tok_in['b1'], 'L0_tok_W2': _L0_tok_in['W2'], 'L0_tok_b2': _L0_tok_in['b2'], 'L0_txt_weight': _L0_txt_in['weight'], 'L0_attn_ln1_g': _L0_attn_in['ln1_g'], 'L0_attn_ln1_b': _L0_attn_in['ln1_b'], 'L0_attn_in_W': _L0_attn_in['in_W'], 'L0_attn_in_b': _L0_attn_in['in_b'], 'L0_attn_dw_W': _L0_attn_in['dw_W'], 'L0_attn_dw_b': _L0_attn_in['dw_b'], 'L0_attn_dt_W': _L0_attn_in['dt_W'], 'L0_attn_dt_b': _L0_attn_in['dt_b'], 'L0_attn_b_W': _L0_attn_in['b_W'], 'L0_attn_b_b': _L0_attn_in['b_b'], 'L0_attn_c_W': _L0_attn_in['c_W'], 'L0_attn_c_b': _L0_attn_in['c_b'], 'L0_attn_a_log': _L0_attn_in['a_log'], 'L0_attn_d_skip': _L0_attn_in['d_skip'], 'L0_attn_out_W': _L0_attn_in['out_W'], 'L0_attn_out_b': _L0_attn_in['out_b'], 'L0_attn_ln2_g': _L0_attn_in['ln2_g'], 'L0_attn_ln2_b': _L0_attn_in['ln2_b'], 'L0_attn_f1_W': _L0_attn_in['f1_W'], 'L0_attn_f1_b': _L0_attn_in['f1_b'], 'L0_attn_f2_W': _L0_attn_in['f2_W'], 'L0_attn_f2_b': _L0_attn_in['f2_b'], 'L0_ffn_w_gate': _L0_ffn_in['w_gate'], 'L0_ffn_w_up': _L0_ffn_in['w_up'], 'L0_ffn_w_down': _L0_ffn_in['w_down'], 'L1_attn_Wq': _L1_attn_in['Wq'], 'L1_attn_bq': _L1_attn_in['bq'], 'L1_attn_Wk': _L1_attn_in['Wk'], 'L1_attn_bk': _L1_attn_in['bk'], 'L1_attn_Wv': _L1_attn_in['Wv'], 'L1_attn_bv': _L1_attn_in['bv'], 'L1_attn_Wo': _L1_attn_in['Wo'], 'L1_attn_bo': _L1_attn_in['bo'], 'L1_attn_beta': _L1_attn_in['beta'], 'L1_attn_t': _L1_attn_in['t'], 'L1_attn_ln_w': _L1_attn_in['ln_w'], 'L1_attn_ln_b': _L1_attn_in['ln_b'], 'L1_ffn_router_w': _L1_ffn_in['router_w'], 'L1_ffn_w1': _L1_ffn_in['w1'], 'L1_ffn_w2': _L1_ffn_in['w2']}

def reference(x, x_txt, L0_tok_W1, L0_tok_b1, L0_tok_W2, L0_tok_b2, L0_txt_weight, L0_attn_ln1_g, L0_attn_ln1_b, L0_attn_in_W, L0_attn_in_b, L0_attn_dw_W, L0_attn_dw_b, L0_attn_dt_W, L0_attn_dt_b, L0_attn_b_W, L0_attn_b_b, L0_attn_c_W, L0_attn_c_b, L0_attn_a_log, L0_attn_d_skip, L0_attn_out_W, L0_attn_out_b, L0_attn_ln2_g, L0_attn_ln2_b, L0_attn_f1_W, L0_attn_f1_b, L0_attn_f2_W, L0_attn_f2_b, L0_ffn_w_gate, L0_ffn_w_up, L0_ffn_w_down, L1_attn_Wq, L1_attn_bq, L1_attn_Wk, L1_attn_bk, L1_attn_Wv, L1_attn_bv, L1_attn_Wo, L1_attn_bo, L1_attn_beta, L1_attn_t, L1_attn_ln_w, L1_attn_ln_b, L1_ffn_router_w, L1_ffn_w1, L1_ffn_w2):
    import jax
    import jax.numpy as jnp

    def _L0_tok_ref(x, W1, b1, W2, b2):
        import jax, jax.numpy as jnp
        import numpy as np
        P = 16
        C = 3
        D = 256

        def _patchify(x, p):
            B, Cc, H, W = x.shape
            gh, gw = (H // p, W // p)
            x = x.reshape(B, Cc, gh, p, gw, p)
            x = x.transpose(0, 2, 4, 1, 3, 5)
            return x.reshape(B, gh * gw, Cc * p * p)
        patches = _patchify(x, P)
        h = jax.nn.silu(jnp.einsum('blk,kd->bld', patches, W1) + b1)
        return jnp.einsum('bld,de->ble', h, W2) + b2

    def _L0_txt_ref(tokens, weight):
        import jax, jax.numpy as jnp
        import numpy as np
        VOCAB = 8000
        DIM = 256
        PADDING_IDX = 0
        return jnp.take(weight, tokens, axis=0)

    def _L0_attn_ref(x, ln1_g, ln1_b, in_W, in_b, dw_W, dw_b, dt_W, dt_b, b_W, b_b, c_W, c_b, a_log, d_skip, out_W, out_b, ln2_g, ln2_b, f1_W, f1_b, f2_W, f2_b):
        import jax, jax.numpy as jnp
        import numpy as np
        from jax import lax
        B, L, D, K = (4, 1024, 256, 3)
        H = 512

        def _layernorm(h, g, b):
            m = jnp.mean(h, axis=-1, keepdims=True)
            v = jnp.mean((h - m) ** 2, axis=-1, keepdims=True)
            return (h - m) / jnp.sqrt(v + 1e-05) * g + b
        nx = _layernorm(x, ln1_g, ln1_b)
        proj = nx @ in_W + in_b
        x_proj, gate = jnp.split(proj, 2, axis=-1)
        xt = jnp.transpose(x_proj, (0, 2, 1))
        mixed = lax.conv_general_dilated(xt, dw_W, window_strides=(1,), padding=[(K // 2, K // 2)], dimension_numbers=('NCH', 'OIH', 'NCH'), feature_group_count=D)
        mixed = jnp.transpose(mixed + dw_b[None, :, None], (0, 2, 1))
        dt = jax.nn.softplus(mixed @ dt_W + dt_b)
        bt = jnp.tanh(mixed @ b_W + b_b)
        ct = jnp.tanh(mixed @ c_W + c_b)
        a = -jnp.exp(a_log)

        def step(state, inp):
            dt_t, b_t, c_t, m_t, g_t = inp
            decay = jnp.exp(dt_t * a)
            state = decay * state + dt_t * b_t * m_t
            y_t = c_t * state + d_skip * m_t
            return (state, y_t * jax.nn.sigmoid(g_t))
        seqs = tuple((jnp.transpose(t, (1, 0, 2)) for t in (dt, bt, ct, mixed, gate)))
        state0 = jnp.zeros((x.shape[0], x.shape[2]), x.dtype)
        _, ys = lax.scan(step, state0, seqs)
        y = jnp.transpose(ys, (1, 0, 2))
        x2 = x + y @ out_W + out_b
        h = _layernorm(x2, ln2_g, ln2_b)
        ffn = jax.nn.gelu(h @ f1_W + f1_b, approximate=False) @ f2_W + f2_b
        return x2 + ffn

    def _L0_ffn_ref(x, w_gate, w_up, w_down):
        import jax, jax.numpy as jnp
        import numpy as np
        HIDDEN = 256
        INNER = 1024

        def _weight_quant(w):
            scale = 1.0 / jnp.clip(jnp.mean(jnp.abs(w)), 1e-05)
            wq = jnp.clip(jnp.round(w * scale), -1.0, 1.0) / scale
            return w + jax.lax.stop_gradient(wq - w)

        def _act_quant(x):
            scale = 127.0 / jnp.clip(jnp.max(jnp.abs(x), axis=-1, keepdims=True), 1e-05)
            xq = jnp.clip(jnp.round(x * scale), -128.0, 127.0) / scale
            return x + jax.lax.stop_gradient(xq - x)

        def _bitlinear(x, w):
            return jnp.einsum('bsi,oi->bso', _act_quant(x), _weight_quant(w))
        gate = jax.nn.silu(_bitlinear(x, w_gate))
        up = _bitlinear(x, w_up)
        return _bitlinear(gate * up, w_down)

    def _L1_attn_ref(x, Wq, bq, Wk, bk, Wv, bv, Wo, bo, beta, t, ln_w, ln_b):
        import jax, jax.numpy as jnp
        import numpy as np
        H = 16
        LN_EPS = 1e-05
        B, N, D = x.shape
        dh = D // H

        def proj(W, b):
            return (x @ W.T + b).reshape(B, N, H, dh).transpose(0, 2, 1, 3)
        Q, K, V = (proj(Wq, bq), proj(Wk, bk), proj(Wv, bv))
        S = jnp.einsum('bhnd,bhmd->bhnm', Q, K) / dh ** 0.5
        W_tau = jax.nn.softmax(S, axis=-1)
        b_ = beta.reshape(1, H, 1, 1)
        t_ = t.reshape(1, H, 1, 1)
        W_sigma = 1.0 / ((1.0 + jnp.abs(S) / b_) ** 2 + t_ ** 2)
        W_sigma = W_sigma / W_sigma.sum(axis=-1, keepdims=True)
        tau = jnp.einsum('bhnm,bhmd->bhnd', W_tau, V).transpose(0, 2, 1, 3).reshape(B, N, D)
        sigma = jnp.einsum('bhnm,bhmd->bhnd', W_sigma, V).transpose(0, 2, 1, 3).reshape(B, N, D)
        f = 0.5 * tau + 0.5 * sigma
        y = f @ Wo.T + bo
        mu = y.mean(axis=-1, keepdims=True)
        var = jnp.mean((y - mu) ** 2, axis=-1, keepdims=True)
        out = x + ln_w * (y - mu) * jax.lax.rsqrt(var + LN_EPS) + ln_b
        return out

    def _L1_ffn_ref(x, router_w, w1, w2):
        import jax, jax.numpy as jnp
        import numpy as np
        NUM_EXPERTS = 8
        TOP_K = 2
        CAP_RATIO = 1.25
        INIT_STD = 0.02
        B, T, H = x.shape
        E, K = (NUM_EXPERTS, TOP_K)
        xf = x.reshape(-1, H)
        N = xf.shape[0]
        P = N * K
        capacity = int(CAP_RATio * N * K / E) + 1 if False else int(CAP_RATIO * N * K / E) + 1
        logits = xf @ router_w.T
        probs = jax.nn.softmax(logits, axis=-1)
        k_probs, k_idx = jax.lax.top_k(probs, K)
        k_probs = k_probs / jnp.sum(k_probs, axis=-1, keepdims=True)
        flat_e = k_idx.reshape(-1)
        onehot = jax.nn.one_hot(flat_e, E, dtype=jnp.int32)
        rank = jnp.take_along_axis(jnp.cumsum(onehot, axis=0) - 1, flat_e[:, None], axis=1)[:, 0]
        keep = rank < capacity
        slot = jnp.minimum(rank, capacity - 1)
        token_id = jnp.arange(P) // K
        dispatched = jnp.where(keep[:, None], xf[token_id], 0.0)
        buf = jnp.zeros((E, capacity, H), x.dtype).at[flat_e, slot].add(dispatched)
        h = jax.nn.silu(jnp.einsum('ech,ehf->ecf', buf, w1))
        out_buf = jnp.einsum('ecf,efh->ech', h, w2)
        pair_out = out_buf[flat_e, slot] * keep[:, None].astype(x.dtype)
        combined = jnp.sum(pair_out.reshape(N, K, H) * k_probs[..., None], axis=1)
        return combined.reshape(B, T, H) + x
    h = _L0_tok_ref(x, L0_tok_W1, L0_tok_b1, L0_tok_W2, L0_tok_b2)
    h = jnp.concatenate([h, _L0_txt_ref(x_txt, L0_txt_weight)], axis=1)
    h = h + _L0_attn_ref(_layernorm(h, axis=-1), L0_attn_ln1_g, L0_attn_ln1_b, L0_attn_in_W, L0_attn_in_b, L0_attn_dw_W, L0_attn_dw_b, L0_attn_dt_W, L0_attn_dt_b, L0_attn_b_W, L0_attn_b_b, L0_attn_c_W, L0_attn_c_b, L0_attn_a_log, L0_attn_d_skip, L0_attn_out_W, L0_attn_out_b, L0_attn_ln2_g, L0_attn_ln2_b, L0_attn_f1_W, L0_attn_f1_b, L0_attn_f2_W, L0_attn_f2_b)
    h = h + _L0_ffn_ref(_layernorm(h, axis=-1), L0_ffn_w_gate, L0_ffn_w_up, L0_ffn_w_down)
    h = h + _L1_attn_ref(_layernorm(h, axis=-1), L1_attn_Wq, L1_attn_bq, L1_attn_Wk, L1_attn_bk, L1_attn_Wv, L1_attn_bv, L1_attn_Wo, L1_attn_bo, L1_attn_beta, L1_attn_t, L1_attn_ln_w, L1_attn_ln_b)
    h = h + _L1_ffn_ref(_layernorm(h, axis=-1), L1_ffn_router_w, L1_ffn_w1, L1_ffn_w2)
    return h

_drawn_inputs = setup_inputs


def setup_inputs(seed=0):
    import zlib

    import numpy as np

    out = dict(_drawn_inputs(seed))
    spreads = {'L0_attn_ln1_g': (1.0, 0.6),
     'L0_attn_ln1_b': (0.0, 0.8),
     'L0_attn_in_b': (0.0, 0.8),
     'L0_attn_dw_b': (0.0, 0.404),
     'L0_attn_dt_b': (0.0, 0.8),
     'L0_attn_b_b': (0.0, 0.8),
     'L0_attn_c_b': (0.0, 0.8),
     'L0_attn_a_log': (0.0, 0.8),
     'L0_attn_d_skip': (1.0, 0.6),
     'L0_attn_out_b': (0.0, 0.1),
     'L0_attn_ln2_g': (1.0, 0.6),
     'L0_attn_ln2_b': (0.0, 0.8),
     'L0_attn_f1_b': (0.0, 0.3),
     'L0_attn_f2_b': (0.0, 0.1),
     'L1_attn_bq': (0.0, 0.59),
     'L1_attn_bk': (0.0, 0.8),
     'L1_attn_bv': (0.0, 0.1),
     'L1_attn_bo': (0.0, 0.1),
     'L1_attn_beta': (1.0, 0.6),
     'L1_attn_t': (1.0, 0.6),
     'L1_attn_ln_w': (1.0, 0.2),
     'L1_attn_ln_b': (0.0, 0.1)}
    factors = {'L0_attn_in_W': 8.0,
     'L0_attn_dw_W': 8.0,
     'L0_attn_dt_W': 8.0,
     'L0_attn_b_W': 8.0,
     'L0_attn_c_W': 8.0,
     'L0_attn_out_W': 3.115,
     'L1_ffn_router_w': 3.545,
     'L1_ffn_w1': 3.133,
     'L1_ffn_w2': 3.107}
    for name, (base, spread) in spreads.items():
        noise = np.random.default_rng([zlib.crc32(name.encode()), seed]).standard_normal(out[name].shape)
        drawn = base * np.exp(spread * noise) if base else spread * noise
        out[name] = jnp.asarray(drawn.astype(out[name].dtype))
    for name, factor in factors.items():
        out[name] = (out[name] * factor).astype(out[name].dtype)
    return out
```

```python
from contextlib import ExitStack, contextmanager

import concourse.bass as bass
from concourse import mybir
from concourse.bass import ds

F32 = mybir.dt.float32
BF16 = mybir.dt.bfloat16
I32 = mybir.dt.int32
U32 = mybir.dt.uint32
ALU = mybir.AluOpType
ACT = mybir.ActivationFunctionType
AX = mybir.AxisListType

P = 128
B, IMG, TXT = 16, 64, 77
L = IMG + TXT
N = B * L
NT = -(-N // P)
NP = NT * P
D = 256
DM = D // P
TC = 3
NCH = NT // TC
CW = TC * P
KP = 768 // P
BPI = 2
SW = BPI * L
F1 = 512
INNER = 1024
FM = INNER // P
HEADS, DH = 16, 16
HG = 8
NKC = -(-L // DH)
LAST0 = L - DH
DUP = (NKC - 1) * DH - LAST0
KB = 3
E = 8
CAP = int(1.25 * N * 2 / E) + 1
CT = 6
CR = -(-CAP // CT)
CAPP = CT * CR
SLOTS = E * CAPP
TRASH = SLOTS
EPS = 1e-5
MAGIC = 12582912.0

VEC = {}
for _name, _n in (("in_b", 4), ("dw0", 2), ("dw1", 2), ("dw2", 2), ("dw_b", 2), ("dt_b", 2), ("b_b", 2),
                  ("c_b", 2), ("a_log", 2), ("d_skip", 2), ("ln1_g", 2), ("ln1_b", 2), ("ln2_g", 2),
                  ("ln2_b", 2), ("f1_b", 4), ("tb1", 2), ("bq", 2), ("bk", 2), ("beta", 2), ("t", 2)):
    VEC[_name] = (sum(n for _, n in VEC.values()), _n)
NV = sum(n for _, n in VEC.values())
ROWS = ("out_b", "f2_b", "bv", "bo", "ln_w", "ln_b")


FFN_WEIGHTS = ("w_gate", "w_up", "w_down")


def pipelined(eng, n, u, front, back):
    front(0, 0)
    with eng.Fori(0, n // u - 1) as i:
        for p in range(u):
            front(i + (p + 1) // u, (p + 1) % u)
            back(i, p)
    for p in range(u):
        if p + 1 < u:
            front(n // u - 1, p + 1)
        back(n // u - 1, p)


def overlapped(eng, n, u, step):
    step((0, 0), None)
    with eng.Fori(0, n // u - 1) as i:
        for p in range(u):
            step((i + (p + 1) // u, (p + 1) % u), (i, p))
    for p in range(u):
        step((n // u - 1, p + 1) if p + 1 < u else None, (n // u - 1, p))


class Steps:

    def __init__(self, eng, sem, i=0, per=0):
        self.eng, self.sem, self.base, self.per, self.n = eng, sem, i * per, per, 0

    def __call__(self, ins):
        ins.then_inc(self.sem, 1)
        self.n += 1

    def wait(self):
        self.eng.wait_ge(self.sem, self.base + self.n)

    def end(self):
        assert self.n == self.per, (self.n, self.per)


class Core:

    def __init__(self, nc, dram, ctx):
        self.nc, self.dram, self.sems = nc, dram, []

    def sb(self, ctx, name, shape, dt=F32):
        return ctx.enter_context(self.nc.sbuf_tensor(name, shape, dt))

    def sem(self, name):
        self.sems.append(self.nc.alloc_semaphore(name=name))
        return self.sems[-1]

    def settled(self, eng):
        eng.wait_ge(self.const_in, 48)

    def passed(self, eng):
        eng.sem_inc(self.waits_passed, 1)

    def vec(self, name, m):
        at, n = VEC[name]
        assert m < n
        return self.vecs[:, at + m:at + m + 1]


@contextmanager
def stage(k):
    k.sems = []
    with ExitStack() as c:
        yield c
    k.nc.clear_and_free_semaphores(k.sems)
    k.nc.all_engine_barrier()


def embed(k, ps):
    nc, dram = k.nc, k.dram
    with stage(k) as c:
        patches = k.sb(c, "patches", [P, KP, B * IMG])
        w1 = k.sb(c, "tok_w1", [P, KP, D])
        w2 = k.sb(c, "tok_w2", [P, DM, D])
        b2 = k.sb(c, "tok_b2", [1, D])
        imask = k.sb(c, "image_mask", [1, NP])
        tmask = k.sb(c, "text_mask", [P, NT])
        tok = k.sb(c, "token_ids", [P, NT], I32)
        h1 = k.sb(c, "h1", [P, DM, NP])
        rows = k.sb(c, "text_rows", [P, NT, D])
        vecs_in, small_in = k.sem("vecs_in"), k.sem("tok_small_in")
        patches_in = [k.sem(f"patches_in{n}") for n in range(2)]
        tok_in, gathered = k.sem("tok_in"), [k.sem(f"gathered{n}") for n in range(NCH)]
        cleared, hid, hid_out = k.sem("h1_cleared"), k.sem("hid_ready"), k.sem("hid_activated")
        emb, emb_out, half = k.sem("emb_ready"), k.sem("emb_out"), k.sem("half_bias")
        wf = {n: k.sb(c, n + "_f32", [P, DM * INNER]) for n in FFN_WEIGHTS}
        junk = k.sb(c, "abs_weights", [P, DM * INNER])
        asum = k.sb(c, "abs_sums", [P, 3])
        ones = k.sb(c, "ones", [P, P])
        wrec = k.sb(c, "inv_mean_abs", [P, 3])
        ffn_in = [k.sem(n + "_in") for n in FFN_WEIGHTS]
        zeros = k.sb(c, "zeros", [CR, CT, D])
        zeroed = k.sem("zeros_ready")
        summed, total, wq_steps = k.sem("abs_summed"), k.sem("abs_total"), k.sem("wq_steps")
        block = c.enter_context(nc.Block())

        @block.sync
        def _(sp):
            sp.dma_start(k.vecs[:], dram["vecs"]).then_inc(vecs_in, 16)
            sp.dma_start(w1[:], dram["tok_W1"]).then_inc(patches_in[0], 16)
            for n in range(2):
                sp.dma_start(patches[:, :, 512 * n:512 * n + 512],
                             dram["patches"][:, :, 512 * n:512 * n + 512]).then_inc(patches_in[n], 16)
            sp.dma_start(w2[:], dram["tok_W2"]).then_inc(small_in, 16)
            sp.dma_start(b2[:], dram["tok_b2"]).then_inc(small_in, 16)
            sp.dma_start(imask[:], dram["imask"]).then_inc(small_in, 16)
            sp.dma_start(tmask[:], dram["tmask"]).then_inc(small_in, 16)
            sp.wait_ge(zeroed, 1)
            for e in range(E):
                sp.dma_start(k.slots_dram[CAPP * e:CAPP * e + CAPP, :].rearrange("(t r) d -> r t d", r=CR),
                             zeros[:]).then_inc(k.zero_filled, 16)
            sp.dma_start(k.ident[:], dram["ident"]).then_inc(k.const_in, 16)
            sp.dma_start(k.triu[:], dram["triu"]).then_inc(k.const_in, 16)
            sp.dma_start(k.rows[:], dram["rows"]).then_inc(k.const_in, 16)
            for n, name in enumerate(FFN_WEIGHTS):
                sp.dma_start(wf[name][:], dram[name].rearrange("p a b -> p (a b)")).then_inc(ffn_in[n], 16)
            for name in WEIGHTS:
                sp.dma_start(k.weights[name][:], dram[name]).then_inc(k.weights_in, 16)

        @block.gpsimd
        def _(pool):
            pool.dma_start(tok[:], dram["tokens"]).then_inc(tok_in, 16)
            nc.gpsimd.memset(h1[:], 0.0).then_inc(cleared, 1)
            nc.gpsimd.memset(zeros[:], 0.0).then_inc(zeroed, 1)
            pool.wait_ge(tok_in, 16)
            for t in range(NT):
                nc.gpsimd.indirect_dma_start(
                    rows[:, t, :], None, dram["table"],
                    bass.IndirectOffsetOnAxis(ap=tok[:, t:t + 1], axis=0)).then_inc(gathered[t // TC], 16)

        @block.tensor
        def _(pe):
            for n in range(2):
                pe.wait_ge(patches_in[n], 16 * (2 - n))
                for m in range(DM):
                    for q in range(KP):
                        last = nc.tensor.matmul(ps[:, 2 * n + m, :], w1[:, q, m * P:m * P + P],
                                                patches[:, q, 512 * n:512 * n + 512],
                                                start=(q == 0), stop=(q == KP - 1))
                    last.then_inc(hid, 1)
            pe.wait_ge(hid_out, 2 * DM)
            pe.wait_ge(half, 4)
            pe.wait_ge(summed, 3)
            nc.tensor.matmul(ps[:, 0, 0:3], ones[:], asum[:], start=True, stop=True).then_inc(total, 1)
            pe.wait_ge(small_in, 64)
            for t in range(NT):
                if t >= 4:
                    pe.wait_ge(emb_out, t - 3)
                out = ps[:, 4 + t % 4, 0:D]
                for m in range(DM):
                    nc.tensor.matmul(out, h1[:, m, t * P:t * P + P], w2[:, m, :], start=(m == 0), stop=False)
                nc.tensor.matmul(out, imask[:, t * P:t * P + P], b2[:], start=False, stop=True).then_inc(emb, 1)

        @block.scalar
        def _(act):
            act.wait_ge(vecs_in, 16)
            act.wait_ge(cleared, 1)
            for n in range(2):
                for m in range(DM):
                    act.wait_ge(hid, 2 * n + m + 1)
                    dst = h1[:, m, 0:N].rearrange("p (b l) -> p b l", b=B)[:, 8 * n:8 * n + 8, 0:IMG]
                    nc.scalar.activation(dst, ps[:, 2 * n + m, :].rearrange("p (b l) -> p b l", b=8),
                                         ACT.Silu, bias=k.vec("tb1", m)).then_inc(hid_out, 1)
            for n, name in enumerate(FFN_WEIGHTS):
                act.wait_ge(ffn_in[n], 16)
                if n:
                    act.wait_ge(summed, n)
                nc.scalar.activation(junk[:], wf[name][:], ACT.Abs, accum_out=asum[:, n:n + 1]).then_inc(summed, 1)

        @block.vector
        def _(dve):
            dve.wait_ge(vecs_in, 16)
            at = VEC["in_b"][0]
            nc.vector.tensor_scalar(k.half_gate_b[:], k.vecs[:, at + 2:at + 4], 0.5, None, ALU.mult).then_inc(half, 1)
            dve.wait_ge(k.const_in, 48)
            nc.vector.tensor_copy(k.identb[:], k.ident[:]).then_inc(half, 1)
            nc.vector.memset(k.mhalf[:], -0.5).then_inc(half, 1)
            nc.vector.memset(ones[:], 1.0).then_inc(half, 1)
            dve.wait_ge(small_in, 64)
            for t in range(NT):
                dve.wait_ge(gathered[t // TC], 16 * TC)
                dve.wait_ge(emb, t + 1)
                nc.vector.scalar_tensor_tensor(k.H[:, t, :], rows[:, t, :], tmask[:, t:t + 1], ps[:, 4 + t % 4, 0:D],
                                               ALU.mult, ALU.add).then_inc(emb_out, 1)
            s = Steps(dve, wq_steps)
            dve.wait_ge(total, 1)
            s(nc.vector.tensor_scalar(k.wmean[:], ps[:, 0, 0:3], 1.0 / (D * INNER), 1e-5, ALU.mult, ALU.max))
            s.wait()
            s(nc.vector.reciprocal(wrec[:], k.wmean[:]))
            for op in range(3):
                s.wait()
                for n, name in enumerate(FFN_WEIGHTS):
                    w = wf[name][:]
                    if op == 0:
                        s(nc.vector.tensor_scalar(w, w, wrec[:, n:n + 1], 1.0, ALU.mult, ALU.min))
                    elif op == 1:
                        s(nc.vector.tensor_scalar(w, w, -1.0, MAGIC, ALU.max, ALU.add))
                    else:
                        s(nc.vector.tensor_scalar(k.wq[name][:].rearrange("p a b -> p (a b)"), w, MAGIC, None,
                                                  ALU.subtract))


def scan_norms(k, ps, nxT):
    nc = k.nc
    with stage(k) as c:
        st = k.sb(c, "s2_stats", [P, TC, 6])
        mv = k.sb(c, "s2_meanvar", [P, TC, 2])
        ve = k.sb(c, "s2_var_eps", [P, 2, TC])
        rs = k.sb(c, "s2_rstd", [P, 2, TC])
        nx = k.sb(c, "s2_nx", [P, TC, D])
        steps, var, rstd = k.sem("s2_steps"), k.sem("s2_var"), k.sem("s2_rstd_ready")
        normed, turned, stored = k.sem("s2_normed"), k.sem("s2_turned"), k.sem("s2_stored")
        block = c.enter_context(nc.Block())

        @block.vector
        def _(dve):
            nc.vector.sem_inc(turned, 1)
            with dve.Fori(0, NCH) as i:
                s = Steps(dve, steps, i, 3 * TC)
                for j in range(TC):
                    s(nc.vector.bn_stats(st[:, j, :], k.H[:, ds(TC * i + j, 1), :]))
                s.wait()
                k.passed(nc.vector)
                for j in range(TC):
                    s(nc.vector.bn_aggr(mv[:, j, :], st[:, j, :]))
                s.wait()
                nc.vector.tensor_scalar(ve[:, 0, :], mv[:, :, 1], EPS, None, ALU.add).then_inc(var, 1)
                nc.vector.tensor_scalar(ve[:, 1, :], mv[:, :, 1], 1.0 + EPS, EPS * EPS,
                                        ALU.mult, ALU.add).then_inc(var, 1)
                dve.wait_ge(rstd, i + 1)
                for j in range(TC):
                    s(nc.vector.tensor_scalar(k.X[:, ds(TC * i + j, 1), :], k.H[:, ds(TC * i + j, 1), :],
                                              mv[:, j, 0:1], rs[:, 0, j:j + 1], ALU.subtract, ALU.mult))
                dve.wait_ge(turned, i + 1)
                for j in range(TC):
                    nc.vector.tensor_scalar(nx[:, j, :], k.H[:, ds(TC * i + j, 1), :], mv[:, j, 0:1],
                                            rs[:, 1, j:j + 1], ALU.subtract, ALU.mult).then_inc(normed, 1)
                s.end()

        @block.gpsimd
        def _(pool):
            with pool.Fori(0, NCH) as i:
                pool.wait_ge(var, 2 * i + 2)
                nc.gpsimd.tensor_tensor(rs[:], ve[:], k.mhalf[:, 0:2 * TC].rearrange("p (a b) -> p a b", a=2),
                                        ALU.pow).then_inc(rstd, 1)

        @block.tensor
        def _(pe):
            nc.tensor.sem_inc(stored, 2)
            with pe.Fori(0, NCH) as i:
                pe.wait_ge(stored, 2 * i + 2)
                for j in range(TC):
                    pe.wait_ge(normed, TC * i + j + 1)
                    for m in range(DM):
                        last = nc.tensor.transpose(ps[:, m, j * P:j * P + P], nx[:, j, m * P:m * P + P], k.ident[:])
                last.then_inc(turned, 1)

        @block.scalar
        def _(act):
            with act.Fori(0, NCH) as i:
                act.wait_ge(turned, i + 2)
                for m in range(DM):
                    nc.scalar.activation(nxT[:, m, ds(CW * i, CW)], ps[:, m, 0:CW], ACT.Identity,
                                         bias=k.vec("ln1_b", m), scale=k.vec("ln1_g", m)).then_inc(stored, 1)


def selective_scan(k, ps, nxT, yT):
    nc = k.nc
    W = k.weights
    with stage(k) as c:
        xp = k.sb(c, "s3_conv_in", [P, DM, BPI, L + 2])
        mixed = k.sb(c, "s3_mixed", [P, DM, SW])
        gate = k.sb(c, "s3_gate", [P, DM, SW])
        az = k.sb(c, "s3_soft", [P, DM, SW])
        z = k.sb(c, "s3_z", [P, DM, SW])
        relu = k.sb(c, "s3_relu", [P, DM, SW])
        dt = k.sb(c, "s3_dt", [P, DM, SW])
        bt = k.sb(c, "s3_bt", [P, DM, SW])
        ct = k.sb(c, "s3_ct", [P, DM, SW])
        decay = k.sb(c, "s3_decay", [P, DM, SW])
        state = k.sb(c, "s3_state", [P, DM, SW])
        nega = k.sb(c, "s3_neg_a", [P, DM])
        a0 = k.sb(c, "s3_exp_a", [P, DM])
        names = ("padded", "nega", "a0", "proj", "xp", "gate", "mix_steps", "mixed", "bcd", "z", "relu", "soft", "dt",
                 "decay", "bt", "ct", "asteps", "dsteps", "scanned")
        (padded, nega_ready, a0_ready, proj, xp_ready, gate_ready, mix_steps, mixed_ready, bcd, z_ready, relu_ready,
         soft_ready, dt_ready, decay_ready, bt_ready, ct_ready, asteps, dsteps, scanned) = (k.sem("s3_" + n) for n in names)
        block = c.enter_context(nc.Block())

        @block.gpsimd
        def _(pool):
            nc.gpsimd.memset(xp[:], 0.0).then_inc(padded, 1)

        @block.tensor
        def _(pe):
            with pe.Fori(0, N // SW) as i:
                for m in range(4):
                    for q in range(DM):
                        last = nc.tensor.matmul(ps[:, m, 0:SW], W["in_W"][:, q, m * P:m * P + P],
                                                nxT[:, q, ds(SW * i, SW)], start=(q == 0), stop=(q == DM - 1))
                    last.then_inc(proj, 1)
                pe.wait_ge(mixed_ready, DM * i + DM)
                pe.wait_ge(gate_ready, DM * i + DM)
                for n, (w, bank) in enumerate((("dt_W", 4), ("b_W", 6), ("c_W", 0))):
                    for m in range(DM):
                        for q in range(DM):
                            last = nc.tensor.matmul(ps[:, bank + m, 0:SW], W[w][:, q, m * P:m * P + P],
                                                    mixed[:, q, :], start=(q == 0), stop=(q == DM - 1))
                        last.then_inc(bcd, 1)
                pe.wait_ge(ct_ready, DM * i + DM)

        @block.scalar
        def _(act):
            nc.scalar.activation(a0[:], k.vecs[:, VEC["a_log"][0]:VEC["a_log"][0] + DM], ACT.Exp).then_inc(a0_ready, 1)
            act.wait_ge(padded, 1)
            act.wait_ge(nega_ready, 1)
            with act.Fori(0, N // SW) as i:
                s = Steps(act, asteps, i, 1 + DM)
                for m in range(DM):
                    act.wait_ge(proj, 4 * i + m + 1)
                    nc.scalar.activation(xp[:, m, :, 1:L + 1], ps[:, m, 0:SW].rearrange("p (b l) -> p b l", b=BPI),
                                         ACT.Identity, bias=k.vec("in_b", m)).then_inc(xp_ready, 1)
                act.wait_ge(scanned, i + 1)
                for m in range(DM):
                    act.wait_ge(proj, 4 * i + DM + m + 1)
                    nc.scalar.activation(gate[:, m, :], ps[:, DM + m, 0:SW], ACT.Tanh,
                                         bias=k.half_gate_b[:, m:m + 1], scale=0.5).then_inc(gate_ready, 1)
                for m in range(DM):
                    act.wait_ge(bcd, 6 * i + m + 1)
                    nc.scalar.activation(z[:, m, :], ps[:, 4 + m, 0:SW], ACT.Identity,
                                         bias=k.vec("dt_b", m)).then_inc(z_ready, 1)
                act.wait_ge(z_ready, DM * i + DM)
                s(nc.scalar.activation(az[:], z[:], ACT.Abs))
                nc.scalar.preload_act_table_set("natural_log_exp_and_others")
                s.wait()
                for m in range(DM):
                    s(nc.scalar.activation(az[:, m, :], az[:, m, :], ACT.Exp, scale=-1.0))
                s.wait()
                nc.scalar.activation(az[:], az[:], ACT.Ln, bias=1.0).then_inc(soft_ready, 1)
                for m in range(DM):
                    act.wait_ge(dt_ready, DM * i + m + 1)
                    nc.scalar.activation(decay[:, m, :], dt[:, m, :], ACT.Exp, scale=nega[:, m:m + 1]).then_inc(decay_ready, 1)
                for m in range(DM):
                    act.wait_ge(bcd, 6 * i + DM + m + 1)
                    nc.scalar.activation(bt[:, m, :], ps[:, 6 + m, 0:SW], ACT.Tanh,
                                         bias=k.vec("b_b", m)).then_inc(bt_ready, 1)
                for m in range(DM):
                    act.wait_ge(bcd, 6 * i + 2 * DM + m + 1)
                    nc.scalar.activation(ct[:, m, :], ps[:, m, 0:SW], ACT.Tanh,
                                         bias=k.vec("c_b", m)).then_inc(ct_ready, 1)
                s.end()

        @block.vector
        def _(dve):
            nc.vector.sem_inc(scanned, 1)
            dve.wait_ge(a0_ready, 1)
            nc.vector.tensor_scalar(nega[:], a0[:], -1.0, None, ALU.mult).then_inc(nega_ready, 1)
            with dve.Fori(0, N // SW) as i:
                mix = Steps(dve, mix_steps, i, 2 * DM)
                for tap in range(3):
                    for m in range(DM):
                        if tap == 0:
                            dve.wait_ge(xp_ready, DM * i + m + 1)
                        x = xp[:, m, :, tap:tap + L]
                        out = mixed[:, m, :].rearrange("p (b l) -> p b l", b=BPI)
                        w = k.vec(f"dw{tap}", m)
                        if tap == 0:
                            mix(nc.vector.tensor_scalar(out, x, w, k.vec("dw_b", m), ALU.mult, ALU.add))
                        elif tap == 1:
                            mix(nc.vector.scalar_tensor_tensor(out, x, w, out, ALU.mult, ALU.add))
                        else:
                            nc.vector.scalar_tensor_tensor(out, x, w, out, ALU.mult, ALU.add).then_inc(mixed_ready, 1)
                    if tap < 2:
                        mix.wait()
                mix.end()
                dve.wait_ge(z_ready, DM * i + DM)
                nc.vector.tensor_scalar(relu[:], z[:], 0.0, None, ALU.max).then_inc(relu_ready, 1)
                dve.wait_ge(relu_ready, i + 1)
                dve.wait_ge(soft_ready, i + 1)
                for m in range(DM):
                    nc.vector.tensor_tensor(dt[:, m, :], relu[:, m, :], az[:, m, :], ALU.add).then_inc(dt_ready, 1)
                s = Steps(dve, dsteps, i, 5 + 2 * DM)
                dve.wait_ge(mixed_ready, DM * i + DM)
                dve.wait_ge(dt_ready, DM * i + DM)
                dve.wait_ge(decay_ready, DM * i + DM)
                s(nc.vector.memset(decay[:].rearrange("p m (b l) -> p m b l", b=BPI)[:, :, :, 0:1], 0.0))
                s(nc.vector.tensor_tensor(dt[:], dt[:], mixed[:], ALU.mult))
                s.wait()
                dve.wait_ge(bt_ready, DM * i + DM)
                s(nc.vector.tensor_tensor(dt[:], dt[:], bt[:], ALU.mult))
                s.wait()
                for m in range(DM):
                    s(nc.vector.tensor_tensor_scan(state[:, m, :], decay[:, m, :], dt[:, m, :], 0.0, ALU.mult, ALU.add))
                s.wait()
                dve.wait_ge(ct_ready, DM * i + DM)
                s(nc.vector.tensor_tensor(state[:], state[:], ct[:], ALU.mult))
                s.wait()
                for m in range(DM):
                    s(nc.vector.scalar_tensor_tensor(state[:, m, :], mixed[:, m, :], k.vec("d_skip", m), state[:, m, :],
                                                     ALU.mult, ALU.add))
                s.wait()
                dve.wait_ge(gate_ready, DM * i + DM)
                s(nc.vector.scalar_tensor_tensor(yT[:, :, ds(SW * i, SW)], gate[:], 1.0, state[:], ALU.add, ALU.mult))
                s.wait()
                nc.vector.sem_inc(scanned, 1)
                s.end()


def scan_output(k, ps, yT):
    nc = k.nc
    W = k.weights
    with stage(k) as c:
        ys = k.sb(c, "s4_y", [P, DM, CW])
        xb = k.sb(c, "s4_xb", [P, TC, D])
        x2 = k.sb(c, "s4_x2", [P, TC, D])
        hn = k.sb(c, "s4_hn", [P, TC, D])
        hx = k.sb(c, "s4_hx", [P, TC, D])
        st = k.sb(c, "s4_stats", [P, TC, 6])
        mv = k.sb(c, "s4_meanvar", [P, TC, 2])
        ve = k.sb(c, "s4_var_eps", [P, TC])
        rs = k.sb(c, "s4_rstd", [P, TC])
        hT = k.sb(c, "s4_hT", [P, DM, CW])
        g = k.sb(c, "s4_gelu", [P, 4, CW])
        names = ("staged", "xb", "proj", "x2", "steps", "var", "rstd", "hn", "turned", "hT", "f1", "gelu", "hx1",
                 "hx", "f2", "done")
        (staged, xb_ready, proj, x2_ready, steps, var, rstd, hn_ready, turned, hT_ready, f1, gelu, hx1, hx_ready, f2,
         done) = (k.sem("s4_" + n) for n in names)
        block = c.enter_context(nc.Block())

        @block.gpsimd
        def _(pool):
            nc.gpsimd.sem_inc(proj, TC)
            nc.gpsimd.sem_inc(done, TC)
            with pool.Fori(0, NCH) as i:
                pool.wait_ge(proj, TC * i + TC)
                nc.gpsimd.tensor_copy(ys[:], yT[:, :, ds(CW * i, CW)]).then_inc(staged, 1)
                for j in range(TC):
                    nc.gpsimd.tensor_tensor(xb[:, j, :], k.X[:, ds(TC * i + j, 1), :], k.row("out_b"),
                                            ALU.add).then_inc(xb_ready, 1)
                pool.wait_ge(var, i + 1)
                nc.gpsimd.tensor_tensor(rs[:], ve[:], k.mhalf[:, 0:TC], ALU.pow).then_inc(rstd, 1)
                pool.wait_ge(done, TC * i + TC)
                for j in range(TC):
                    nc.gpsimd.tensor_tensor(hx[:, j, :], x2[:, j, :], k.row("f2_b"), ALU.add).then_inc(hx1, 1)
                pool.wait_ge(hx1, TC * i + TC)
                for j in range(TC):
                    nc.gpsimd.tensor_tensor(hx[:, j, :], hx[:, j, :], k.H[:, ds(TC * i + j, 1), :],
                                            ALU.add).then_inc(hx_ready, 1)

        @block.tensor
        def _(pe):
            nc.tensor.sem_inc(hT_ready, DM)
            with pe.Fori(0, NCH) as i:
                pe.wait_ge(staged, i + 1)
                pe.wait_ge(done, TC * i + TC)
                for j in range(TC):
                    for q in range(DM):
                        last = nc.tensor.matmul(k.tile_out(ps, j), ys[:, q, j * P:j * P + P], W["out_W"][:, q, :],
                                                start=(q == 0 and j != 1), stop=(q == DM - 1), skip_group_check=True)
                    last.then_inc(proj, 1)
                for j in range(TC):
                    pe.wait_ge(hn_ready, TC * i + j + 1)
                    for m in range(DM):
                        last = nc.tensor.transpose(ps[:, 2 + m, j * P:j * P + P], hn[:, j, m * P:m * P + P], k.ident[:])
                last.then_inc(turned, 1)
                pe.wait_ge(hT_ready, DM * i + 2 * DM)
                for m in range(4):
                    for q in range(DM):
                        last = nc.tensor.matmul(ps[:, 4 + m, 0:CW], W["f1_W"][:, q, m * P:m * P + P], hT[:, q, :],
                                                start=(q == 0), stop=(q == DM - 1))
                    last.then_inc(f1, 1)
                pe.wait_ge(x2_ready, TC * i + TC)
                pe.wait_ge(gelu, 4 * i + 4)
                for j in range(TC):
                    for q in range(4):
                        last = nc.tensor.matmul(k.tile_out(ps, j), g[:, q, j * P:j * P + P], W["f2_W"][:, q, :],
                                                start=(q == 0 and j != 1), stop=(q == 3), skip_group_check=True)
                    last.then_inc(f2, 1)

        @block.scalar
        def _(act):
            with act.Fori(0, NCH) as i:
                act.wait_ge(turned, i + 1)
                for m in range(DM):
                    nc.scalar.activation(hT[:, m, :], ps[:, 2 + m, 0:CW], ACT.Identity, bias=k.vec("ln2_b", m),
                                         scale=k.vec("ln2_g", m)).then_inc(hT_ready, 1)
                for m in range(4):
                    act.wait_ge(f1, 4 * i + m + 1)
                    nc.scalar.activation(g[:, m, :], ps[:, 4 + m, 0:CW], ACT.Gelu, bias=k.vec("f1_b", m)).then_inc(gelu, 1)

        @block.vector
        def _(dve):
            with dve.Fori(0, NCH) as i:
                for j in range(TC):
                    dve.wait_ge(xb_ready, TC * i + j + 1)
                    dve.wait_ge(proj, TC * i + TC + max(j, 1) + 1)
                    nc.vector.scalar_tensor_tensor(x2[:, j, :], k.tile_out(ps, j), 0.5, xb[:, j, :],
                                                   ALU.mult, ALU.add).then_inc(x2_ready, 1)
                s = Steps(dve, steps, i, 2 * TC)
                dve.wait_ge(x2_ready, TC * i + TC)
                for j in range(TC):
                    s(nc.vector.bn_stats(st[:, j, :], x2[:, j, :]))
                s.wait()
                k.passed(nc.vector)
                for j in range(TC):
                    s(nc.vector.bn_aggr(mv[:, j, :], st[:, j, :]))
                s.wait()
                s.end()
                nc.vector.tensor_scalar(ve[:], mv[:, :, 1], EPS, None, ALU.add).then_inc(var, 1)
                dve.wait_ge(rstd, i + 1)
                for j in range(TC):
                    nc.vector.tensor_scalar(hn[:, j, :], x2[:, j, :], mv[:, j, 0:1], rs[:, j:j + 1],
                                            ALU.subtract, ALU.mult).then_inc(hn_ready, 1)
                for j in range(TC):
                    dve.wait_ge(hx_ready, TC * i + j + 1)
                    dve.wait_ge(f2, TC * i + max(j, 1) + 1)
                    nc.vector.tensor_tensor(k.H[:, ds(TC * i + j, 1), :], k.tile_out(ps, j), hx[:, j, :],
                                            ALU.add).then_inc(done, 1)


def quant_rows(k, ps, xqT, dq):
    nc = k.nc
    with stage(k) as c:
        st = k.sb(c, "s5_stats", [P, TC, 6])
        mv = k.sb(c, "s5_meanvar", [P, TC, 2])
        ve = k.sb(c, "s5_var_eps", [P, TC])
        rs = k.sb(c, "s5_rstd", [P, TC])
        xs = k.sb(c, "s5_x", [P, TC, D])
        am = k.sb(c, "s5_absmax", [P, TC])
        rec = k.sb(c, "s5_inv_absmax", [P, TC])
        xq = k.sb(c, "s5_xq", [P, TC, D], BF16)
        steps, var, rstd = k.sem("s5_steps"), k.sem("s5_var"), k.sem("s5_rstd_ready")
        quant, turned, stored = k.sem("s5_quant"), k.sem("s5_turned"), k.sem("s5_stored")
        block = c.enter_context(nc.Block())
        tp = ps[:, 0, :].bitcast(BF16)[:, 0:DM * CW].rearrange("p (m t) -> p m t", m=DM)

        @block.vector
        def _(dve):
            nc.vector.sem_inc(turned, 1)
            with dve.Fori(0, NCH) as i:
                s = Steps(dve, steps, i, 4 * TC + 5)
                for j in range(TC):
                    s(nc.vector.bn_stats(st[:, j, :], k.H[:, ds(TC * i + j, 1), :]))
                s.wait()
                k.passed(nc.vector)
                for j in range(TC):
                    s(nc.vector.bn_aggr(mv[:, j, :], st[:, j, :]))
                s.wait()
                nc.vector.tensor_scalar(ve[:], mv[:, :, 1], EPS, None, ALU.add).then_inc(var, 1)
                dve.wait_ge(rstd, i + 1)
                for j in range(TC):
                    s(nc.vector.tensor_scalar(xs[:, j, :], k.H[:, ds(TC * i + j, 1), :],
                                              mv[:, j, 0:1], rs[:, j:j + 1], ALU.subtract, ALU.mult))
                s.wait()
                s(nc.vector.tensor_reduce(am[:], xs[:], AX.X, ALU.max, apply_absolute_value=True))
                s.wait()
                s(nc.vector.tensor_scalar(am[:], am[:], 1e-5, None, ALU.max))
                s.wait()
                s(nc.vector.reciprocal(rec[:], am[:]))
                s(nc.vector.tensor_scalar(dq[:, ds(TC * i, TC)], am[:], 1.0 / 127.0, None, ALU.mult))
                s.wait()
                s(nc.vector.tensor_scalar(rec[:], rec[:], 127.0, None, ALU.mult))
                s.wait()
                for j in range(TC):
                    s(nc.vector.tensor_scalar(xs[:, j, :], xs[:, j, :], rec[:, j:j + 1], MAGIC, ALU.mult, ALU.add))
                s.wait()
                dve.wait_ge(turned, i + 1)
                nc.vector.tensor_scalar(xq[:], xs[:], MAGIC, 127.0, ALU.subtract, ALU.min).then_inc(quant, 1)
                s.end()

        @block.gpsimd
        def _(pool):
            with pool.Fori(0, NCH) as i:
                pool.wait_ge(var, i + 1)
                nc.gpsimd.tensor_tensor(rs[:], ve[:], k.mhalf[:, 0:TC], ALU.pow).then_inc(rstd, 1)

        @block.tensor
        def _(pe):
            nc.tensor.sem_inc(stored, 1)
            with pe.Fori(0, NCH) as i:
                pe.wait_ge(stored, i + 1)
                pe.wait_ge(quant, i + 1)
                for j in range(TC):
                    for m in range(DM):
                        last = nc.tensor.transpose(tp[:, m, j * P:j * P + P], xq[:, j, m * P:m * P + P], k.identb[:])
                last.then_inc(turned, 1)

        @block.scalar
        def _(act):
            with act.Fori(0, NCH) as i:
                act.wait_ge(turned, i + 2)
                nc.scalar.activation(xqT[:, :, ds(CW * i, CW)], tp, ACT.Copy).then_inc(stored, 1)


def ternary_ffn(k, ps, xqT, dq):
    nc = k.nc
    with stage(k) as c:
        dqg = k.sb(c, "s5_gate_scale", [P, NT])
        dqu = k.sb(c, "s5_up_scale", [P, NT])
        sg = k.sb(c, "s5_silu", [P, 2, INNER])
        g = k.sb(c, "s5_g", [P, 2, INNER])
        gq = k.sb(c, "s5_gq", [P, 2, INNER], BF16)
        gqT = k.sb(c, "s5_gqT", [P, 2, FM, P], BF16)
        am = k.sb(c, "s5_g_absmax", [P, 2])
        rec = k.sb(c, "s5_g_inv_absmax", [P, 2])
        dqd = k.sb(c, "s5_down_scale", [P, 2])
        names = ("scales", "gate", "up", "silu", "g", "steps", "gq", "turned", "gqT", "down", "done")
        (scales, gate, up, silu, g_ready, steps, gq_ready, turned, gqT_ready, down,
         done) = (k.sem("s5b_" + n) for n in names)
        block = c.enter_context(nc.Block())
        tp = [ps[:, 4 + p, :].bitcast(BF16).rearrange("p (m t) -> p m t", m=FM) for p in range(2)]

        @block.tensor
        def _(pe):
            nc.tensor.sem_inc(silu, 2)
            nc.tensor.sem_inc(g_ready, 2)
            nc.tensor.sem_inc(done, 2)

            def front(i, p):
                t = 2 * i + p
                for h in range(2):
                    pe.wait_ge(silu, 2 * t + h + 1)
                    for q in range(DM):
                        last = nc.tensor.matmul(ps[:, 2 * h, :], xqT[:, q, ds(P * t, P)],
                                                k.wq["w_gate"][:, q, 512 * h:512 * h + 512],
                                                start=(q == 0), stop=(q == DM - 1))
                    last.then_inc(gate, 1)
                    pe.wait_ge(g_ready, 2 * t + h + 1)
                    for q in range(DM):
                        last = nc.tensor.matmul(ps[:, 2 * h + 1, :], xqT[:, q, ds(P * t, P)],
                                                k.wq["w_up"][:, q, 512 * h:512 * h + 512],
                                                start=(q == 0), stop=(q == DM - 1))
                    last.then_inc(up, 1)

            def back(i, p):
                t = 2 * i + p
                pe.wait_ge(gq_ready, t + 1)
                for m in range(FM):
                    last = nc.tensor.transpose(tp[p][:, m, :], gq[:, p, m * P:m * P + P], k.identb[:])
                last.then_inc(turned, 1)
                pe.wait_ge(gqT_ready, t + 1)
                pe.wait_ge(done, t + 1)
                for m in range(FM):
                    last = nc.tensor.matmul(ps[:, 6 + p, 0:D], gqT[:, p, m, :], k.wq["w_down"][:, m, :],
                                            start=(m == 0), stop=(m == FM - 1))
                last.then_inc(down, 1)

            pipelined(pe, NT, 2, front, back)

        @block.scalar
        def _(act):
            act.wait_ge(scales, 2)

            def front(i, p):
                t = 2 * i + p
                for h in range(2):
                    act.wait_ge(gate, 2 * t + h + 1)
                    act.wait_ge(g_ready, 2 * t + h + 1)
                    k.passed(nc.scalar)
                    nc.scalar.activation(sg[:, p, 512 * h:512 * h + 512], ps[:, 2 * h, :], ACT.Silu,
                                         scale=dqg[:, ds(t, 1)]).then_inc(silu, 1)

            def back(i, p):
                act.wait_ge(turned, 2 * i + p + 1)
                act.wait_ge(down, 2 * i + p + 1)
                nc.scalar.activation(gqT[:, p], tp[p], ACT.Copy).then_inc(gqT_ready, 1)

            nc.scalar.sem_inc(down, 2)
            pipelined(act, NT, 2, front, back)

        @block.vector
        def _(dve):
            nc.vector.tensor_scalar(dqg[:], dq[:], k.wmean[:, 0:1], None, ALU.mult).then_inc(scales, 1)
            nc.vector.tensor_scalar(dqu[:], dq[:], k.wmean[:, 1:2], None, ALU.mult).then_inc(scales, 1)
            dve.wait_ge(scales, 2)

            def front(i, p):
                t = 2 * i + p
                for h in range(2):
                    dve.wait_ge(silu, 2 * t + 2 + h + 1)
                    dve.wait_ge(up, 2 * t + h + 1)
                    cols = slice(512 * h, 512 * h + 512)
                    nc.vector.scalar_tensor_tensor(g[:, p, cols], ps[:, 2 * h + 1, :], dqu[:, ds(t, 1)], sg[:, p, cols],
                                                   ALU.mult, ALU.mult).then_inc(g_ready, 1)
                s = Steps(dve, steps, t, 5)
                dve.wait_ge(g_ready, 2 * t + 4)
                s(nc.vector.tensor_reduce(am[:, p:p + 1], g[:, p, :], AX.X, ALU.max, apply_absolute_value=True))
                s.wait()
                s(nc.vector.tensor_scalar(am[:, p:p + 1], am[:, p:p + 1], 1e-5, None, ALU.max))
                s.wait()
                s(nc.vector.reciprocal(rec[:, p:p + 1], am[:, p:p + 1]))
                s(nc.vector.tensor_scalar(dqd[:, p:p + 1], am[:, p:p + 1], k.wmean[:, 2:3], 1.0 / 127.0,
                                          ALU.mult, ALU.mult))
                s.wait()
                s(nc.vector.tensor_scalar(g[:, p, :], g[:, p, :], rec[:, p:p + 1], 127.0, ALU.mult, ALU.mult))
                s.wait()
                s.end()
                nc.vector.tensor_scalar(gq[:, p, :], g[:, p, :], MAGIC, MAGIC, ALU.add, ALU.subtract).then_inc(gq_ready, 1)

            def back(i, p):
                t = 2 * i + p
                dve.wait_ge(down, t + 3)
                nc.vector.scalar_tensor_tensor(k.H[:, ds(t, 1), :], ps[:, 6 + p, 0:D], dqd[:, p:p + 1],
                                               k.H[:, ds(t, 1), :], ALU.mult, ALU.add).then_inc(done, 1)

            pipelined(dve, NT, 2, front, back)


def attention_inputs(k, ps, qT, kT):
    nc = k.nc
    W = k.weights
    with stage(k) as c:
        st = k.sb(c, "s6_stats", [P, TC, 6])
        mv = k.sb(c, "s6_meanvar", [P, TC, 2])
        ve = k.sb(c, "s6_var_eps", [P, TC])
        rs = k.sb(c, "s6_rstd", [P, TC])
        xs = k.sb(c, "s6_x", [P, TC, D])
        xT = k.sb(c, "s6_xT", [P, DM, CW])
        vs = k.sb(c, "s6_v", [P, 2, TC, D])
        names = ("steps", "var", "rstd", "normed", "turned", "xT", "qk", "qk_out", "v", "v_out", "kept")
        (steps, var, rstd, normed, turned, xT_ready, qk, qk_out, v_ready, v_out, kept) = (k.sem("s6_" + n) for n in names)
        v_stored = [k.sem(f"s6_v_stored{n}") for n in range(2)]
        block = c.enter_context(nc.Block())

        @block.vector
        def _(dve):
            nc.vector.sem_inc(turned, 1)
            for n in range(2):
                nc.vector.sem_inc(v_stored[n], 16)

            def chunk(i, n):
                u = 2 * i + n
                s = Steps(dve, steps, u, 2 * TC)
                for j in range(TC):
                    s(nc.vector.bn_stats(st[:, j, :], k.H[:, ds(TC * u + j, 1), :]))
                s.wait()
                k.passed(nc.vector)
                for j in range(TC):
                    s(nc.vector.bn_aggr(mv[:, j, :], st[:, j, :]))
                s.wait()
                s.end()
                nc.vector.tensor_scalar(ve[:], mv[:, :, 1], EPS, None, ALU.add).then_inc(var, 1)
                dve.wait_ge(rstd, u + 1)
                dve.wait_ge(turned, u + 1)
                dve.wait_ge(kept, u + 1)
                for j in range(TC):
                    nc.vector.tensor_scalar(xs[:, j, :], k.H[:, ds(TC * u + j, 1), :],
                                            mv[:, j, 0:1], rs[:, j:j + 1], ALU.subtract, ALU.mult).then_inc(normed, 1)
                dve.wait_ge(v_stored[n], 16 * i + 16)
                for j in range(TC):
                    dve.wait_ge(v_ready, TC * u + max(j, 1) + 1)
                    nc.vector.tensor_tensor(vs[:, n, j, :], k.tile_out(ps[:, 6:8], j), k.row("bv"),
                                            ALU.add).then_inc(v_out, 1)

            with dve.Fori(0, NCH // 2) as i:
                for n in range(2):
                    chunk(i, n)

        @block.gpsimd
        def _(pool):
            nc.gpsimd.sem_inc(kept, 1)
            with pool.Fori(0, NCH) as i:
                pool.wait_ge(var, i + 1)
                nc.gpsimd.tensor_tensor(rs[:], ve[:], k.mhalf[:, 0:TC], ALU.pow).then_inc(rstd, 1)
                pool.wait_ge(normed, TC * i + TC)
                nc.gpsimd.tensor_copy(k.X[:, ds(TC * i, TC), :], xs[:]).then_inc(kept, 1)

        @block.tensor
        def _(pe):
            nc.tensor.sem_inc(xT_ready, DM)
            nc.tensor.sem_inc(v_out, TC)
            nc.tensor.sem_inc(qk_out, 4)
            with pe.Fori(0, NCH) as i:
                pe.wait_ge(xT_ready, DM * i + DM)
                for j in range(TC):
                    pe.wait_ge(normed, TC * i + j + 1)
                    for m in range(DM):
                        last = nc.tensor.transpose(ps[:, m, j * P:j * P + P], xs[:, j, m * P:m * P + P], k.ident[:])
                last.then_inc(turned, 1)
                pe.wait_ge(xT_ready, DM * i + 2 * DM)
                pe.wait_ge(qk_out, 4 * i + 4)
                for n, w in enumerate(("Wq", "Wk")):
                    for m in range(DM):
                        for q in range(DM):
                            last = nc.tensor.matmul(ps[:, 2 + 2 * n + m, 0:CW], W[w][:, q, m * P:m * P + P], xT[:, q, :],
                                                    start=(q == 0), stop=(q == DM - 1))
                        last.then_inc(qk, 1)
                pe.wait_ge(v_out, TC * i + TC)
                for j in range(TC):
                    for q in range(DM):
                        last = nc.tensor.matmul(k.tile_out(ps[:, 6:8], j), xT[:, q, j * P:j * P + P], W["Wv"][:, q, :],
                                                start=(q == 0 and j != 1), stop=(q == DM - 1), skip_group_check=True)
                    last.then_inc(v_ready, 1)

        @block.scalar
        def _(act):
            with act.Fori(0, NCH) as i:
                act.wait_ge(turned, i + 2)
                act.wait_ge(v_out, TC * i + TC)
                for m in range(DM):
                    nc.scalar.activation(xT[:, m, :], ps[:, m, 0:CW], ACT.Copy).then_inc(xT_ready, 1)
                for m in range(DM):
                    act.wait_ge(qk, 4 * i + m + 1)
                    nc.scalar.activation(qT[:, m, ds(CW * i, CW)], ps[:, 2 + m, 0:CW], ACT.Identity, scale=0.25,
                                         bias=k.quarter_bq[:, m:m + 1]).then_inc(qk_out, 1)
                for m in range(DM):
                    act.wait_ge(qk, 4 * i + DM + m + 1)
                    nc.scalar.activation(kT[:, m, ds(CW * i, CW)], ps[:, 4 + m, 0:CW], ACT.Identity,
                                         bias=k.vec("bk", m)).then_inc(qk_out, 1)

        @block.sync
        def _(sp):
            with sp.Fori(0, NCH // 2) as i:
                for n in range(2):
                    sp.wait_ge(v_out, 2 * TC * i + TC * n + 2 * TC)
                    sp.dma_start(k.v_dram.rearrange("(t p) d -> p t d", p=P)[:, ds(2 * TC * i + TC * n, TC), :],
                                 vs[:, n]).then_inc(v_stored[n], 16)
            for n in range(2):
                sp.wait_ge(v_stored[n], 16 * (NCH // 2) + 16)


def attention(k, ps, qT, kT, fT):
    nc = k.nc
    NU = 2 * B
    NV8 = HG + HG
    with stage(k) as c:
        kb = k.sb(c, "s7_key_blocks", [P, 2, NKC, P])
        vb = k.sb(c, "s7_value_blocks", [P, 2, NKC, P])
        v8 = k.sb(c, "s7_values", [P, 2, NKC, D])
        a = k.sb(c, "s7_abs", [P, 2, NKC, L])
        w = k.sb(c, "s7_ln_cauchy", [P, NKC, L])
        pw = k.sb(c, "s7_exp_and_cauchy", [P, 2, NKC, 2 * L])
        zs = k.sb(c, "s7_chunk_sums", [P, 2, 2 * L])
        mx = k.sb(c, "s7_max", [P, L])
        cm = k.sb(c, "s7_head_max", [P, 2, HG])
        nm = k.sb(c, "s7_neg_max", [HG, L], BF16)
        lz = k.sb(c, "s7_ln_sums", [P, 2 * L])
        rz = k.sb(c, "s7_inv_sums", [P, 2 * L])
        t1 = k.sb(c, "s7_softmax_part", [P, L])
        t2 = k.sb(c, "s7_cauchy_part", [P, L])
        hsel = k.sb(c, "s7_head_rows", [HG, P], BF16)
        hself = k.sb(c, "s7_head_rows_f32", [HG, P])
        hsum = k.sb(c, "s7_head_sum", [P, 2, P])
        tb = k.sb(c, "s7_tb2", [P, 2])
        tbb = k.sb(c, "s7_tb", [P, 2])
        names = ("const", "tb1", "hsel", "kb", "vb", "scores", "max", "abs", "t1", "cm", "t2", "nm", "shifted", "exp",
                 "sq", "ln", "cauchy", "exp_summed", "cauchy_summed", "sums", "lz", "rz", "parts")
        (const, tb1, hsel_ready, kb_ready, vb_ready, scores, max_ready, abs_ready, t1_ready, cm_ready, t2_ready,
         nm_ready, shifted, exp_ready, sq_ready, ln_ready, cauchy, exp_summed, cauchy_summed, sums, lz_ready, rz_ready,
         parts) = (k.sem("s7_" + n) for n in names)
        v_in = [k.sem(f"s7_v_in{n}") for n in range(2)]
        block = c.enter_context(nc.Block())

        def bank(n, j):
            return ps[:, 3 * n + j // KB, (j % KB) * L:(j % KB) * L + L]

        def banks(n):
            return ps[:, 3 * n:3 * n + 3, 0:KB * L]

        o_pw, z_p = ps[:, 6, 0:2 * L], ps[:, 6, 2 * L:3 * L]
        tr1, tr2, z_w = ps[:, 7, 0:P], ps[0:L - P, 7, P:2 * P], ps[:, 7, 2 * P:2 * P + L]
        cm_t = ps[0:HG, 7, 0:L]

        @block.sync
        def _(sp):
            sp.dma_start(hself[:], k.dram["head_rows"]).then_inc(const, 16)
            sp.dma_start(hsum[:], k.dram["head_sum"]).then_inc(const, 16)
            with sp.Fori(0, B // 2) as i:
                for n in range(2):
                    b = 2 * i + n
                    sp.wait_ge(vb_ready, 8 * i + 4 * n + 4)
                    for h in range(HG):
                        rows = slice(DH * h, DH * h + DH)
                        src = k.v_dram[ds(L * b, (NKC - 1) * DH), :].rearrange("(j m) d -> m j d", m=DH)
                        sp.dma_start(v8[rows, n, 0:NKC - 1, :], src).then_inc(v_in[n], 16)
                        sp.dma_start(v8[rows, n, NKC - 1, :],
                                     k.v_dram[ds(L * b + LAST0, DH), :]).then_inc(v_in[n], 16)

        @block.gpsimd
        def _(pool):
            nc.gpsimd.sem_inc(vb_ready, 8)
            pool.wait_ge(const, 32)
            same_head = hsum[:, 0:1, :].to_broadcast([P, NKC - 1, P])

            def over_heads(keys):
                return keys.rearrange("p (j h m) -> p j h m", h=1, m=DH)

            def keys(i, p):
                u, n, b = 4 * i + p, p % 2, 2 * i + p // 2
                pool.wait_ge(scores, u + 1)
                k.passed(nc.gpsimd)
                out = kb[:, n].rearrange("p j (h m) -> p j h m", h=HG)
                mask = hsum[:, 0:1, :].rearrange("p j (h m) -> p j h m", h=HG)
                nk = NKC - 1
                nc.gpsimd.tensor_tensor(out[:, 0:nk], over_heads(kT[:, n, ds(L * b, nk * DH)]).to_broadcast([P, nk, HG, DH]),
                                        mask.to_broadcast([P, nk, HG, DH]), ALU.mult).then_inc(kb_ready, 1)
                nc.gpsimd.tensor_tensor(out[:, nk], over_heads(kT[:, n, ds(L * b + LAST0, DH)])[:, 0].to_broadcast([P, HG, DH]),
                                        mask[:, 0], ALU.mult).then_inc(kb_ready, 1)

            def values(i, p):
                u, n, slot = 4 * i + p, p % 2, p // 2
                if n == 0:
                    pool.wait_ge(v_in[slot], 16 * NV8 * (i + 1))
                pool.wait_ge(sums, u + 1)
                cols = slice(P * n, P * n + P)
                nc.gpsimd.tensor_tensor(vb[:, n, 0:NKC - 1, :], v8[:, slot, 0:NKC - 1, cols], same_head,
                                        ALU.mult).then_inc(vb_ready, 1)
                nc.gpsimd.tensor_tensor(vb[:, n, NKC - 1, :], v8[:, slot, NKC - 1, cols], hsum[:, 1, :],
                                        ALU.mult).then_inc(vb_ready, 1)

            pipelined(pool, NU, 4, keys, values)

        @block.tensor
        def _(pe):
            nc.tensor.sem_inc(scores, 2)
            nc.tensor.sem_inc(sums, 2)
            pe.wait_ge(const, 32)
            pe.wait_ge(hsel_ready, 1)

            def score(i, p):
                u, n, b = 4 * i + p, p % 2, 2 * i + p // 2
                pe.wait_ge(kb_ready, 2 * u + 2)
                pe.wait_ge(exp_ready, u + 1)
                for j in range(NKC):
                    last = nc.tensor.matmul(bank(n, j), kb[:, n, j, :], qT[:, n, ds(L * b, L)],
                                            start=(j % KB == 0), stop=False, skip_group_check=True)
                last.then_inc(scores, 1)

            def outputs(i, p, chunks):
                u, n = 4 * i + p, p % 2
                if 0 in chunks:
                    pe.wait_ge(vb_ready, 2 * u + 10)
                    pe.wait_ge(parts, 3 * u + 3)
                    pe.wait_ge(exp_ready, u + 3)
                    pe.wait_ge(cauchy, u + 2)
                for j in chunks:
                    nc.tensor.matmul(o_pw, vb[:, n, j, :], pw[:, n, j, :], start=(j == 0), stop=(j == NKC - 1),
                                     skip_group_check=True)

            def turn_maxima(i, p):
                pe.wait_ge(max_ready, 4 * i + p + 1)
                nc.tensor.transpose(tr1, mx[:, 0:P], k.ident[:])
                nc.tensor.transpose(tr2, mx[:, P:L], k.ident[:]).then_inc(t1_ready, 1)

            def turn_head_maxima(i, p):
                pe.wait_ge(cm_ready, 2 * (4 * i + p) + 2)
                nc.tensor.transpose(cm_t[:, 0:P], cm[:, 0, :], k.ident[:])
                nc.tensor.transpose(cm_t[:, P:L], cm[0:L - P, 1, :], k.ident[0:L - P, 0:L - P]).then_inc(t2_ready, 1)

            def shift(i, p):
                u, n = 4 * i + p, p % 2
                pe.wait_ge(nm_ready, u + 1)
                pe.wait_ge(abs_ready, u + 1)
                for r in range(3):
                    last = nc.tensor.matmul(ps[:, 3 * n + r, 0:KB * L].rearrange("p (j l) -> p j l", j=KB), hsel[:],
                                            nm[:].rearrange("h (o l) -> h o l", o=1).to_broadcast([HG, KB, L]),
                                            start=False, stop=True, skip_group_check=True)
                last.then_inc(shifted, 1)

            def head_sums(i, p):
                u, n = 4 * i + p, p % 2
                pe.wait_ge(exp_summed, u + 1)
                pe.wait_ge(cauchy_summed, u + 1)
                for dst, cols in ((z_p, slice(0, L)), (z_w, slice(L, 2 * L))):
                    nc.tensor.matmul(dst, hsum[:, 0, :], zs[:, n, cols], start=(dst is z_w), stop=False,
                                     skip_group_check=True)
                    last = nc.tensor.matmul(dst, hsum[:, 1, :], pw[:, n, NKC - 1, cols], start=False, stop=True,
                                            skip_group_check=True)
                last.then_inc(sums, 1)

            def step(new, old):
                if new:
                    score(*new)
                if old:
                    outputs(*old, range(0, 4))
                if new:
                    turn_maxima(*new)
                if old:
                    outputs(*old, range(4, 7))
                if new:
                    turn_head_maxima(*new)
                if old:
                    outputs(*old, range(7, NKC))
                if new:
                    shift(*new)
                if old:
                    head_sums(*old)

            overlapped(pe, NU, 4, step)

        @block.scalar
        def _(act):
            nc.scalar.sem_inc(exp_ready, 2)
            nc.scalar.sem_inc(sq_ready, 2)
            nc.scalar.sem_inc(cauchy, 1)
            act.wait_ge(const, 32)
            nc.scalar.preload_act_table_set("natural_log_exp_and_others")
            nc.scalar.activation(hsel[:], hself[:], ACT.Copy).then_inc(hsel_ready, 1)
            act.wait_ge(tb1, 2)

            def step(new, old):
                if new:
                    u, n = 4 * new[0] + new[1], new[1] % 2
                    act.wait_ge(abs_ready, u + 1)
                    act.wait_ge(cauchy, u + 1)
                    nc.scalar.activation(w[:], a[:, n], ACT.Square, bias=k.vec("beta", n)).then_inc(sq_ready, 1)
                    act.wait_ge(sq_ready, u + 3)
                    nc.scalar.activation(w[:], w[:], ACT.Ln, bias=tb[:, n:n + 1]).then_inc(ln_ready, 1)
                    act.wait_ge(shifted, u + 1)
                    act.wait_ge(sums, u + 1)
                    nc.scalar.activation(pw[:, n, :, 0:L].rearrange("p (r j) l -> p r j l", r=3),
                                         banks(n).rearrange("p r (j l) -> p r j l", j=KB), ACT.Exp).then_inc(exp_ready, 1)
                if old:
                    u = 4 * old[0] + old[1]
                    act.wait_ge(sums, u + 3)
                    act.wait_ge(parts, 3 * u + 3)
                    nc.scalar.activation(lz[:, 0:L], z_p, ACT.Ln).then_inc(lz_ready, 1)
                    nc.scalar.activation(lz[:, L:2 * L], z_w, ACT.Ln).then_inc(lz_ready, 1)
                    act.wait_ge(lz_ready, 2 * u + 2)
                    nc.scalar.activation(rz[:], lz[:], ACT.Exp, scale=-1.0).then_inc(rz_ready, 1)
                if new:
                    u, n = 4 * new[0] + new[1], new[1] % 2
                    act.wait_ge(ln_ready, u + 1)
                    nc.scalar.activation(pw[:, n, :, L:2 * L], w[:], ACT.Exp, scale=-1.0).then_inc(cauchy, 1)

            overlapped(act, NU, 4, step)

        @block.vector
        def _(dve):
            at, bt = VEC["t"][0], VEC["beta"][0]
            nc.vector.sem_inc(parts, 3)
            nc.vector.tensor_tensor(tbb[:], k.vecs[:, at:at + 2], k.vecs[:, bt:bt + 2], ALU.mult).then_inc(tb1, 1)
            dve.wait_ge(tb1, 1)
            nc.vector.tensor_tensor(tb[:], tbb[:], tbb[:], ALU.mult).then_inc(tb1, 1)

            def chunk_sums(n, cols):
                return nc.vector.tensor_reduce(zs[:, n, cols], pw[:, n, 0:NKC - 1, cols].rearrange("p j l -> p l j"),
                                               AX.X, ALU.add)

            def step(new, old):
                if new:
                    u, n = 4 * new[0] + new[1], new[1] % 2
                    dve.wait_ge(scores, u + 3)
                    src = banks(n).rearrange("p r (j l) -> p l r j", j=KB)
                    nc.vector.tensor_reduce(mx[:], src, AX.XY, ALU.max).then_inc(max_ready, 1)
                    dve.wait_ge(sq_ready, u + 1)
                    nc.vector.tensor_scalar(a[:, n].bitcast(I32).rearrange("p (r j) l -> p r (j l)", r=3),
                                            banks(n).bitcast(I32), 0x7FFFFFFF, None, ALU.bitwise_and).then_inc(abs_ready, 1)
                    dve.wait_ge(t1_ready, u + 1)
                    nc.vector.tensor_reduce(cm[:, 0, :], tr1.rearrange("p (h m) -> p h m", h=HG), AX.X,
                                            ALU.max).then_inc(cm_ready, 1)
                    nc.vector.tensor_reduce(cm[0:L - P, 1, :], tr2.rearrange("p (h m) -> p h m", h=HG), AX.X,
                                            ALU.max).then_inc(cm_ready, 1)
                if old:
                    u, n = 4 * old[0] + old[1], old[1] % 2
                    dve.wait_ge(cauchy, u + 2)
                    chunk_sums(n, slice(L, 2 * L)).then_inc(cauchy_summed, 1)
                if new:
                    u, n = 4 * new[0] + new[1], new[1] % 2
                    dve.wait_ge(t2_ready, u + 1)
                    nc.vector.tensor_scalar(nm[:], cm_t, -1.0, None, ALU.mult).then_inc(nm_ready, 1)
                    dve.wait_ge(exp_ready, u + 3)
                    chunk_sums(n, slice(0, L)).then_inc(exp_summed, 1)
                if old:
                    u, n, b = 4 * old[0] + old[1], old[1] % 2, 2 * old[0] + old[1] // 2
                    dve.wait_ge(rz_ready, u + 1)
                    dve.wait_ge(parts, 3 * u + 3)
                    nc.vector.scalar_tensor_tensor(t1[:], o_pw[:, 0:L], 0.5, rz[:, 0:L], ALU.mult, ALU.mult).then_inc(parts, 1)
                    nc.vector.scalar_tensor_tensor(t2[:], o_pw[:, L:2 * L], 0.5, rz[:, L:2 * L], ALU.mult,
                                                   ALU.mult).then_inc(parts, 1)
                    dve.wait_ge(parts, 3 * u + 5)
                    nc.vector.tensor_tensor(fT[:, n, ds(L * b, L)], t1[:], t2[:], ALU.add).then_inc(parts, 1)

            overlapped(dve, NU, 4, step)


def attention_output(k, ps, fT):
    nc = k.nc
    W = k.weights
    with stage(k) as c:
        fs = k.sb(c, "s8_f", [P, DM, CW])
        hx = k.sb(c, "s8_hx", [P, TC, D])
        y = k.sb(c, "s8_y", [P, TC, D])
        st = k.sb(c, "s8_stats", [P, TC, 6])
        mv = k.sb(c, "s8_meanvar", [P, TC, 2])
        ve = k.sb(c, "s8_var_eps", [P, TC])
        rs = k.sb(c, "s8_rstd", [P, TC])
        names = ("staged", "hx1", "hx", "proj", "y", "steps", "var", "rstd", "done")
        staged, hx1, hx_ready, proj, y_ready, steps, var, rstd, done = (k.sem("s8_" + n) for n in names)
        block = c.enter_context(nc.Block())

        @block.gpsimd
        def _(pool):
            nc.gpsimd.sem_inc(proj, TC)
            nc.gpsimd.sem_inc(done, TC)
            with pool.Fori(0, NCH) as i:
                pool.wait_ge(proj, TC * i + TC)
                nc.gpsimd.tensor_copy(fs[:], fT[:, :, ds(CW * i, CW)]).then_inc(staged, 1)
                pool.wait_ge(done, TC * i + TC)
                nc.gpsimd.tensor_tensor(hx[:], k.H[:, ds(TC * i, TC), :], k.X[:, ds(TC * i, TC), :], ALU.add).then_inc(hx1, 1)
                pool.wait_ge(hx1, i + 1)
                for j in range(TC):
                    nc.gpsimd.tensor_tensor(hx[:, j, :], hx[:, j, :], k.row("ln_b"), ALU.add).then_inc(hx_ready, 1)
                pool.wait_ge(var, i + 1)
                nc.gpsimd.tensor_tensor(rs[:], ve[:], k.mhalf[:, 0:TC], ALU.pow).then_inc(rstd, 1)

        @block.tensor
        def _(pe):
            nc.tensor.sem_inc(y_ready, TC)
            with pe.Fori(0, NCH) as i:
                pe.wait_ge(staged, i + 1)
                pe.wait_ge(y_ready, TC * i + TC)
                for j in range(TC):
                    for q in range(DM):
                        last = nc.tensor.matmul(k.tile_out(ps, j), fs[:, q, j * P:j * P + P], W["Wo"][:, q, :],
                                                start=(q == 0 and j != 1), stop=(q == DM - 1), skip_group_check=True)
                    last.then_inc(proj, 1)

        @block.vector
        def _(dve):
            with dve.Fori(0, NCH) as i:
                s = Steps(dve, steps, i, 4 * TC)
                dve.wait_ge(done, TC * i + TC)
                for j in range(TC):
                    dve.wait_ge(proj, TC * i + TC + max(j, 1) + 1)
                    nc.vector.tensor_tensor(y[:, j, :], k.tile_out(ps, j), k.row("bo"), ALU.add).then_inc(y_ready, 1)
                dve.wait_ge(y_ready, TC * i + 2 * TC)
                for j in range(TC):
                    s(nc.vector.bn_stats(st[:, j, :], y[:, j, :]))
                s.wait()
                k.passed(nc.vector)
                for j in range(TC):
                    s(nc.vector.bn_aggr(mv[:, j, :], st[:, j, :]))
                s.wait()
                nc.vector.tensor_scalar(ve[:], mv[:, :, 1], EPS, None, ALU.add).then_inc(var, 1)
                dve.wait_ge(rstd, i + 1)
                for j in range(TC):
                    s(nc.vector.tensor_scalar(y[:, j, :], y[:, j, :], mv[:, j, 0:1], rs[:, j:j + 1],
                                              ALU.subtract, ALU.mult))
                s.wait()
                for j in range(TC):
                    s(nc.vector.tensor_tensor(y[:, j, :], y[:, j, :], k.row("ln_w"), ALU.mult))
                s.wait()
                for j in range(TC):
                    dve.wait_ge(hx_ready, TC * i + j + 1)
                    nc.vector.tensor_tensor(k.H[:, ds(TC * i + j, 1), :], y[:, j, :], hx[:, j, :], ALU.add).then_inc(done, 1)
                s.end()


def route(k, ps):
    nc = k.nc
    with stage(k) as c:
        sb = lambda name, shape, dt=F32: k.sb(c, "s9_" + name, shape, dt)
        st, mv, ve, rs = sb("stats", [P, 6]), sb("meanvar", [P, 2]), sb("var_eps", [P, 1]), sb("rstd", [P, 1])
        xs = sb("x", [P, 2, D])
        xT = sb("xT", [P, DM, P])
        logits, top, idx = sb("logits", [P, E]), sb("top8", [P, 8]), sb("top_index", [P, 8], U32)
        idf, ex, den = sb("index_f32", [P, 2]), sb("exp", [P, 1]), sb("den", [P, 1])
        diff, both, before = sb("diff", [P, 1]), sb("both", [P, E]), sb("before", [P, E])
        oh = sb("one_hot", [P, 2, E])
        bothb = sb("both_bf16", [P, E], BF16)
        total = sb("total", [P, E])
        totalb = sb("total_bf16", [P, E], BF16)
        triub, onesb = sb("triu_bf16", [P, P], BF16), sb("ones_bf16", [P, P], BF16)
        junk = sb("junk", [P, 2, E])
        rank, keep, slot, trash = sb("rank", [P, 2]), sb("keep", [P, 2]), sb("slot", [P, 2]), sb("trash", [P, 2])
        iota, pair = sb("iota", [P, E]), sb("pair", [P, NT, 2])
        valid = sb("valid", [P, NT])
        to = sb("scatter_index", [P, 2, 2], I32)
        names = ("consts", "init", "steps", "var", "rstd", "xs", "turned", "xT", "logits", "diff", "exp", "both",
                 "rank", "to")
        (consts, init, steps, var, rstd, xs_ready, turned, xT_ready, logits_ready, diff_ready, exp_ready, both_ready,
         rank_ready, to_ready) = (k.sem("s9_" + n) for n in names)
        scattered = [k.sem(f"s9_scattered{n}") for n in range(2)]
        block = c.enter_context(nc.Block())

        @block.sync
        def _(sp):
            sp.dma_start(iota[:], k.dram["iota"]).then_inc(consts, 16)
            sp.dma_start(pair[:], k.dram["pair"]).then_inc(consts, 16)
            sp.dma_start(valid[:], k.dram["valid"]).then_inc(consts, 16)

        @block.vector
        def _(dve):
            s = Steps(dve, init)
            s(nc.vector.tensor_copy(triub[:], k.triu[:]))
            s(nc.vector.memset(onesb[:], 1.0))
            s(nc.vector.memset(total[:], 0.0))
            s(nc.vector.memset(totalb[:], 0.0))
            dve.wait_ge(consts, 48)
            s.wait()

            def tile(i, n, first):
                t = 2 * i + n
                h = k.H[:, ds(t, 1), :]
                s = Steps(dve, steps, t, 26)
                s(nc.vector.bn_stats(st[:], h))
                s.wait()
                k.passed(nc.vector)
                s(nc.vector.bn_aggr(mv[:], st[:]))
                s.wait()
                nc.vector.tensor_scalar(ve[:], mv[:, 1:2], EPS, None, ALU.add).then_inc(var, 1)
                dve.wait_ge(rstd, t + 1)
                if not first:
                    dve.wait_ge(scattered[n], 32 * i)
                nc.vector.tensor_scalar(xs[:, n, :], h, mv[:, 0:1], rs[:], ALU.subtract, ALU.mult).then_inc(xs_ready, 1)
                dve.wait_ge(xs_ready, t + 1)
                s(nc.vector.tensor_tensor(h, h, xs[:, n, :], ALU.add))
                dve.wait_ge(logits_ready, t + 1)
                s(nc.vector.tensor_copy(logits[:], ps[:, 2, 0:E]))
                s.wait()
                k.passed(nc.vector)
                s(nc.vector.max(top[:], logits[:]))
                s.wait()
                k.passed(nc.vector)
                s(nc.vector.max_index(idx[:], top[:], logits[:]))
                nc.vector.tensor_tensor(diff[:], top[:, 1:2], top[:, 0:1], ALU.subtract).then_inc(diff_ready, 1)
                s.wait()
                s(nc.vector.tensor_copy(idf[:], idx[:, 0:2]))
                s.wait()
                for j in range(2):
                    s(nc.vector.tensor_scalar(oh[:, j, :], iota[:], idf[:, j:j + 1], valid[:, ds(t, 1)],
                                              ALU.is_equal, ALU.mult))
                s.wait()
                s(nc.vector.tensor_tensor(both[:], oh[:, 0, :], oh[:, 1, :], ALU.add))
                s.wait()
                nc.vector.tensor_copy(bothb[:], both[:]).then_inc(both_ready, 1)
                dve.wait_ge(exp_ready, t + 1)
                s(nc.vector.tensor_scalar(den[:], ex[:], 1.0, None, ALU.add))
                s.wait()
                s(nc.vector.reciprocal(k.prob[:, ds(t, 1), 0], den[:]))
                s.wait()
                s(nc.vector.tensor_tensor(k.prob[:, ds(t, 1), 1], k.prob[:, ds(t, 1), 0], ex[:], ALU.mult))
                dve.wait_ge(rank_ready, t + 1)
                s(nc.vector.tensor_copy(before[:], ps[:, 3, 0:E]))
                s(nc.vector.tensor_tensor(total[:], total[:], both[:], ALU.add))
                s.wait()
                s(nc.vector.tensor_copy(totalb[:], total[:]))
                for j in range(2):
                    s(nc.vector.tensor_tensor(junk[:, j, :], before[:], oh[:, j, :], ALU.mult))
                s.wait()
                s(nc.vector.tensor_reduce(rank[:], junk[:], AX.X, ALU.add))
                s.wait()
                s(nc.vector.tensor_scalar(keep[:], rank[:], float(CAP), valid[:, ds(t, 1)], ALU.is_lt, ALU.mult))
                s(nc.vector.tensor_scalar(rank[:], rank[:], float(CAP - 1), None, ALU.min))
                s.wait()
                s(nc.vector.scalar_tensor_tensor(slot[:], idf[:], float(CAPP), rank[:], ALU.mult, ALU.add))
                s(nc.vector.tensor_tensor(k.prob[:, ds(t, 1), :], k.prob[:, ds(t, 1), :], keep[:], ALU.mult))
                s.wait()
                s(nc.vector.tensor_copy(k.source[:, ds(t, 1), :], slot[:]))
                s(nc.vector.tensor_tensor(trash[:], slot[:], pair[:, ds(t, 1), :], ALU.subtract))
                s.wait()
                s(nc.vector.tensor_tensor(trash[:], trash[:], keep[:], ALU.mult))
                s.wait()
                nc.vector.tensor_tensor(to[:, n, :], trash[:], pair[:, ds(t, 1), :], ALU.add).then_inc(to_ready, 1)
                s.end()

            for n in range(2):
                tile(0, n, True)
            with dve.Fori(1, NT // 2) as i:
                for n in range(2):
                    tile(i, n, False)

        @block.gpsimd
        def _(pool):
            pool.wait_ge(k.zero_filled, 16 * k.fills)
            with pool.Fori(0, NT // 2) as i:
                for n in range(2):
                    pool.wait_ge(var, 2 * i + n + 1)
                    nc.gpsimd.tensor_tensor(rs[:], ve[:], k.mhalf[:, 0:1], ALU.pow).then_inc(rstd, 1)
                    k.settled(pool)
                    pool.wait_ge(to_ready, 2 * i + n + 1)
                    for j in range(2):
                        nc.gpsimd.indirect_dma_start(
                            k.slots_dram, bass.IndirectOffsetOnAxis(ap=to[:, n, j:j + 1], axis=0),
                            xs[:, n, :], None).then_inc(scattered[n], 16)
            for n in range(2):
                pool.wait_ge(scattered[n], 32 * (NT // 2))

        @block.tensor
        def _(pe):
            pe.wait_ge(init, 4)
            with pe.Fori(0, NT // 2) as i:
                for n in range(2):
                    t = 2 * i + n
                    pe.wait_ge(xs_ready, t + 1)
                    for m in range(DM):
                        last = nc.tensor.transpose(ps[:, m, 0:P], xs[:, n, m * P:m * P + P], k.ident[:])
                    last.then_inc(turned, 1)
                    pe.wait_ge(xT_ready, t + 1)
                    for q in range(DM):
                        last = nc.tensor.matmul(ps[:, 2, 0:E], xT[:, q, :], k.weights["router"][:, q, :],
                                                start=(q == 0), stop=(q == DM - 1))
                    last.then_inc(logits_ready, 1)
                    pe.wait_ge(both_ready, t + 1)
                    nc.tensor.matmul(ps[:, 3, 0:E], triub[:], bothb[:], start=True, stop=False)
                    nc.tensor.matmul(ps[:, 3, 0:E], onesb[:], totalb[:], start=False, stop=True).then_inc(rank_ready, 1)

        @block.scalar
        def _(act):
            with act.Fori(0, NT) as t:
                act.wait_ge(turned, t + 1)
                nc.scalar.activation(xT[:], ps[:, 0:DM, 0:P], ACT.Copy).then_inc(xT_ready, 1)
                act.wait_ge(diff_ready, t + 1)
                nc.scalar.activation(ex[:], diff[:], ACT.Exp).then_inc(exp_ready, 1)


def experts(k, ps):
    nc = k.nc
    with stage(k) as c:
        w1 = k.sb(c, "s10_w1", [P, 2, DM, INNER])
        w2 = k.sb(c, "s10_w2", [P, 2, FM, D])
        rows = k.sb(c, "s10_rows", [CR, 2, CT, D])
        xT = k.sb(c, "s10_xT", [P, DM, CAPP])
        hid = k.sb(c, "s10_hidden", [P, FM, CAPP])
        out = k.sb(c, "s10_out", [CR, 2, CT // 2, D])
        HC = CAPP // 2
        w_in = [k.sem(f"s10_w_in{n}") for n in range(2)]
        r_in = [k.sem(f"s10_rows_in{n}") for n in range(2)]
        names = ("turned", "xT", "h", "hid", "y", "out")
        turned, xT_ready, h_ready, hid_ready, y_ready, out_ready = (k.sem("s10_" + n) for n in names)
        stored = [k.sem(f"s10_stored{n}") for n in range(2)]
        block = c.enter_context(nc.Block())

        @block.sync
        def _(sp):
            def load(e, i, n):
                src = k.slots_dram[ds(CAPP * e, CAPP), :].rearrange("(t r) d -> r t d", r=CR)
                sp.dma_start(rows[:, n], src).then_inc(r_in[n], 16)
                sp.dma_start(w1[:, n], k.dram["w1"][:, ds(e, 1)]).then_inc(w_in[n], 16)
                sp.dma_start(w2[:, n], k.dram["w2"][:, ds(e, 1)]).then_inc(w_in[n], 16)

            def store(e):
                for half in range(2):
                    sp.wait_ge(out_ready, CT * e + 3 * half + 3 + 1)
                    dst = k.outs_dram[ds(CAPP * e + 3 * CR * half, 3 * CR), :].rearrange("(t r) d -> r t d", r=CR)
                    sp.dma_start(dst, out[:, half]).then_inc(stored[half], 16)

            for n in range(2):
                load(n, 0, n)
            with sp.Fori(1, E // 2) as i:
                for n in range(2):
                    store(2 * i + n - 2)
                    load(2 * i + n, i, n)
            for n in range(2):
                store(E - 2 + n)
            for half in range(2):
                sp.wait_ge(stored[half], 16 * E + 16)

        @block.tensor
        def _(pe):
            nc.tensor.sem_inc(y_ready, 2 * CT)
            nc.tensor.sem_inc(xT_ready, 1)
            nc.tensor.sem_inc(hid_ready, 2)
            nc.tensor.sem_inc(out_ready, 1)

            def front(i, n):
                e = 2 * i + n
                pe.wait_ge(r_in[n], 16 * i + 16)
                for m in range(DM):
                    for t in range(CT):
                        b = 2 * m + t // 3
                        if t % 3 == 0:
                            pe.wait_ge(xT_ready, 4 * e + b + 1)
                        last = nc.tensor.transpose(ps[:, b % 2, (t % 3) * CR:(t % 3) * CR + CR],
                                                   rows[:, n, t, m * P:m * P + P], k.ident[0:CR, 0:CR])
                        if t % 3 == 2:
                            last.then_inc(turned, 1)

            with pe.Fori(0, E // 2) as i:
                for n in range(2):
                    e = 2 * i + n
                    front(i, n)
                    pe.wait_ge(w_in[n], 32 * i + 32)
                    pe.wait_ge(xT_ready, 4 * e + 5)
                    for f in range(FM):
                        for half in range(2):
                            r = 2 * f + half
                            pe.wait_ge(hid_ready, 2 * FM * e + r + 1)
                            for q in range(DM):
                                last = nc.tensor.matmul(ps[:, 2 + r % 2, 0:HC], w1[:, n, q, f * P:f * P + P],
                                                        xT[:, q, half * HC:half * HC + HC],
                                                        start=(q == 0), stop=(q == DM - 1))
                            last.then_inc(h_ready, 1)
                    pe.wait_ge(hid_ready, 2 * FM * e + 2 * FM + 2)
                    for t in range(CT):
                        pe.wait_ge(out_ready, CT * e + t + 1)
                        for f in range(FM):
                            last = nc.tensor.matmul(ps[0:CR, 4 + t % 2, 0:D], hid[:, f, t * CR:t * CR + CR], w2[:, n, f, :],
                                                    start=(f == 0), stop=(f == FM - 1))
                        last.then_inc(y_ready, 1)

        @block.scalar
        def _(act):
            with act.Fori(0, E) as e:
                act.wait_ge(y_ready, CT * e + 2 * CT)
                for r in range(2 * FM):
                    act.wait_ge(h_ready, 2 * FM * e + r + 1)
                    nc.scalar.activation(hid[:, r // 2, (r % 2) * HC:(r % 2) * HC + HC], ps[:, 2 + r % 2, 0:HC],
                                         ACT.Silu).then_inc(hid_ready, 1)

        @block.vector
        def _(dve):
            for n in range(2):
                nc.vector.sem_inc(stored[n], 16)
            with dve.Fori(0, E) as e:
                for b in range(4):
                    dve.wait_ge(turned, 4 * e + b + 1)
                    nc.vector.tensor_copy(xT[:, b // 2, (b % 2) * HC:(b % 2) * HC + HC], ps[:, b % 2, 0:HC]).then_inc(xT_ready, 1)
                for t in range(CT):
                    if t % 3 == 0:
                        dve.wait_ge(stored[t // 3], 16 * e + 16)
                    dve.wait_ge(y_ready, CT * e + 2 * CT + t + 1)
                    nc.vector.tensor_copy(out[:, t // 3, t % 3, :], ps[0:CR, 4 + t % 2, 0:D]).then_inc(out_ready, 1)


def combine(k):
    nc = k.nc
    with stage(k) as c:
        idx = k.sb(c, "s11_index", [P, 2, 2], I32)
        g = k.sb(c, "s11_rows", [P, 2, 2, D])
        y = k.sb(c, "s11_y", [P, 2, D])
        idx_ready, mixed, done = k.sem("s11_index"), k.sem("s11_mixed"), k.sem("s11_done")
        got = [k.sem(f"s11_got{n}") for n in range(2)]
        stored = [k.sem(f"s11_stored{n}") for n in range(2)]
        block = c.enter_context(nc.Block())

        @block.gpsimd
        def _(pool):
            nc.gpsimd.sem_inc(done, 2)
            with pool.Fori(0, NT // 2) as i:
                for n in range(2):
                    t = 2 * i + n
                    pool.wait_ge(done, t + 1)
                    nc.gpsimd.tensor_copy(idx[:, n, :], k.source[:, ds(t, 1), :]).then_inc(idx_ready, 1)
                    k.settled(pool)
                    pool.wait_ge(idx_ready, t + 1)
                    for j in range(2):
                        nc.gpsimd.indirect_dma_start(
                            g[:, n, j, :], None, k.outs_dram,
                            bass.IndirectOffsetOnAxis(ap=idx[:, n, j:j + 1], axis=0)).then_inc(got[n], 16)

        @block.vector
        def _(dve):
            for n in range(2):
                nc.vector.sem_inc(stored[n], 16)
            with dve.Fori(0, NT // 2) as i:
                for n in range(2):
                    t = 2 * i + n
                    dve.wait_ge(got[n], 32 * i + 32)
                    dve.wait_ge(stored[n], 16 * i + 16)
                    nc.vector.scalar_tensor_tensor(y[:, n, :], g[:, n, 0, :], k.prob[:, ds(t, 1), 0], k.H[:, ds(t, 1), :],
                                                   ALU.mult, ALU.add).then_inc(mixed, 1)
                    dve.wait_ge(mixed, t + 1)
                    nc.vector.scalar_tensor_tensor(y[:, n, :], g[:, n, 1, :], k.prob[:, ds(t, 1), 1], y[:, n, :],
                                                   ALU.mult, ALU.add).then_inc(done, 1)

        @block.sync
        def _(sp):
            out = k.out.rearrange("(t p) d -> p t d", p=P)
            with sp.Fori(0, NT // 2) as i:
                for n in range(2):
                    t = 2 * i + n
                    sp.wait_ge(done, t + 3)
                    sp.dma_start(out[:, ds(t, 1), :], y[:, n, :]).then_inc(stored[n], 16)
            for n in range(2):
                sp.wait_ge(stored[n], 16 * (NT // 2) + 16)


WEIGHTS = {"in_W": (DM, 2 * D), "dt_W": (DM, D), "b_W": (DM, D), "c_W": (DM, D), "out_W": (DM, D),
           "f1_W": (DM, F1), "f2_W": (F1 // P, D), "Wq": (DM, D), "Wk": (DM, D), "Wv": (DM, D), "Wo": (DM, D),
           "router": (DM, E)}


LATE = ("Wq", "Wk", "Wv", "Wo", "router")


def program(nc, dram, out):
    with ExitStack() as ctx:
        k = Core(nc, dram, ctx)
        k.out = out
        k.H = k.sb(ctx, "H", [P, NT, D])
        k.X = k.sb(ctx, "X", [P, NT, D])
        k.vecs = k.sb(ctx, "vecs_sb", [P, NV])
        k.rows = k.sb(ctx, "rows_sb", [P, len(ROWS), D])
        k.ident = k.sb(ctx, "ident_sb", [P, P])
        k.identb = k.sb(ctx, "ident_bf16", [P, P], BF16)
        k.triu = k.sb(ctx, "triu_sb", [P, P])
        k.half_gate_b = k.sb(ctx, "half_gate_b", [P, DM])
        k.quarter_bq = k.sb(ctx, "quarter_bq", [P, DM])
        k.slots_dram = nc.dram_tensor("expert_rows", (SLOTS + 2 * NP, D), F32, kind="Internal").ap()
        k.outs_dram = nc.dram_tensor("expert_outputs", (SLOTS, D), F32, kind="Internal").ap()
        k.zero_filled, k.fills = k.sem("zero_filled"), E
        k.v_dram = nc.dram_tensor("values", (NP, D), F32, kind="Internal").ap()
        k.mhalf = k.sb(ctx, "minus_half", [P, 2 * TC])
        k.wmean = k.sb(ctx, "mean_abs_w", [P, 3])
        k.weights = {n: k.sb(ctx, n + "_sb", [P, *WEIGHTS[n]]) for n in LATE}
        early = ctx.enter_context(ExitStack())
        k.weights |= {n: k.sb(early, n + "_sb", [P, *s]) for n, s in WEIGHTS.items() if n not in LATE}
        k.wq = {n: k.sb(early, n + "_ternary", [P, *s], BF16)
                for n, s in (("w_gate", (DM, INNER)), ("w_up", (DM, INNER)), ("w_down", (FM, D)))}
        k.const_in, k.weights_in = k.sem("const_in"), k.sem("weights_in")
        k.waits_passed = k.sem("waits_passed")
        k.row = lambda name: k.rows[:, ROWS.index(name), :]
        k.tile_out = lambda ps, j: ps[:, j // 2, (j % 2) * D:(j % 2) * D + D]
        ps = ctx.enter_context(nc.psum_tensor("ps", [P, 8, 512], F32))
        embed(k, ps)
        with ExitStack() as c:
            nxT = k.sb(c, "nxT", [P, DM, NP])
            yT = k.sb(c, "yT", [P, DM, NP])
            scan_norms(k, ps, nxT)
            with nc.Block() as block:
                @block.tensor
                def _(pe):
                    pe.wait_ge(k.weights_in, 16 * len(WEIGHTS))

                @block.gpsimd
                def _(pool):
                    nc.gpsimd.memset(yT[:, :, N:NP], 0.0)
            selective_scan(k, ps, nxT, yT)
            scan_output(k, ps, yT)
        with ExitStack() as c:
            xqT = k.sb(c, "xqT", [P, DM, NP], BF16)
            dq = k.sb(c, "row_scale", [P, NT])
            quant_rows(k, ps, xqT, dq)
            ternary_ffn(k, ps, xqT, dq)
        with ExitStack() as c:
            early.close()
            fT = k.sb(c, "fT", [P, DM, NP])
            with ExitStack() as c2:
                qT = k.sb(c2, "qT", [P, DM, NP])
                kT = k.sb(c2, "kT", [P, DM, NP])
                with nc.Block() as block:
                    @block.gpsimd
                    def _(pool):
                        nc.gpsimd.memset(fT[:, :, N:NP], 0.0)

                    @block.vector
                    def _(dve):
                        at = VEC["bq"][0]
                        nc.vector.tensor_scalar(k.quarter_bq[:], k.vecs[:, at:at + 2], 0.25, None, ALU.mult)
                attention_inputs(k, ps, qT, kT)
                attention(k, ps, qT, kT, fT)
            attention_output(k, ps, fT)
        with ExitStack() as c:
            k.prob = k.sb(c, "pair_weights", [P, NT, 2])
            k.source = k.sb(c, "pair_rows", [P, NT, 2], I32)
            route(k, ps)
            experts(k, ps)
            combine(k)


def columns(v):
    import numpy as np
    return np.ascontiguousarray(v.reshape(-1, P).T)


def folded(w):
    import numpy as np
    return np.ascontiguousarray(w.reshape(-1, P, w.shape[1]).transpose(1, 0, 2))


def layout(a):
    import numpy as np
    g = {}
    x = a["x"].reshape(B, 3, 8, 16, 8, 16).transpose(1, 3, 5, 0, 2, 4).reshape(768, B * IMG)
    g["patches"] = folded(x)
    g["tok_W1"], g["tok_W2"] = folded(a["L0_tok_W1"]), folded(a["L0_tok_W2"])
    g["tok_b2"] = a["L0_tok_b2"].reshape(1, D)
    ids = np.zeros((NP,), np.int32)
    ids[:N].reshape(B, L)[:, IMG:] = a["x_txt"]
    g["tokens"] = np.ascontiguousarray(ids.reshape(NT, P).T)
    g["table"] = a["L0_txt_weight"]
    is_text = np.zeros((NP,), np.float32)
    is_text[:N].reshape(B, L)[:, IMG:] = 1.0
    is_image = np.zeros((NP,), np.float32)
    is_image[:N].reshape(B, L)[:, :IMG] = 1.0
    g["tmask"] = np.ascontiguousarray(is_text.reshape(NT, P).T)
    g["imask"] = is_image.reshape(1, NP)
    g["ident"] = np.eye(P, dtype=np.float32)
    g["triu"] = np.triu(np.ones((P, P), np.float32), 1)
    h = np.arange(P) // DH
    g["head_rows"] = (np.arange(HG)[:, None] == h[None, :]).astype(np.float32)
    same = (h[:, None] == h[None, :]).astype(np.float32)
    g["head_sum"] = np.stack([same, same * (np.arange(P) % DH >= DUP)[:, None].astype(np.float32)], 1)
    g["iota"] = np.ascontiguousarray(np.broadcast_to(np.arange(E, dtype=np.float32), (P, E)))
    token = np.arange(NP, dtype=np.float32).reshape(NT, P).T
    g["pair"] = np.ascontiguousarray(np.stack([TRASH + 2 * token, TRASH + 2 * token + 1], 2))
    g["valid"] = (token < N).astype(np.float32)
    g["w1"] = np.ascontiguousarray(a["L1_ffn_w1"].reshape(E, DM, P, INNER).transpose(2, 0, 1, 3))
    g["w2"] = np.ascontiguousarray(a["L1_ffn_w2"].reshape(E, FM, P, D).transpose(2, 0, 1, 3))
    s = "L0_attn_"
    vec = {"in_b": a[s + "in_b"], "dw0": a[s + "dw_W"][:, 0, 0], "dw1": a[s + "dw_W"][:, 0, 1],
           "dw2": a[s + "dw_W"][:, 0, 2], "tb1": a["L0_tok_b1"], "bq": a["L1_attn_bq"], "bk": a["L1_attn_bk"],
           "beta": np.repeat(a["L1_attn_beta"], DH), "t": np.repeat(a["L1_attn_t"], DH)}
    for n in ("dw_b", "dt_b", "b_b", "c_b", "a_log", "d_skip", "ln1_g", "ln1_b", "ln2_g", "ln2_b", "f1_b"):
        vec[n] = a[s + n]
    g["vecs"] = np.concatenate([columns(vec[n]) for n in VEC], 1)
    row = {"out_b": a[s + "out_b"], "f2_b": a[s + "f2_b"], "bv": a["L1_attn_bv"], "bo": a["L1_attn_bo"],
           "ln_w": a["L1_attn_ln_w"], "ln_b": a["L1_attn_ln_b"]}
    g["rows"] = np.ascontiguousarray(np.broadcast_to(np.stack([row[n] for n in ROWS]), (P, len(ROWS), D)))
    for n in ("in_W", "dt_W", "b_W", "c_W", "out_W", "f1_W", "f2_W"):
        g[n] = folded(a[s + n])
    for n in ("Wq", "Wk", "Wv", "Wo"):
        g[n] = folded(a["L1_attn_" + n].T)
    for n in FFN_WEIGHTS:
        g[n] = folded(a["L0_ffn_" + n].T)
    g["router"] = folded(a["L1_ffn_router_w"].T)
    return g


def kernel(**inputs):
    import numpy as np
    import concourse.bacc as bacc
    from concourse.bass_utils import run_bass_kernel_spmd as run

    nc = bacc.Bacc("TRN2", target_bir_lowering=False, num_devices=1)
    arrays, dram = {}, {}
    for name, a in layout({n: np.asarray(v) for n, v in inputs.items()}).items():
        a = np.ascontiguousarray(a)
        arrays[f"in_{name}_dram"] = a
        dram[name] = nc.dram_tensor(f"in_{name}_dram", a.shape, mybir.dt.from_np(a.dtype), kind="ExternalInput").ap()
    out = nc.dram_tensor("out_0_dram", (NP, D), F32, kind="ExternalOutput").ap()
    program(nc, dram, out)
    r = run(nc, [arrays], core_ids=[0])
    return r.results[0]["out_0_dram"][:N].reshape(B, L, D)
```

```python
from contextlib import ExitStack, contextmanager

import concourse.bass as bass
from concourse import mybir
from concourse.bass import ds

F32 = mybir.dt.float32
F32R = mybir.dt.float32r
BF16 = mybir.dt.bfloat16
I32 = mybir.dt.int32
U32 = mybir.dt.uint32
ALU = mybir.AluOpType
ACT = mybir.ActivationFunctionType
AX = mybir.AxisListType

P = 128
B, IMG, TXT = 16, 64, 77
L = IMG + TXT
N = B * L
NT = -(-N // P)
NP = NT * P
D = 256
DM = D // P
TC = 3
NCH = NT // TC
CW = TC * P
KP = 768 // P
BPI = 2
SW = BPI * L
F1 = 512
INNER = 1024
FM = INNER // P
HEADS, DH = 16, 16
HG = 8
NKC = -(-L // DH)
LAST0 = L - DH
DUP = (NKC - 1) * DH - LAST0
KB = 3
E = 8
CAP = int(1.25 * N * 2 / E) + 1
CT = 6
CR = -(-CAP // CT)
CAPP = CT * CR
SLOTS = E * CAPP
TRASH = SLOTS
EPS = 1e-5
MAGIC = 12582912.0

VEC = {}
for _name, _n in (("in_b", 4), ("dw0", 2), ("dw1", 2), ("dw2", 2), ("dw_b", 2), ("dt_b", 2), ("b_b", 2),
                  ("c_b", 2), ("a_log", 2), ("d_skip", 2), ("ln1_g", 2), ("ln1_b", 2), ("ln2_g", 2),
                  ("ln2_b", 2), ("f1_b", 4), ("tb1", 2), ("bq", 2), ("bk", 2), ("beta", 2), ("t", 2)):
    VEC[_name] = (sum(n for _, n in VEC.values()), _n)
NV = sum(n for _, n in VEC.values())
ROWS = ("out_b", "f2_b", "bv", "bo", "ln_w", "ln_b")


FFN_WEIGHTS = ("w_gate", "w_up", "w_down")


def pipelined(eng, n, u, front, back):
    front(0, 0)
    with eng.Fori(0, n // u - 1) as i:
        for p in range(u):
            front(i + (p + 1) // u, (p + 1) % u)
            back(i, p)
    for p in range(u):
        if p + 1 < u:
            front(n // u - 1, p + 1)
        back(n // u - 1, p)


def overlapped(eng, n, u, step):
    step((0, 0), None)
    with eng.Fori(0, n // u - 1) as i:
        for p in range(u):
            step((i + (p + 1) // u, (p + 1) % u), (i, p))
    for p in range(u):
        step((n // u - 1, p + 1) if p + 1 < u else None, (n // u - 1, p))


def overlapped_twice(eng, n, step):
    step((0, 0), None, None)
    step((0, 1), (0, 0), None)
    with eng.Fori(0, n // 2 - 1) as i:
        for p in range(2):
            step((i + 1, p), (i + p, 1 - p), (i, p))
    step(None, (n // 2 - 1, 1), (n // 2 - 1, 0))
    step(None, None, (n // 2 - 1, 1))


class Steps:

    def __init__(self, eng, sem, i=0, per=0):
        self.eng, self.sem, self.base, self.per, self.n = eng, sem, i * per, per, 0

    def __call__(self, ins):
        ins.then_inc(self.sem, 1)
        self.n += 1

    def wait(self):
        self.eng.wait_ge(self.sem, self.base + self.n)

    def end(self):
        assert self.n == self.per, (self.n, self.per)


class Core:

    def __init__(self, nc, dram, ctx):
        self.nc, self.dram, self.sems = nc, dram, []

    def sb(self, ctx, name, shape, dt=F32):
        return ctx.enter_context(self.nc.sbuf_tensor(name, shape, dt))

    def sem(self, name):
        self.sems.append(self.nc.alloc_semaphore(name=name))
        return self.sems[-1]

    def passed(self, eng):
        eng.sem_inc(self.waits_passed, 1)

    def vec(self, name, m):
        at, n = VEC[name]
        assert m < n
        return self.vecs[:, at + m:at + m + 1]


@contextmanager
def stage(k):
    k.sems = []
    with ExitStack() as c:
        yield c
    k.nc.clear_and_free_semaphores(k.sems)
    k.nc.all_engine_barrier()


def embed(k, ps):
    nc, dram = k.nc, k.dram
    with stage(k) as c:
        patches = k.sb(c, "patches", [P, KP, B * IMG])
        w1 = k.sb(c, "tok_w1", [P, KP, D])
        w2 = k.sb(c, "tok_w2", [P, DM, D])
        b2 = k.sb(c, "tok_b2", [1, D])
        imask = k.sb(c, "image_mask", [1, NP])
        tmask = k.sb(c, "text_mask", [P, NT])
        tok = k.sb(c, "token_ids", [P, NT], I32)
        h1 = k.sb(c, "h1", [P, DM, NP])
        rows = k.sb(c, "text_rows", [P, NT, D])
        vecs_in, small_in = k.sem("vecs_in"), k.sem("tok_small_in")
        patches_in = [k.sem(f"patches_in{n}") for n in range(2)]
        tok_in, gathered = k.sem("tok_in"), [k.sem(f"gathered{n}") for n in range(NCH)]
        cleared, hid, hid_out = k.sem("h1_cleared"), k.sem("hid_ready"), k.sem("hid_activated")
        emb, emb_out, half = k.sem("emb_ready"), k.sem("emb_out"), k.sem("half_bias")
        wf = {n: k.sb(c, n + "_f32", [P, DM * INNER]) for n in FFN_WEIGHTS}
        junk = k.sb(c, "abs_weights", [P, DM * INNER])
        asum = k.sb(c, "abs_sums", [P, 3])
        ones = k.sb(c, "ones", [P, P])
        wrec = k.sb(c, "inv_mean_abs", [P, 3])
        ffn_in = [k.sem(n + "_in") for n in FFN_WEIGHTS]
        zeros = k.sb(c, "zeros", [CR, CT, D])
        zeroed, inv_mean, scaled = k.sem("zeros_ready"), k.sem("inv_mean_ready"), k.sem("weights_scaled")
        summed, total, wq_steps = k.sem("abs_summed"), k.sem("abs_total"), k.sem("wq_steps")
        block = c.enter_context(nc.Block())

        @block.sync
        def _(sp):
            sp.dma_start(k.vecs[:], dram["vecs"]).then_inc(vecs_in, 16)
            sp.dma_start(w1[:], dram["tok_W1"]).then_inc(patches_in[0], 16)
            for n in range(2):
                sp.dma_start(patches[:, :, 512 * n:512 * n + 512],
                             dram["patches"][:, :, 512 * n:512 * n + 512]).then_inc(patches_in[n], 16)
            sp.dma_start(w2[:], dram["tok_W2"]).then_inc(small_in, 16)
            sp.dma_start(b2[:], dram["tok_b2"]).then_inc(small_in, 16)
            sp.dma_start(imask[:], dram["imask"]).then_inc(small_in, 16)
            sp.dma_start(tmask[:], dram["tmask"]).then_inc(small_in, 16)
            sp.dma_start(k.ident[:], dram["ident"]).then_inc(k.const_in, 16)
            sp.dma_start(k.triu[:], dram["triu"]).then_inc(k.const_in, 16)
            sp.dma_start(k.rows[:], dram["rows"]).then_inc(k.const_in, 16)
            for n, name in enumerate(FFN_WEIGHTS):
                sp.dma_start(wf[name][:], dram[name].rearrange("p a b -> p (a b)")).then_inc(ffn_in[n], 16)
            for name in WEIGHTS:
                sp.dma_start(k.weights[name][:], dram[name]).then_inc(k.weights_in, 16)
            sp.wait_ge(zeroed, 1)
            for e in range(E):
                sp.dma_start(k.slots_dram[CAPP * e:CAPP * e + CAPP, :].rearrange("(t r) d -> r t d", r=CR),
                             zeros[:]).then_inc(k.zero_filled, 16)

        @block.gpsimd
        def _(pool):
            pool.dma_start(tok[:], dram["tokens"]).then_inc(tok_in, 16)
            nc.gpsimd.memset(h1[:], 0.0).then_inc(cleared, 1)
            nc.gpsimd.memset(zeros[:], 0.0).then_inc(zeroed, 1)
            pool.wait_ge(tok_in, 16)
            for t in range(NT):
                nc.gpsimd.indirect_dma_start(
                    rows[:, t, :], None, dram["table"],
                    bass.IndirectOffsetOnAxis(ap=tok[:, t:t + 1], axis=0)).then_inc(gathered[t // TC], 16)

        @block.tensor
        def _(pe):
            for n in range(2):
                pe.wait_ge(patches_in[n], 16 * (2 - n))
                for m in range(DM):
                    for q in range(KP):
                        last = nc.tensor.matmul(ps[:, 2 * n + m, :], w1[:, q, m * P:m * P + P],
                                                patches[:, q, 512 * n:512 * n + 512],
                                                start=(q == 0), stop=(q == KP - 1))
                    last.then_inc(hid, 1)
            pe.wait_ge(hid_out, 2 * DM)
            pe.wait_ge(small_in, 64)
            for t in range(NT):
                if t >= 4:
                    pe.wait_ge(emb_out, t - 3)
                out = ps[:, 4 + t % 4, 0:D]
                for m in range(DM):
                    nc.tensor.matmul(out, h1[:, m, t * P:t * P + P], w2[:, m, :], start=(m == 0), stop=False)
                nc.tensor.matmul(out, imask[:, t * P:t * P + P], b2[:], start=False, stop=True).then_inc(emb, 1)
            pe.wait_ge(half, 4)
            pe.wait_ge(summed, 3)
            nc.tensor.matmul(ps[:, 0, 0:3], ones[:], asum[:], start=True, stop=True).then_inc(total, 1)

        @block.scalar
        def _(act):
            act.wait_ge(vecs_in, 16)
            act.wait_ge(cleared, 1)
            for n in range(2):
                for m in range(DM):
                    act.wait_ge(hid, 2 * n + m + 1)
                    dst = h1[:, m, 0:N].rearrange("p (b l) -> p b l", b=B)[:, 8 * n:8 * n + 8, 0:IMG]
                    nc.scalar.activation(dst, ps[:, 2 * n + m, :].rearrange("p (b l) -> p b l", b=8),
                                         ACT.Silu, bias=k.vec("tb1", m)).then_inc(hid_out, 1)
            for n, name in enumerate(FFN_WEIGHTS):
                act.wait_ge(ffn_in[n], 16)
                if n:
                    act.wait_ge(summed, n)
                nc.scalar.activation(junk[:], wf[name][:], ACT.Abs, accum_out=asum[:, n:n + 1]).then_inc(summed, 1)
            act.wait_ge(inv_mean, 1)
            for n, name in enumerate(FFN_WEIGHTS):
                nc.scalar.activation(wf[name][:], wf[name][:], ACT.Copy, scale=wrec[:, n:n + 1]).then_inc(scaled, 1)

        @block.vector
        def _(dve):
            dve.wait_ge(vecs_in, 16)
            at = VEC["in_b"][0]
            nc.vector.tensor_scalar(k.half_gate_b[:], k.vecs[:, at + 2:at + 4], 0.5, None, ALU.mult).then_inc(half, 1)
            dve.wait_ge(k.const_in, 48)
            nc.vector.tensor_copy(k.identb[:], k.ident[:]).then_inc(half, 1)
            nc.vector.memset(k.mhalf[:], -0.5).then_inc(half, 1)
            nc.vector.memset(ones[:], 1.0).then_inc(half, 1)
            dve.wait_ge(small_in, 64)
            for t in range(NT):
                dve.wait_ge(gathered[t // TC], 16 * TC)
                dve.wait_ge(emb, t + 1)
                nc.vector.scalar_tensor_tensor(k.H[:, t, :], rows[:, t, :], tmask[:, t:t + 1], ps[:, 4 + t % 4, 0:D],
                                               ALU.mult, ALU.add).then_inc(emb_out, 1)
            s = Steps(dve, wq_steps)
            dve.wait_ge(total, 1)
            s(nc.vector.tensor_scalar(k.wmean[:], ps[:, 0, 0:3], 1.0 / (D * INNER), 1e-5, ALU.mult, ALU.max))
            s.wait()
            s(nc.vector.reciprocal(wrec[:], k.wmean[:]))
            s.wait()
            nc.vector.sem_inc(inv_mean, 1)
            for n, name in enumerate(FFN_WEIGHTS):
                dve.wait_ge(scaled, n + 1)
                s(nc.vector.tensor_scalar(wf[name][:], wf[name][:], 1.0, -1.0, ALU.min, ALU.max))
                s.wait()
                nc.vector.tensor_scalar(k.wq[name][:].rearrange("p a b -> p (a b)"), wf[name][:], MAGIC, MAGIC,
                                        ALU.add, ALU.subtract)


def scan_norms(k, ps, nxT):
    nc = k.nc
    with stage(k) as c:
        st = k.sb(c, "s2_stats", [P, TC, 6])
        mv = k.sb(c, "s2_meanvar", [P, TC, 2])
        ve = k.sb(c, "s2_var_eps", [P, 2, TC])
        rs = k.sb(c, "s2_rstd", [P, 2, TC])
        nx = k.sb(c, "s2_nx", [P, TC, D])
        steps, var, rstd = k.sem("s2_steps"), k.sem("s2_var"), k.sem("s2_rstd_ready")
        normed, turned, stored = k.sem("s2_normed"), k.sem("s2_turned"), k.sem("s2_stored")
        block = c.enter_context(nc.Block())

        @block.vector
        def _(dve):
            nc.vector.sem_inc(turned, 1)
            with dve.Fori(0, NCH) as i:
                s = Steps(dve, steps, i, 3 * TC)
                for j in range(TC):
                    s(nc.vector.bn_stats(st[:, j, :], k.H[:, ds(TC * i + j, 1), :]))
                s.wait()
                k.passed(nc.vector)
                for j in range(TC):
                    s(nc.vector.bn_aggr(mv[:, j, :], st[:, j, :]))
                s.wait()
                nc.vector.tensor_scalar(ve[:, 0, :], mv[:, :, 1], EPS, None, ALU.add).then_inc(var, 1)
                nc.vector.tensor_scalar(ve[:, 1, :], mv[:, :, 1], 1.0 + EPS, EPS * EPS,
                                        ALU.mult, ALU.add).then_inc(var, 1)
                dve.wait_ge(rstd, i + 1)
                for j in range(TC):
                    s(nc.vector.tensor_scalar(k.X[:, ds(TC * i + j, 1), :], k.H[:, ds(TC * i + j, 1), :],
                                              mv[:, j, 0:1], rs[:, 0, j:j + 1], ALU.subtract, ALU.mult))
                dve.wait_ge(turned, i + 1)
                for j in range(TC):
                    nc.vector.tensor_scalar(nx[:, j, :], k.H[:, ds(TC * i + j, 1), :], mv[:, j, 0:1],
                                            rs[:, 1, j:j + 1], ALU.subtract, ALU.mult).then_inc(normed, 1)
                s.end()

        @block.gpsimd
        def _(pool):
            with pool.Fori(0, NCH) as i:
                pool.wait_ge(var, 2 * i + 2)
                nc.gpsimd.tensor_tensor(rs[:], ve[:], k.mhalf[:, 0:2 * TC].rearrange("p (a b) -> p a b", a=2),
                                        ALU.pow).then_inc(rstd, 1)

        @block.tensor
        def _(pe):
            nc.tensor.sem_inc(stored, 2)
            with pe.Fori(0, NCH) as i:
                pe.wait_ge(stored, 2 * i + 2)
                for j in range(TC):
                    pe.wait_ge(normed, TC * i + j + 1)
                    for m in range(DM):
                        last = nc.tensor.transpose(ps[:, m, j * P:j * P + P], nx[:, j, m * P:m * P + P], k.ident[:])
                last.then_inc(turned, 1)

        @block.scalar
        def _(act):
            with act.Fori(0, NCH) as i:
                act.wait_ge(turned, i + 2)
                for m in range(DM):
                    nc.scalar.activation(nxT[:, m, ds(CW * i, CW)], ps[:, m, 0:CW], ACT.Identity,
                                         bias=k.vec("ln1_b", m), scale=k.vec("ln1_g", m)).then_inc(stored, 1)


def selective_scan(k, ps, nxT, yT):
    nc = k.nc
    NS = N // SW
    W = k.weights
    with stage(k) as c:
        xp = k.sb(c, "s3_conv_in", [P, DM, BPI, L + 2])
        mixed = k.sb(c, "s3_mixed", [P, 2, DM, SW])
        gate = k.sb(c, "s3_gate", [P, 2, DM, SW])
        az = k.sb(c, "s3_soft", [P, DM, SW])
        z = k.sb(c, "s3_z", [P, DM, SW])
        relu = k.sb(c, "s3_relu", [P, DM, SW])
        dt = k.sb(c, "s3_dt", [P, DM, SW])
        bt = k.sb(c, "s3_bt", [P, 2, DM, SW])
        ct = k.sb(c, "s3_ct", [P, 2, DM, SW])
        decay = k.sb(c, "s3_decay", [P, 2, DM, SW])
        state = k.sb(c, "s3_state", [P, DM, SW])
        nega = k.sb(c, "s3_neg_a", [P, DM])
        a0 = k.sb(c, "s3_exp_a", [P, DM])
        names = ("padded", "nega", "a0", "proj", "xp", "gate", "mix_steps", "mixed", "bcd", "z", "relu", "soft", "dt",
                 "decay", "bt", "ct", "asteps", "dsteps", "scanned")
        (padded, nega_ready, a0_ready, proj, xp_ready, gate_ready, mix_steps, mixed_ready, bcd, z_ready, relu_ready,
         soft_ready, dt_ready, decay_ready, bt_ready, ct_ready, asteps, dsteps, scanned) = (k.sem("s3_" + n) for n in names)
        block = c.enter_context(nc.Block())

        @block.gpsimd
        def _(pool):
            nc.gpsimd.memset(xp[:], 0.0).then_inc(padded, 1)

        @block.tensor
        def _(pe):
            def step(new, old):
                if old:
                    i, p = 2 * old[0] + old[1], old[1]
                    pe.wait_ge(mixed_ready, DM * i + DM)
                    for w, bank in (("dt_W", 4), ("b_W", 6), ("c_W", 0)):
                        for m in range(DM):
                            for q in range(DM):
                                last = nc.tensor.matmul(ps[:, bank + m, 0:SW], W[w][:, q, m * P:m * P + P],
                                                        mixed[:, p, q, :], start=(q == 0), stop=(q == DM - 1))
                            last.then_inc(bcd, 1)
                if new:
                    i = 2 * new[0] + new[1]
                    for m in range(4):
                        if m == 0:
                            pe.wait_ge(ct_ready, DM * i + DM)
                        if m == DM:
                            pe.wait_ge(gate_ready, DM * i + DM)
                        for q in range(DM):
                            last = nc.tensor.matmul(ps[:, m, 0:SW], W["in_W"][:, q, m * P:m * P + P],
                                                    nxT[:, q, ds(SW * i, SW)], start=(q == 0), stop=(q == DM - 1))
                        last.then_inc(proj, 1)

            overlapped(pe, NS, 2, step)

        @block.scalar
        def _(act):
            nc.scalar.sem_inc(ct_ready, DM)
            nc.scalar.sem_inc(gate_ready, DM)
            nc.scalar.activation(a0[:], k.vecs[:, VEC["a_log"][0]:VEC["a_log"][0] + DM], ACT.Exp).then_inc(a0_ready, 1)
            act.wait_ge(padded, 1)
            act.wait_ge(nega_ready, 1)

            def step(new, old):
                if old:
                    i, p = 2 * old[0] + old[1], old[1]
                    s = Steps(act, asteps, i, 1 + DM)
                    for m in range(DM):
                        act.wait_ge(bcd, 6 * i + m + 1)
                        nc.scalar.activation(z[:, m, :], ps[:, 4 + m, 0:SW], ACT.Identity,
                                             bias=k.vec("dt_b", m)).then_inc(z_ready, 1)
                    act.wait_ge(scanned, i + 1)
                    for m in range(DM):
                        act.wait_ge(bcd, 6 * i + DM + m + 1)
                        nc.scalar.activation(bt[:, p, m, :], ps[:, 6 + m, 0:SW], ACT.Tanh,
                                             bias=k.vec("b_b", m)).then_inc(bt_ready, 1)
                    for m in range(DM):
                        act.wait_ge(bcd, 6 * i + 2 * DM + m + 1)
                        nc.scalar.activation(ct[:, p, m, :], ps[:, m, 0:SW], ACT.Tanh,
                                             bias=k.vec("c_b", m)).then_inc(ct_ready, 1)
                    act.wait_ge(z_ready, DM * i + DM)
                    s(nc.scalar.activation(az[:], z[:], ACT.Abs))
                    nc.scalar.preload_act_table_set("natural_log_exp_and_others")
                    s.wait()
                    for m in range(DM):
                        s(nc.scalar.activation(az[:, m, :], az[:, m, :], ACT.Exp, scale=-1.0))
                    s.wait()
                    nc.scalar.activation(az[:], az[:], ACT.Ln, bias=1.0).then_inc(soft_ready, 1)
                    s.end()
                if new:
                    u = 2 * new[0] + new[1]
                    for m in range(DM):
                        act.wait_ge(proj, 4 * u + m + 1)
                        nc.scalar.activation(xp[:, m, :, 1:L + 1], ps[:, m, 0:SW].rearrange("p (b l) -> p b l", b=BPI),
                                             ACT.Identity, bias=k.vec("in_b", m)).then_inc(xp_ready, 1)
                if old:
                    for m in range(DM):
                        act.wait_ge(dt_ready, DM * i + m + 1)
                        nc.scalar.activation(decay[:, p, m, :], dt[:, m, :], ACT.Exp,
                                             scale=nega[:, m:m + 1]).then_inc(decay_ready, 1)
                if new:
                    for m in range(DM):
                        act.wait_ge(proj, 4 * u + DM + m + 1)
                        nc.scalar.activation(gate[:, new[1], m, :], ps[:, DM + m, 0:SW], ACT.Tanh,
                                             bias=k.half_gate_b[:, m:m + 1], scale=0.5).then_inc(gate_ready, 1)

            overlapped(act, NS, 2, step)

        @block.vector
        def _(dve):
            nc.vector.sem_inc(scanned, 2)
            dve.wait_ge(a0_ready, 1)
            nc.vector.tensor_scalar(nega[:], a0[:], -1.0, None, ALU.mult).then_inc(nega_ready, 1)

            def softplus(i, p):
                i = 2 * i + p
                dve.wait_ge(z_ready, DM * i + DM)
                nc.vector.tensor_scalar(relu[:], z[:], 0.0, None, ALU.max).then_inc(relu_ready, 1)
                dve.wait_ge(relu_ready, i + 1)
                dve.wait_ge(soft_ready, i + 1)
                for m in range(DM):
                    nc.vector.tensor_tensor(dt[:, m, :], relu[:, m, :], az[:, m, :], ALU.add).then_inc(dt_ready, 1)

            def convolution(i, p):
                i = 2 * i + p
                mix = Steps(dve, mix_steps, i, 2 * DM)
                for tap in range(3):
                    for m in range(DM):
                        if tap == 0:
                            dve.wait_ge(xp_ready, DM * i + m + 1)
                        x = xp[:, m, :, tap:tap + L]
                        out = mixed[:, p, m, :].rearrange("p (b l) -> p b l", b=BPI)
                        w = k.vec(f"dw{tap}", m)
                        if tap == 0:
                            mix(nc.vector.tensor_scalar(out, x, w, k.vec("dw_b", m), ALU.mult, ALU.add))
                        elif tap == 1:
                            mix(nc.vector.scalar_tensor_tensor(out, x, w, out, ALU.mult, ALU.add))
                        else:
                            nc.vector.scalar_tensor_tensor(out, x, w, out, ALU.mult, ALU.add).then_inc(mixed_ready, 1)
                    if tap < 2:
                        mix.wait()
                mix.end()

            def scan(i, p):
                i = 2 * i + p
                s = Steps(dve, dsteps, i, 5 + 2 * DM)
                dve.wait_ge(decay_ready, DM * i + DM)
                s(nc.vector.memset(decay[:, p].rearrange("p m (b l) -> p m b l", b=BPI)[:, :, :, 0:1], 0.0))
                s(nc.vector.tensor_tensor(dt[:], dt[:], mixed[:, p], ALU.mult))
                s.wait()
                dve.wait_ge(bt_ready, DM * i + DM)
                s(nc.vector.tensor_tensor(dt[:], dt[:], bt[:, p], ALU.mult))
                s.wait()
                for m in range(DM):
                    s(nc.vector.tensor_tensor_scan(state[:, m, :], decay[:, p, m, :], dt[:, m, :], 0.0, ALU.mult, ALU.add))
                s.wait()
                dve.wait_ge(ct_ready, DM * i + 2 * DM)
                s(nc.vector.tensor_tensor(state[:], state[:], ct[:, p], ALU.mult))
                s.wait()
                for m in range(DM):
                    s(nc.vector.scalar_tensor_tensor(state[:, m, :], mixed[:, p, m, :], k.vec("d_skip", m), state[:, m, :],
                                                     ALU.mult, ALU.add))
                s.wait()
                dve.wait_ge(gate_ready, DM * i + 2 * DM)
                s(nc.vector.scalar_tensor_tensor(yT[:, :, ds(SW * i, SW)], gate[:, p], 1.0, state[:], ALU.add, ALU.mult))
                s.wait()
                nc.vector.sem_inc(scanned, 1)
                s.end()

            def step(new, old):
                if old:
                    softplus(*old)
                if new:
                    convolution(*new)
                if old:
                    scan(*old)

            overlapped(dve, NS, 2, step)


def scan_output(k, ps, yT):
    nc = k.nc
    W = k.weights
    with stage(k) as c:
        ys = k.sb(c, "s4_y", [P, DM, CW])
        xb = k.sb(c, "s4_xb", [P, TC, D])
        x2 = k.sb(c, "s4_x2", [P, 2, TC, D])
        hn = k.sb(c, "s4_hn", [P, TC, D])
        hx = k.sb(c, "s4_hx", [P, 2, TC, D])
        st = k.sb(c, "s4_stats", [P, TC, 6])
        mv = k.sb(c, "s4_meanvar", [P, TC, 2])
        ve = k.sb(c, "s4_var_eps", [P, TC])
        rs = k.sb(c, "s4_rstd", [P, TC])
        hT = k.sb(c, "s4_hT", [P, DM, CW])
        g = k.sb(c, "s4_gelu", [P, 4, CW])
        names = ("staged", "xb", "proj", "x2", "steps", "var", "rstd", "hn", "turned", "hT", "f1", "gelu", "hx1",
                 "hx", "f2", "done")
        (staged, xb_ready, proj, x2_ready, steps, var, rstd, hn_ready, turned, hT_ready, f1, gelu, hx1, hx_ready, f2,
         done) = (k.sem("s4_" + n) for n in names)
        block = c.enter_context(nc.Block())

        @block.gpsimd
        def _(pool):
            nc.gpsimd.sem_inc(done, 2 * TC)
            with pool.Fori(0, NCH // 2) as i:
                for p in range(2):
                    u = 2 * i + p
                    for j in range(TC):
                        nc.gpsimd.tensor_tensor(xb[:, j, :], k.X[:, ds(TC * u + j, 1), :], k.row("out_b"),
                                                ALU.add).then_inc(xb_ready, 1)
                    pool.wait_ge(var, u + 1)
                    nc.gpsimd.tensor_tensor(rs[:], ve[:], k.mhalf[:, 0:TC], ALU.pow).then_inc(rstd, 1)
                    pool.wait_ge(done, TC * u + TC)
                    for j in range(TC):
                        nc.gpsimd.tensor_tensor(hx[:, p, j, :], x2[:, p, j, :], k.row("f2_b"), ALU.add).then_inc(hx1, 1)
                    pool.wait_ge(hx1, TC * u + TC)
                    for j in range(TC):
                        nc.gpsimd.tensor_tensor(hx[:, p, j, :], hx[:, p, j, :], k.H[:, ds(TC * u + j, 1), :],
                                                ALU.add).then_inc(hx_ready, 1)

        @block.tensor
        def _(pe):
            def step(new, old):
                if old:
                    u = 2 * old[0] + old[1]
                    for j in range(TC):
                        pe.wait_ge(hn_ready, TC * u + j + 1)
                        for m in range(DM):
                            last = nc.tensor.transpose(ps[:, 2 + m, j * P:j * P + P], hn[:, j, m * P:m * P + P], k.ident[:])
                    last.then_inc(turned, 1)
                if new:
                    v = 2 * new[0] + new[1]
                    pe.wait_ge(staged, v + 1)
                    for j in range(TC):
                        for q in range(DM):
                            last = nc.tensor.matmul(k.tile_out(ps[:, 6:8], j), ys[:, q, j * P:j * P + P], W["out_W"][:, q, :],
                                                    start=(q == 0 and j != 1), stop=(q == DM - 1), skip_group_check=True)
                        last.then_inc(proj, 1)
                if old:
                    pe.wait_ge(hT_ready, DM * u + DM)
                    for m in range(4):
                        if new and m == 2:
                            pe.wait_ge(x2_ready, TC * v + TC)
                        for q in range(DM):
                            last = nc.tensor.matmul(ps[:, 4 + m, 0:CW], W["f1_W"][:, q, m * P:m * P + P], hT[:, q, :],
                                                    start=(q == 0), stop=(q == DM - 1))
                        last.then_inc(f1, 1)
                    pe.wait_ge(done, TC * u + 2 * TC)
                    pe.wait_ge(gelu, 4 * u + 4)
                    for j in range(TC):
                        for q in range(4):
                            last = nc.tensor.matmul(k.tile_out(ps, j), g[:, q, j * P:j * P + P], W["f2_W"][:, q, :],
                                                    start=(q == 0 and j != 1), stop=(q == 3), skip_group_check=True)
                        last.then_inc(f2, 1)

            overlapped(pe, NCH, 2, step)

        @block.scalar
        def _(act):
            nc.scalar.sem_inc(proj, TC)
            nc.scalar.sem_inc(f2, TC)

            def step(new, old):
                if new:
                    v = 2 * new[0] + new[1]
                    act.wait_ge(proj, TC * v + TC)
                    nc.scalar.activation(ys[:], yT[:, :, ds(CW * v, CW)], ACT.Copy).then_inc(staged, 1)
                if old:
                    u = 2 * old[0] + old[1]
                    act.wait_ge(f2, TC * u + TC)
                    for m in range(4):
                        act.wait_ge(f1, 4 * u + m + 1)
                        nc.scalar.activation(g[:, m, :], ps[:, 4 + m, 0:CW], ACT.Gelu, bias=k.vec("f1_b", m)).then_inc(gelu, 1)

            overlapped(act, NCH, 2, step)

        @block.vector
        def _(dve):
            nc.vector.sem_inc(turned, 1)

            def step(new, old):
                if old:
                    u = 2 * old[0] + old[1]
                    dve.wait_ge(turned, u + 2)
                    for m in range(DM):
                        nc.vector.tensor_scalar(hT[:, m, :], ps[:, 2 + m, 0:CW], k.vec("ln2_g", m), k.vec("ln2_b", m),
                                                ALU.mult, ALU.add).then_inc(hT_ready, 1)
                if new:
                    v, p = 2 * new[0] + new[1], new[1]
                    for j in range(TC):
                        dve.wait_ge(xb_ready, TC * v + j + 1)
                        dve.wait_ge(proj, TC * v + TC + max(j, 1) + 1)
                        nc.vector.scalar_tensor_tensor(x2[:, p, j, :], k.tile_out(ps[:, 6:8], j), 0.5, xb[:, j, :],
                                                       ALU.mult, ALU.add).then_inc(x2_ready, 1)
                    s = Steps(dve, steps, v, 2 * TC)
                    dve.wait_ge(x2_ready, TC * v + TC)
                    for j in range(TC):
                        s(nc.vector.bn_stats(st[:, j, :], x2[:, p, j, :]))
                    s.wait()
                    k.passed(nc.vector)
                    for j in range(TC):
                        s(nc.vector.bn_aggr(mv[:, j, :], st[:, j, :]))
                    s.wait()
                    s.end()
                    nc.vector.tensor_scalar(ve[:], mv[:, :, 1], EPS, None, ALU.add).then_inc(var, 1)
                    dve.wait_ge(rstd, v + 1)
                    dve.wait_ge(turned, v + 1)
                    for j in range(TC):
                        nc.vector.tensor_scalar(hn[:, j, :], x2[:, p, j, :], mv[:, j, 0:1], rs[:, j:j + 1],
                                                ALU.subtract, ALU.mult).then_inc(hn_ready, 1)
                if old:
                    for j in range(TC):
                        dve.wait_ge(hx_ready, TC * u + j + 1)
                        dve.wait_ge(f2, TC * u + TC + max(j, 1) + 1)
                        nc.vector.tensor_tensor(k.H[:, ds(TC * u + j, 1), :], k.tile_out(ps, j), hx[:, old[1], j, :],
                                                ALU.add).then_inc(done, 1)

            overlapped(dve, NCH, 2, step)


def quant_rows(k, ps, xqT, dq):
    nc = k.nc
    with stage(k) as c:
        st = k.sb(c, "s5_stats", [P, TC, 6])
        mv = k.sb(c, "s5_meanvar", [P, TC, 2])
        ve = k.sb(c, "s5_var_eps", [P, TC])
        rs = k.sb(c, "s5_rstd", [P, TC])
        xs = k.sb(c, "s5_x", [P, TC, D])
        am = k.sb(c, "s5_absmax", [P, TC])
        rec = k.sb(c, "s5_inv_absmax", [P, TC])
        xq = k.sb(c, "s5_xq", [P, TC, D], BF16)
        steps, var, rstd = k.sem("s5_steps"), k.sem("s5_var"), k.sem("s5_rstd_ready")
        quant, turned, stored = k.sem("s5_quant"), k.sem("s5_turned"), k.sem("s5_stored")
        block = c.enter_context(nc.Block())
        tp = ps[:, 0, :].bitcast(BF16)[:, 0:DM * CW].rearrange("p (m t) -> p m t", m=DM)

        @block.vector
        def _(dve):
            nc.vector.sem_inc(turned, 1)
            with dve.Fori(0, NCH) as i:
                s = Steps(dve, steps, i, 4 * TC + 5)
                for j in range(TC):
                    s(nc.vector.bn_stats(st[:, j, :], k.H[:, ds(TC * i + j, 1), :]))
                s.wait()
                k.passed(nc.vector)
                for j in range(TC):
                    s(nc.vector.bn_aggr(mv[:, j, :], st[:, j, :]))
                s.wait()
                nc.vector.tensor_scalar(ve[:], mv[:, :, 1], EPS, None, ALU.add).then_inc(var, 1)
                dve.wait_ge(rstd, i + 1)
                for j in range(TC):
                    s(nc.vector.tensor_scalar(xs[:, j, :], k.H[:, ds(TC * i + j, 1), :],
                                              mv[:, j, 0:1], rs[:, j:j + 1], ALU.subtract, ALU.mult))
                s.wait()
                s(nc.vector.tensor_reduce(am[:], xs[:], AX.X, ALU.max, apply_absolute_value=True))
                s.wait()
                s(nc.vector.tensor_scalar(am[:], am[:], 1e-5, None, ALU.max))
                s.wait()
                s(nc.vector.reciprocal(rec[:], am[:]))
                s(nc.vector.tensor_scalar(dq[:, ds(TC * i, TC)], am[:], 1.0 / 127.0, None, ALU.mult))
                s.wait()
                s(nc.vector.tensor_scalar(rec[:], rec[:], 127.0, None, ALU.mult))
                s.wait()
                for j in range(TC):
                    s(nc.vector.tensor_scalar(xs[:, j, :], xs[:, j, :], rec[:, j:j + 1], MAGIC, ALU.mult, ALU.add))
                s.wait()
                dve.wait_ge(turned, i + 1)
                nc.vector.tensor_scalar(xq[:], xs[:], MAGIC, 127.0, ALU.subtract, ALU.min).then_inc(quant, 1)
                s.end()

        @block.gpsimd
        def _(pool):
            with pool.Fori(0, NCH) as i:
                pool.wait_ge(var, i + 1)
                nc.gpsimd.tensor_tensor(rs[:], ve[:], k.mhalf[:, 0:TC], ALU.pow).then_inc(rstd, 1)

        @block.tensor
        def _(pe):
            nc.tensor.sem_inc(stored, 1)
            with pe.Fori(0, NCH) as i:
                pe.wait_ge(stored, i + 1)
                pe.wait_ge(quant, i + 1)
                for j in range(TC):
                    for m in range(DM):
                        last = nc.tensor.transpose(tp[:, m, j * P:j * P + P], xq[:, j, m * P:m * P + P], k.identb[:])
                last.then_inc(turned, 1)

        @block.scalar
        def _(act):
            with act.Fori(0, NCH) as i:
                act.wait_ge(turned, i + 2)
                nc.scalar.activation(xqT[:, :, ds(CW * i, CW)], tp, ACT.Copy).then_inc(stored, 1)


def ternary_ffn(k, ps, xqT, dq):
    nc = k.nc
    with stage(k) as c:
        dqg = k.sb(c, "s5_gate_scale", [P, NT])
        dqu = k.sb(c, "s5_up_scale", [P, NT])
        sg = k.sb(c, "s5_silu", [P, 2, INNER])
        g = k.sb(c, "s5_g", [P, 2, INNER])
        gq = k.sb(c, "s5_gq", [P, 2, INNER], BF16)
        gqT = k.sb(c, "s5_gqT", [P, 2, FM, P], BF16)
        am = k.sb(c, "s5_g_absmax", [P, 2])
        rec = k.sb(c, "s5_g_inv_absmax", [P, 2])
        dqd = k.sb(c, "s5_down_scale", [P, NT])
        names = ("scales", "gate", "up", "silu", "g", "steps", "rec", "scaled", "gq", "turned", "gqT", "down", "done")
        (scales, gate, up, silu, g_ready, steps, rec_ready, scaled, gq_ready, turned, gqT_ready, down,
         done) = (k.sem("s5b_" + n) for n in names)
        block = c.enter_context(nc.Block())
        tp = [ps[:, 4 + p, :].bitcast(BF16).rearrange("p (m t) -> p m t", m=FM) for p in range(2)]

        @block.tensor
        def _(pe):
            nc.tensor.sem_inc(silu, 2)
            nc.tensor.sem_inc(g_ready, 2)
            nc.tensor.sem_inc(done, 2)

            def front(i, p):
                t = 2 * i + p
                for h in range(2):
                    pe.wait_ge(silu, 2 * t + h + 1)
                    for q in range(DM):
                        last = nc.tensor.matmul(ps[:, 2 * h, :], xqT[:, q, ds(P * t, P)],
                                                k.wq["w_gate"][:, q, 512 * h:512 * h + 512],
                                                start=(q == 0), stop=(q == DM - 1))
                    last.then_inc(gate, 1)
                    pe.wait_ge(g_ready, 2 * t + h + 1)
                    for q in range(DM):
                        last = nc.tensor.matmul(ps[:, 2 * h + 1, :], xqT[:, q, ds(P * t, P)],
                                                k.wq["w_up"][:, q, 512 * h:512 * h + 512],
                                                start=(q == 0), stop=(q == DM - 1))
                    last.then_inc(up, 1)

            def back(i, p):
                t = 2 * i + p
                pe.wait_ge(gq_ready, t + 3)
                for m in range(FM):
                    last = nc.tensor.transpose(tp[p][:, m, :], gq[:, p, m * P:m * P + P], k.identb[:])
                last.then_inc(turned, 1)
                pe.wait_ge(gqT_ready, t + 1)
                pe.wait_ge(done, t + 1)
                for m in range(FM):
                    last = nc.tensor.matmul(ps[:, 6 + p, 0:D], gqT[:, p, m, :], k.wq["w_down"][:, m, :],
                                            start=(m == 0), stop=(m == FM - 1))
                last.then_inc(down, 1)

            def step(new, middle, old):
                if new:
                    front(*new)
                if old:
                    back(*old)

            overlapped_twice(pe, NT, step)

        @block.scalar
        def _(act):
            act.wait_ge(scales, 2)

            def front(i, p):
                t = 2 * i + p
                for h in range(2):
                    act.wait_ge(gate, 2 * t + h + 1)
                    act.wait_ge(g_ready, 2 * t + h + 1)
                    k.passed(nc.scalar)
                    nc.scalar.activation(sg[:, p, 512 * h:512 * h + 512], ps[:, 2 * h, :], ACT.Silu,
                                         scale=dqg[:, ds(t, 1)]).then_inc(silu, 1)

            def back(i, p):
                act.wait_ge(turned, 2 * i + p + 1)
                act.wait_ge(down, 2 * i + p + 1)
                nc.scalar.activation(gqT[:, p], tp[p], ACT.Copy).then_inc(gqT_ready, 1)

            def step(new, middle, old):
                if new:
                    front(*new)
                if old:
                    back(*old)
                if middle:
                    i, p = middle
                    act.wait_ge(rec_ready, 2 * i + p + 1)
                    k.passed(nc.scalar)
                    nc.scalar.activation(g[:, p, :], g[:, p, :], ACT.Copy, scale=rec[:, p:p + 1]).then_inc(scaled, 1)

            nc.scalar.sem_inc(down, 2)
            overlapped_twice(act, NT, step)

        @block.vector
        def _(dve):
            nc.vector.tensor_scalar(dqg[:], dq[:], k.wmean[:, 0:1], None, ALU.mult).then_inc(scales, 1)
            nc.vector.tensor_scalar(dqu[:], dq[:], k.wmean[:, 1:2], None, ALU.mult).then_inc(scales, 1)
            dve.wait_ge(scales, 2)

            nc.vector.sem_inc(gq_ready, 2)

            def front(i, p):
                t = 2 * i + p
                dve.wait_ge(gq_ready, t + 1)
                for h in range(2):
                    dve.wait_ge(silu, 2 * t + 2 + h + 1)
                    dve.wait_ge(up, 2 * t + h + 1)
                    cols = slice(512 * h, 512 * h + 512)
                    nc.vector.scalar_tensor_tensor(g[:, p, cols], ps[:, 2 * h + 1, :], dqu[:, ds(t, 1)], sg[:, p, cols],
                                                   ALU.mult, ALU.mult).then_inc(g_ready, 1)
                s = Steps(dve, steps, t, 4)
                dve.wait_ge(g_ready, 2 * t + 4)
                s(nc.vector.tensor_reduce(am[:, p:p + 1], g[:, p, :], AX.X, ALU.max, apply_absolute_value=True))
                s.wait()
                s(nc.vector.tensor_scalar(am[:, p:p + 1], am[:, p:p + 1], 1e-5, None, ALU.max))
                s.wait()
                s(nc.vector.reciprocal(rec[:, p:p + 1], am[:, p:p + 1]))
                s(nc.vector.tensor_scalar(dqd[:, ds(t, 1)], am[:, p:p + 1], k.wmean[:, 2:3], 1.0 / 127.0,
                                          ALU.mult, ALU.mult))
                s.wait()
                s.end()
                nc.vector.tensor_scalar(rec[:, p:p + 1], rec[:, p:p + 1], 127.0, None, ALU.mult).then_inc(rec_ready, 1)

            def rounded(i, p):
                dve.wait_ge(scaled, 2 * i + p + 1)
                nc.vector.tensor_scalar(gq[:, p, :], g[:, p, :], MAGIC, MAGIC, ALU.add, ALU.subtract).then_inc(gq_ready, 1)

            def back(i, p):
                t = 2 * i + p
                dve.wait_ge(down, t + 3)
                nc.vector.scalar_tensor_tensor(k.H[:, ds(t, 1), :], ps[:, 6 + p, 0:D], dqd[:, ds(t, 1)],
                                               k.H[:, ds(t, 1), :], ALU.mult, ALU.add).then_inc(done, 1)

            def step(new, middle, old):
                if new:
                    front(*new)
                if middle:
                    rounded(*middle)
                if old:
                    back(*old)

            overlapped_twice(dve, NT, step)


def attention_inputs(k, ps, qT, kT):
    nc = k.nc
    W = k.weights
    with stage(k) as c:
        st = k.sb(c, "s6_stats", [P, TC, 6])
        mv = k.sb(c, "s6_meanvar", [P, TC, 2])
        ve = k.sb(c, "s6_var_eps", [P, TC])
        rs = k.sb(c, "s6_rstd", [P, TC])
        xs = k.sb(c, "s6_x", [P, TC, D])
        xT = k.sb(c, "s6_xT", [P, 2, DM, CW])
        vs = k.sb(c, "s6_v", [P, 2, TC, D])
        names = ("steps", "var", "rstd", "normed", "turned", "xT", "qk", "qk_out", "v", "v_out", "kept")
        (steps, var, rstd, normed, turned, xT_ready, qk, qk_out, v_ready, v_out, kept) = (k.sem("s6_" + n) for n in names)
        v_stored = [k.sem(f"s6_v_stored{n}") for n in range(2)]
        block = c.enter_context(nc.Block())

        @block.vector
        def _(dve):
            nc.vector.sem_inc(turned, 1)
            nc.vector.sem_inc(kept, 1)
            for n in range(2):
                nc.vector.sem_inc(v_stored[n], 16)

            def step(new, old):
                if new:
                    v = 2 * new[0] + new[1]
                    s = Steps(dve, steps, v, 2 * TC)
                    for j in range(TC):
                        s(nc.vector.bn_stats(st[:, j, :], k.H[:, ds(TC * v + j, 1), :]))
                    s.wait()
                    k.passed(nc.vector)
                    for j in range(TC):
                        s(nc.vector.bn_aggr(mv[:, j, :], st[:, j, :]))
                    s.wait()
                    s.end()
                    nc.vector.tensor_scalar(ve[:], mv[:, :, 1], EPS, None, ALU.add).then_inc(var, 1)
                    dve.wait_ge(rstd, v + 1)
                    dve.wait_ge(turned, v + 1)
                    dve.wait_ge(kept, v + 1)
                    for j in range(TC):
                        nc.vector.tensor_scalar(xs[:, j, :], k.H[:, ds(TC * v + j, 1), :],
                                                mv[:, j, 0:1], rs[:, j:j + 1], ALU.subtract, ALU.mult).then_inc(normed, 1)
                if old:
                    u, n = 2 * old[0] + old[1], old[1]
                    dve.wait_ge(v_stored[n], 16 * old[0] + 16)
                    for j in range(TC):
                        dve.wait_ge(v_ready, TC * u + max(j, 1) + 1)
                        nc.vector.tensor_tensor(vs[:, n, j, :], k.tile_out(ps[:, 6:8], j), k.row("bv"),
                                                ALU.add).then_inc(v_out, 1)

            overlapped(dve, NCH, 2, step)

        @block.gpsimd
        def _(pool):
            with pool.Fori(0, NCH) as i:
                pool.wait_ge(var, i + 1)
                nc.gpsimd.tensor_tensor(rs[:], ve[:], k.mhalf[:, 0:TC], ALU.pow).then_inc(rstd, 1)
                pool.wait_ge(normed, TC * i + TC)
                nc.gpsimd.tensor_copy(k.X[:, ds(TC * i, TC), :], xs[:]).then_inc(kept, 1)

        @block.tensor
        def _(pe):
            nc.tensor.sem_inc(v_out, TC)
            nc.tensor.sem_inc(qk_out, 4)
            nc.tensor.sem_inc(xT_ready, DM)

            def step(new, old):
                if old:
                    u = 2 * old[0] + old[1]
                    pe.wait_ge(qk_out, 4 * u + 4)
                    for n, w in enumerate(("Wq", "Wk")):
                        for m in range(DM):
                            for q in range(DM):
                                last = nc.tensor.matmul(ps[:, 2 + 2 * n + m, 0:CW], W[w][:, q, m * P:m * P + P],
                                                        xT[:, old[1], q, :], start=(q == 0), stop=(q == DM - 1))
                            last.then_inc(qk, 1)
                if new:
                    v = 2 * new[0] + new[1]
                    pe.wait_ge(xT_ready, DM * v + DM)
                    for j in range(TC):
                        pe.wait_ge(normed, TC * v + j + 1)
                        for m in range(DM):
                            last = nc.tensor.transpose(ps[:, m, j * P:j * P + P], xs[:, j, m * P:m * P + P], k.ident[:])
                    last.then_inc(turned, 1)
                if old:
                    pe.wait_ge(v_out, TC * u + TC)
                    for j in range(TC):
                        for q in range(DM):
                            last = nc.tensor.matmul(k.tile_out(ps[:, 6:8], j), xT[:, old[1], q, j * P:j * P + P],
                                                    W["Wv"][:, q, :], start=(q == 0 and j != 1), stop=(q == DM - 1),
                                                    skip_group_check=True)
                        last.then_inc(v_ready, 1)
                if new:
                    pe.wait_ge(xT_ready, DM * v + 2 * DM)

            overlapped(pe, NCH, 2, step)

        @block.scalar
        def _(act):
            def step(new, old):
                if old:
                    u = 2 * old[0] + old[1]
                    for m in range(DM):
                        act.wait_ge(qk, 4 * u + m + 1)
                        nc.scalar.activation(qT[:, m, ds(CW * u, CW)], ps[:, 2 + m, 0:CW], ACT.Identity, scale=0.25,
                                             bias=k.quarter_bq[:, m:m + 1]).then_inc(qk_out, 1)
                    for m in range(DM):
                        act.wait_ge(qk, 4 * u + DM + m + 1)
                        nc.scalar.activation(kT[:, m, ds(CW * u, CW)], ps[:, 4 + m, 0:CW], ACT.Identity,
                                             bias=k.vec("bk", m)).then_inc(qk_out, 1)
                if new:
                    act.wait_ge(turned, 2 * new[0] + new[1] + 2)
                    for m in range(DM):
                        nc.scalar.activation(xT[:, new[1], m, :], ps[:, m, 0:CW], ACT.Copy).then_inc(xT_ready, 1)

            overlapped(act, NCH, 2, step)

        @block.sync
        def _(sp):
            with sp.Fori(0, NCH // 2) as i:
                for n in range(2):
                    sp.wait_ge(v_out, 2 * TC * i + TC * n + 2 * TC)
                    sp.dma_start(k.v_dram.rearrange("(t p) d -> p t d", p=P)[:, ds(2 * TC * i + TC * n, TC), :],
                                 vs[:, n]).then_inc(v_stored[n], 16)
            for n in range(2):
                sp.wait_ge(v_stored[n], 16 * (NCH // 2) + 16)


def attention(k, ps, qT, kT, fT):
    nc = k.nc
    NU = 2 * B
    NV8 = HG + HG
    with stage(k) as c:
        kb = k.sb(c, "s7_key_blocks", [P, 2, NKC, P])
        vb = k.sb(c, "s7_value_blocks", [P, 2, NKC, P])
        v8 = k.sb(c, "s7_values", [P, 2, NKC, D])
        a = k.sb(c, "s7_abs", [P, 2, NKC, L])
        w = k.sb(c, "s7_ln_cauchy", [P, NKC, L])
        pw = k.sb(c, "s7_exp_and_cauchy", [P, 2, NKC, 2 * L])
        zs = k.sb(c, "s7_chunk_sums", [P, 2, 2 * L])
        mx = k.sb(c, "s7_max", [P, L])
        cm = k.sb(c, "s7_head_max", [P, 2, HG])
        nm = k.sb(c, "s7_neg_max", [HG, L], BF16)
        lz = k.sb(c, "s7_ln_sums", [P, 2 * L])
        rz = k.sb(c, "s7_inv_sums", [P, 2 * L])
        t1 = k.sb(c, "s7_softmax_part", [P, L])
        t2 = k.sb(c, "s7_cauchy_part", [P, L])
        hsel = k.sb(c, "s7_head_rows", [HG, P], BF16)
        hself = k.sb(c, "s7_head_rows_f32", [HG, P])
        hsum = k.sb(c, "s7_head_sum", [P, 2, P])
        tb = k.sb(c, "s7_tb2", [P, 2])
        tbb = k.sb(c, "s7_tb", [P, 2])
        names = ("const", "tb1", "hsel", "kb", "vb", "scores", "max", "abs", "t1", "cm", "t2", "nm", "shifted", "exp",
                 "sq", "ln", "cauchy", "exp_summed", "cauchy_summed", "sums", "lz", "rz", "parts")
        (const, tb1, hsel_ready, kb_ready, vb_ready, scores, max_ready, abs_ready, t1_ready, cm_ready, t2_ready,
         nm_ready, shifted, exp_ready, sq_ready, ln_ready, cauchy, exp_summed, cauchy_summed, sums, lz_ready, rz_ready,
         parts) = (k.sem("s7_" + n) for n in names)
        v_in = [k.sem(f"s7_v_in{n}") for n in range(2)]
        block = c.enter_context(nc.Block())

        def bank(n, j):
            return ps[:, 3 * n + j // KB, (j % KB) * L:(j % KB) * L + L]

        def banks(n):
            return ps[:, 3 * n:3 * n + 3, 0:KB * L]

        o_pw, z_p = ps[:, 6, 0:2 * L], ps[:, 6, 2 * L:3 * L]
        tr1, tr2, z_w = ps[:, 7, 0:P], ps[0:L - P, 7, P:2 * P], ps[:, 7, 2 * P:2 * P + L]
        cm_t = ps[0:HG, 7, 0:L]

        @block.sync
        def _(sp):
            sp.dma_start(hself[:], k.dram["head_rows"]).then_inc(const, 16)
            sp.dma_start(hsum[:], k.dram["head_sum"]).then_inc(const, 16)
            with sp.Fori(0, B // 2) as i:
                for n in range(2):
                    b = 2 * i + n
                    sp.wait_ge(vb_ready, 8 * i + 4 * n + 4)
                    for h in range(HG):
                        rows = slice(DH * h, DH * h + DH)
                        src = k.v_dram[ds(L * b, (NKC - 1) * DH), :].rearrange("(j m) d -> m j d", m=DH)
                        sp.dma_start(v8[rows, n, 0:NKC - 1, :], src).then_inc(v_in[n], 16)
                        sp.dma_start(v8[rows, n, NKC - 1, :],
                                     k.v_dram[ds(L * b + LAST0, DH), :]).then_inc(v_in[n], 16)

        @block.gpsimd
        def _(pool):
            nc.gpsimd.sem_inc(vb_ready, 8)
            pool.wait_ge(const, 32)
            same_head = hsum[:, 0:1, :].to_broadcast([P, NKC - 1, P])

            def over_heads(keys):
                return keys.rearrange("p (j h m) -> p j h m", h=1, m=DH)

            def keys(i, p):
                u, n, b = 4 * i + p, p % 2, 2 * i + p // 2
                pool.wait_ge(scores, u + 1)
                k.passed(nc.gpsimd)
                out = kb[:, n].rearrange("p j (h m) -> p j h m", h=HG)
                mask = hsum[:, 0:1, :].rearrange("p j (h m) -> p j h m", h=HG)
                nk = NKC - 1
                nc.gpsimd.tensor_tensor(out[:, 0:nk], over_heads(kT[:, n, ds(L * b, nk * DH)]).to_broadcast([P, nk, HG, DH]),
                                        mask.to_broadcast([P, nk, HG, DH]), ALU.mult).then_inc(kb_ready, 1)
                nc.gpsimd.tensor_tensor(out[:, nk], over_heads(kT[:, n, ds(L * b + LAST0, DH)])[:, 0].to_broadcast([P, HG, DH]),
                                        mask[:, 0], ALU.mult).then_inc(kb_ready, 1)

            def values(i, p):
                u, n, slot = 4 * i + p, p % 2, p // 2
                if n == 0:
                    pool.wait_ge(v_in[slot], 16 * NV8 * (i + 1))
                pool.wait_ge(sums, u + 1)
                cols = slice(P * n, P * n + P)
                nc.gpsimd.tensor_tensor(vb[:, n, 0:NKC - 1, :], v8[:, slot, 0:NKC - 1, cols], same_head,
                                        ALU.mult).then_inc(vb_ready, 1)
                nc.gpsimd.tensor_tensor(vb[:, n, NKC - 1, :], v8[:, slot, NKC - 1, cols], hsum[:, 1, :],
                                        ALU.mult).then_inc(vb_ready, 1)

            pipelined(pool, NU, 4, keys, values)

        @block.tensor
        def _(pe):
            nc.tensor.sem_inc(scores, 2)
            nc.tensor.sem_inc(sums, 2)
            pe.wait_ge(const, 32)
            pe.wait_ge(hsel_ready, 1)

            def score(i, p):
                u, n, b = 4 * i + p, p % 2, 2 * i + p // 2
                pe.wait_ge(kb_ready, 2 * u + 2)
                pe.wait_ge(exp_ready, u + 1)
                for j in range(NKC):
                    last = nc.tensor.matmul(bank(n, j), kb[:, n, j, :], qT[:, n, ds(L * b, L)],
                                            start=(j % KB == 0), stop=False, skip_group_check=True)
                last.then_inc(scores, 1)

            def outputs(i, p, chunks):
                u, n = 4 * i + p, p % 2
                if 0 in chunks:
                    pe.wait_ge(vb_ready, 2 * u + 10)
                    pe.wait_ge(parts, 3 * u + 3)
                    pe.wait_ge(exp_ready, u + 3)
                    pe.wait_ge(cauchy, u + 2)
                for j in chunks:
                    nc.tensor.matmul(o_pw, vb[:, n, j, :], pw[:, n, j, :], start=(j == 0), stop=(j == NKC - 1),
                                     skip_group_check=True)

            def turn_maxima(i, p):
                pe.wait_ge(max_ready, 4 * i + p + 1)
                nc.tensor.transpose(tr1, mx[:, 0:P], k.ident[:])
                nc.tensor.transpose(tr2, mx[:, P:L], k.ident[:]).then_inc(t1_ready, 1)

            def turn_head_maxima(i, p):
                pe.wait_ge(cm_ready, 2 * (4 * i + p) + 2)
                nc.tensor.transpose(cm_t[:, 0:P], cm[:, 0, :], k.ident[:])
                nc.tensor.transpose(cm_t[:, P:L], cm[0:L - P, 1, :], k.ident[0:L - P, 0:L - P]).then_inc(t2_ready, 1)

            def shift(i, p):
                u, n = 4 * i + p, p % 2
                pe.wait_ge(nm_ready, u + 1)
                pe.wait_ge(abs_ready, u + 1)
                for r in range(3):
                    last = nc.tensor.matmul(ps[:, 3 * n + r, 0:KB * L].rearrange("p (j l) -> p j l", j=KB), hsel[:],
                                            nm[:].rearrange("h (o l) -> h o l", o=1).to_broadcast([HG, KB, L]),
                                            start=False, stop=True, skip_group_check=True)
                last.then_inc(shifted, 1)

            def head_sums(i, p):
                u, n = 4 * i + p, p % 2
                pe.wait_ge(exp_summed, u + 1)
                pe.wait_ge(cauchy_summed, u + 1)
                for dst, cols in ((z_p, slice(0, L)), (z_w, slice(L, 2 * L))):
                    nc.tensor.matmul(dst, hsum[:, 0, :], zs[:, n, cols], start=(dst is z_w), stop=False,
                                     skip_group_check=True)
                    last = nc.tensor.matmul(dst, hsum[:, 1, :], pw[:, n, NKC - 1, cols], start=False, stop=True,
                                            skip_group_check=True)
                last.then_inc(sums, 1)

            def step(new, old):
                if new:
                    score(*new)
                if old:
                    outputs(*old, range(0, 4))
                if new:
                    turn_maxima(*new)
                if old:
                    outputs(*old, range(4, 7))
                if new:
                    turn_head_maxima(*new)
                if old:
                    outputs(*old, range(7, NKC))
                if new:
                    shift(*new)
                if old:
                    head_sums(*old)

            overlapped(pe, NU, 4, step)

        @block.scalar
        def _(act):
            nc.scalar.sem_inc(exp_ready, 2)
            nc.scalar.sem_inc(sq_ready, 2)
            nc.scalar.sem_inc(cauchy, 1)
            act.wait_ge(const, 32)
            nc.scalar.preload_act_table_set("natural_log_exp_and_others")
            nc.scalar.activation(hsel[:], hself[:], ACT.Copy).then_inc(hsel_ready, 1)
            act.wait_ge(tb1, 2)

            def step(new, old):
                if new:
                    u, n = 4 * new[0] + new[1], new[1] % 2
                    act.wait_ge(abs_ready, u + 1)
                    act.wait_ge(cauchy, u + 1)
                    nc.scalar.activation(w[:], a[:, n], ACT.Square, bias=k.vec("beta", n)).then_inc(sq_ready, 1)
                    act.wait_ge(sq_ready, u + 3)
                    nc.scalar.activation(w[:], w[:], ACT.Ln, bias=tb[:, n:n + 1]).then_inc(ln_ready, 1)
                    act.wait_ge(shifted, u + 1)
                    act.wait_ge(sums, u + 1)
                    nc.scalar.activation(pw[:, n, :, 0:L].rearrange("p (r j) l -> p r j l", r=3),
                                         banks(n).rearrange("p r (j l) -> p r j l", j=KB), ACT.Exp).then_inc(exp_ready, 1)
                if old:
                    u = 4 * old[0] + old[1]
                    act.wait_ge(sums, u + 3)
                    act.wait_ge(parts, 3 * u + 3)
                    nc.scalar.activation(lz[:, 0:L], z_p, ACT.Ln).then_inc(lz_ready, 1)
                    nc.scalar.activation(lz[:, L:2 * L], z_w, ACT.Ln).then_inc(lz_ready, 1)
                    act.wait_ge(lz_ready, 2 * u + 2)
                    nc.scalar.activation(rz[:], lz[:], ACT.Exp, scale=-1.0).then_inc(rz_ready, 1)
                if new:
                    u, n = 4 * new[0] + new[1], new[1] % 2
                    act.wait_ge(ln_ready, u + 1)
                    nc.scalar.activation(pw[:, n, :, L:2 * L], w[:], ACT.Exp, scale=-1.0).then_inc(cauchy, 1)

            overlapped(act, NU, 4, step)

        @block.vector
        def _(dve):
            at, bt = VEC["t"][0], VEC["beta"][0]
            nc.vector.sem_inc(parts, 3)
            nc.vector.tensor_tensor(tbb[:], k.vecs[:, at:at + 2], k.vecs[:, bt:bt + 2], ALU.mult).then_inc(tb1, 1)
            dve.wait_ge(tb1, 1)
            nc.vector.tensor_tensor(tb[:], tbb[:], tbb[:], ALU.mult).then_inc(tb1, 1)

            def chunk_sums(n, cols):
                return nc.vector.tensor_reduce(zs[:, n, cols], pw[:, n, 0:NKC - 1, cols].rearrange("p j l -> p l j"),
                                               AX.X, ALU.add)

            def step(new, old):
                if new:
                    u, n = 4 * new[0] + new[1], new[1] % 2
                    dve.wait_ge(scores, u + 3)
                    src = banks(n).rearrange("p r (j l) -> p l r j", j=KB)
                    nc.vector.tensor_reduce(mx[:], src, AX.XY, ALU.max).then_inc(max_ready, 1)
                    dve.wait_ge(sq_ready, u + 1)
                    nc.vector.tensor_scalar(a[:, n].bitcast(I32).rearrange("p (r j) l -> p r (j l)", r=3),
                                            banks(n).bitcast(I32), 0x7FFFFFFF, None, ALU.bitwise_and).then_inc(abs_ready, 1)
                    dve.wait_ge(t1_ready, u + 1)
                    nc.vector.tensor_reduce(cm[:, 0, :], tr1.rearrange("p (h m) -> p h m", h=HG), AX.X,
                                            ALU.max).then_inc(cm_ready, 1)
                    nc.vector.tensor_reduce(cm[0:L - P, 1, :], tr2.rearrange("p (h m) -> p h m", h=HG), AX.X,
                                            ALU.max).then_inc(cm_ready, 1)
                if old:
                    u, n = 4 * old[0] + old[1], old[1] % 2
                    dve.wait_ge(cauchy, u + 2)
                    chunk_sums(n, slice(L, 2 * L)).then_inc(cauchy_summed, 1)
                if new:
                    u, n = 4 * new[0] + new[1], new[1] % 2
                    dve.wait_ge(t2_ready, u + 1)
                    nc.vector.tensor_scalar(nm[:], cm_t, -1.0, None, ALU.mult).then_inc(nm_ready, 1)
                    dve.wait_ge(exp_ready, u + 3)
                    chunk_sums(n, slice(0, L)).then_inc(exp_summed, 1)
                if old:
                    u, n, b = 4 * old[0] + old[1], old[1] % 2, 2 * old[0] + old[1] // 2
                    dve.wait_ge(rz_ready, u + 1)
                    dve.wait_ge(parts, 3 * u + 3)
                    nc.vector.scalar_tensor_tensor(t1[:], o_pw[:, 0:L], 0.5, rz[:, 0:L], ALU.mult, ALU.mult).then_inc(parts, 1)
                    nc.vector.scalar_tensor_tensor(t2[:], o_pw[:, L:2 * L], 0.5, rz[:, L:2 * L], ALU.mult,
                                                   ALU.mult).then_inc(parts, 1)
                    dve.wait_ge(parts, 3 * u + 5)
                    nc.vector.tensor_tensor(fT[:, n, ds(L * b, L)], t1[:], t2[:], ALU.add).then_inc(parts, 1)

            overlapped(dve, NU, 4, step)


def attention_output(k, ps, fT):
    nc = k.nc
    W = k.weights
    with stage(k) as c:
        fs = k.sb(c, "s8_f", [P, DM, CW])
        hx = k.sb(c, "s8_hx", [P, TC, D])
        y = k.sb(c, "s8_y", [P, TC, D])
        st = k.sb(c, "s8_stats", [P, TC, 6])
        mv = k.sb(c, "s8_meanvar", [P, TC, 2])
        ve = k.sb(c, "s8_var_eps", [P, TC])
        rs = k.sb(c, "s8_rstd", [P, TC])
        names = ("staged", "hx1", "hx", "proj", "y", "steps", "var", "rstd", "done")
        staged, hx1, hx_ready, proj, y_ready, steps, var, rstd, done = (k.sem("s8_" + n) for n in names)
        block = c.enter_context(nc.Block())

        @block.gpsimd
        def _(pool):
            nc.gpsimd.sem_inc(proj, TC)
            nc.gpsimd.sem_inc(done, TC)
            with pool.Fori(0, NCH) as i:
                pool.wait_ge(proj, TC * i + TC)
                nc.gpsimd.tensor_copy(fs[:], fT[:, :, ds(CW * i, CW)]).then_inc(staged, 1)
                pool.wait_ge(done, TC * i + TC)
                nc.gpsimd.tensor_tensor(hx[:], k.H[:, ds(TC * i, TC), :], k.X[:, ds(TC * i, TC), :], ALU.add).then_inc(hx1, 1)
                pool.wait_ge(hx1, i + 1)
                for j in range(TC):
                    nc.gpsimd.tensor_tensor(hx[:, j, :], hx[:, j, :], k.row("ln_b"), ALU.add).then_inc(hx_ready, 1)
                pool.wait_ge(var, i + 1)
                nc.gpsimd.tensor_tensor(rs[:], ve[:], k.mhalf[:, 0:TC], ALU.pow).then_inc(rstd, 1)

        @block.tensor
        def _(pe):
            nc.tensor.sem_inc(y_ready, TC)
            with pe.Fori(0, NCH) as i:
                pe.wait_ge(staged, i + 1)
                pe.wait_ge(y_ready, TC * i + TC)
                for j in range(TC):
                    for q in range(DM):
                        last = nc.tensor.matmul(k.tile_out(ps, j), fs[:, q, j * P:j * P + P], W["Wo"][:, q, :],
                                                start=(q == 0 and j != 1), stop=(q == DM - 1), skip_group_check=True)
                    last.then_inc(proj, 1)

        @block.vector
        def _(dve):
            with dve.Fori(0, NCH) as i:
                s = Steps(dve, steps, i, 4 * TC)
                dve.wait_ge(done, TC * i + TC)
                for j in range(TC):
                    dve.wait_ge(proj, TC * i + TC + max(j, 1) + 1)
                    nc.vector.tensor_tensor(y[:, j, :], k.tile_out(ps, j), k.row("bo"), ALU.add).then_inc(y_ready, 1)
                dve.wait_ge(y_ready, TC * i + 2 * TC)
                for j in range(TC):
                    s(nc.vector.bn_stats(st[:, j, :], y[:, j, :]))
                s.wait()
                k.passed(nc.vector)
                for j in range(TC):
                    s(nc.vector.bn_aggr(mv[:, j, :], st[:, j, :]))
                s.wait()
                nc.vector.tensor_scalar(ve[:], mv[:, :, 1], EPS, None, ALU.add).then_inc(var, 1)
                dve.wait_ge(rstd, i + 1)
                for j in range(TC):
                    s(nc.vector.tensor_scalar(y[:, j, :], y[:, j, :], mv[:, j, 0:1], rs[:, j:j + 1],
                                              ALU.subtract, ALU.mult))
                s.wait()
                for j in range(TC):
                    s(nc.vector.tensor_tensor(y[:, j, :], y[:, j, :], k.row("ln_w"), ALU.mult))
                s.wait()
                for j in range(TC):
                    dve.wait_ge(hx_ready, TC * i + j + 1)
                    nc.vector.tensor_tensor(k.H[:, ds(TC * i + j, 1), :], y[:, j, :], hx[:, j, :], ALU.add).then_inc(done, 1)
                s.end()


def route(k, ps):
    nc = k.nc
    with stage(k) as c:
        sb = lambda name, shape, dt=F32: k.sb(c, "s9_" + name, shape, dt)
        st, mv, ve, rs = sb("stats", [P, TC, 6]), sb("meanvar", [P, TC, 2]), sb("var_eps", [P, TC]), sb("rstd", [P, TC])
        xs = sb("x", [P, 2, TC, D])
        xT = sb("xT", [P, DM, CW])
        logits, rest, found = sb("logits", [P, TC, E]), sb("logits_rest", [P, TC, E]), sb("found", [P, TC, E])
        top, which = sb("top2", [P, 2, TC]), sb("top2_index_less_8", [P, 2, TC])
        ex, den, diff = sb("exp", [P, TC]), sb("den", [P, TC]), sb("diff", [P, TC])
        oh = sb("one_hot", [P, 2, TC, E])
        both, before = sb("both", [P, TC, E]), sb("before", [P, TC, E])
        bothb = sb("both_bf16", [P, TC, E], BF16)
        total = sb("total", [P, TC + 1, E])
        totalb = sb("total_bf16", [P, TC, E], BF16)
        triub, onesb = sb("triu_bf16", [P, P], BF16), sb("ones_bf16", [P, P], BF16)
        junk = sb("junk", [P, 2, TC, E])
        rank, keep, slot, trash = (sb(n, [P, 2, TC]) for n in ("rank", "keep", "slot", "trash"))
        iota, iota8, pair = sb("iota", [P, E]), sb("iota_less_8", [P, E]), sb("pair", [P, NT, 2])
        valid = sb("valid", [P, NT])
        to = sb("scatter_index", [P, 2, TC, 2], I32)
        names = ("consts", "init", "steps", "bsteps", "var", "rstd", "xs", "turned", "xT", "logits", "logits_out",
                 "diff", "exp", "both", "rank", "to", "xs_free")
        (consts, init, steps, bsteps, var, rstd, xs_ready, turned, xT_ready, logits_ready, logits_out, diff_ready,
         exp_ready, both_ready, rank_ready, to_ready, xs_free) = (k.sem("s9_" + n) for n in names)
        scattered = [k.sem(f"s9_scattered{n}") for n in range(2)]
        w1_in, w2_in, w1_high = k.sem("s9_w1_in"), k.sem("s9_w2_in"), k.sem("s9_w1_high")
        block = c.enter_context(nc.Block())

        def over_experts(x):
            return x.rearrange("p (t e) -> p t e", e=1).to_broadcast([P, TC, E])

        def over_tiles(x):
            return x.rearrange("p (t e) -> p t e", t=1).to_broadcast([P, TC, E])

        def over_pair(x):
            return x.rearrange("p (j t) -> p j t", j=1).to_broadcast([P, 2, TC])

        @block.sync
        def _(sp):
            sp.dma_start(iota[:], k.dram["iota"]).then_inc(consts, 16)
            sp.dma_start(pair[:], k.dram["pair"]).then_inc(consts, 16)
            sp.dma_start(valid[:], k.dram["valid"]).then_inc(consts, 16)
            sp.dma_start(k.w1[:], k.dram["w1"][:, 0:1]).then_inc(w1_in, 16)
            sp.dma_start(k.w2[:], k.dram["w2"][:, 0:1]).then_inc(w2_in, 16)
            sp.sem_inc(xs_free, 2)
            with sp.Fori(0, NCH // 2) as i:
                for p in range(2):
                    sp.wait_ge(scattered[p], 32 * TC * i + 32 * TC)
                    sp.sem_inc(xs_free, 1)
            sp.wait_ge(w2_in, 16)

        @block.vector
        def _(dve):
            s = Steps(dve, init)
            dve.wait_ge(consts, 48)
            s(nc.vector.tensor_copy(triub[:], k.triu[:]))
            s(nc.vector.memset(onesb[:], 1.0))
            s(nc.vector.memset(total[:], 0.0))
            s(nc.vector.tensor_scalar(iota8[:], iota[:], float(-E), None, ALU.add))
            s.wait()

            def front(i, p):
                u = 2 * i + p
                h = k.H[:, ds(TC * u, TC), :]
                s = Steps(dve, steps, u, 2 * TC + 1)
                for j in range(TC):
                    s(nc.vector.bn_stats(st[:, j, :], k.H[:, ds(TC * u + j, 1), :]))
                s.wait()
                k.passed(nc.vector)
                for j in range(TC):
                    s(nc.vector.bn_aggr(mv[:, j, :], st[:, j, :]))
                s.wait()
                nc.vector.tensor_scalar(ve[:], mv[:, :, 1], EPS, None, ALU.add).then_inc(var, 1)
                dve.wait_ge(rstd, u + 1)
                dve.wait_ge(xs_free, u + 1)
                for j in range(TC):
                    nc.vector.tensor_scalar(xs[:, p, j, :], k.H[:, ds(TC * u + j, 1), :], mv[:, j, 0:1], rs[:, j:j + 1],
                                            ALU.subtract, ALU.mult).then_inc(xs_ready, 1)
                dve.wait_ge(xs_ready, TC * u + TC)
                s(nc.vector.tensor_tensor(h, h, xs[:, p], ALU.add))
                s.end()

            def back(i, p):
                u = 2 * i + p
                tiles = ds(TC * u, TC)
                s = Steps(dve, bsteps, u, 34)
                dve.wait_ge(logits_ready, u + 1)
                nc.vector.tensor_copy(logits[:], ps[:, 2 + p, 0:TC * E]).then_inc(logits_out, 1)
                dve.wait_ge(logits_out, u + 3)
                for j, x in enumerate((logits, rest)):
                    s(nc.vector.tensor_reduce(top[:, j, :], x[:], AX.X, ALU.max))
                    s.wait()
                    s(nc.vector.tensor_tensor(found[:], x[:], over_experts(top[:, j, :]), ALU.is_equal))
                    s.wait()
                    s(nc.vector.scalar_tensor_tensor(found[:], found[:], float(-E), over_tiles(iota[:]), ALU.mult, ALU.add))
                    s.wait()
                    s(nc.vector.tensor_reduce(which[:, j, :], found[:], AX.X, ALU.min))
                    s.wait()
                    s(nc.vector.tensor_tensor(oh[:, j], over_tiles(iota8[:]), over_experts(which[:, j, :]), ALU.is_equal))
                    s.wait()
                    if j == 0:
                        s(nc.vector.scalar_tensor_tensor(rest[:], oh[:, 0], -3e38, logits[:], ALU.mult, ALU.add))
                        s.wait()
                nc.vector.tensor_tensor(diff[:], top[:, 1, :], top[:, 0, :], ALU.subtract).then_inc(diff_ready, 1)
                for j in range(2):
                    s(nc.vector.tensor_tensor(oh[:, j], oh[:, j], valid[:, tiles].rearrange("p (t e) -> p t e", e=1)
                                              .to_broadcast([P, TC, E]), ALU.mult))
                s.wait()
                s(nc.vector.tensor_tensor(both[:], oh[:, 0], oh[:, 1], ALU.add))
                s.wait()
                s(nc.vector.tensor_copy(bothb[:], both[:]))
                for j in range(TC):
                    s(nc.vector.tensor_tensor(total[:, j + 1, :], total[:, j, :], both[:, j, :], ALU.add))
                    s.wait()
                nc.vector.tensor_copy(totalb[:], total[:, 0:TC, :]).then_inc(both_ready, 1)
                dve.wait_ge(both_ready, u + 1)
                s(nc.vector.tensor_copy(total[:, 0, :], total[:, TC, :]))
                dve.wait_ge(exp_ready, u + 1)
                s(nc.vector.tensor_scalar(den[:], ex[:], 1.0, None, ALU.add))
                s.wait()
                s(nc.vector.reciprocal(k.prob[:, 0, tiles], den[:]))
                s.wait()
                s(nc.vector.tensor_tensor(k.prob[:, 1, tiles], k.prob[:, 0, tiles], ex[:], ALU.mult))
                dve.wait_ge(rank_ready, u + 1)
                s(nc.vector.tensor_copy(before[:], ps[:, 4, 0:TC * E]))
                s.wait()
                for j in range(2):
                    s(nc.vector.tensor_tensor(junk[:, j], before[:], oh[:, j], ALU.mult))
                s.wait()
                s(nc.vector.tensor_reduce(rank[:], junk[:], AX.X, ALU.add))
                s.wait()
                s(nc.vector.tensor_scalar(keep[:], rank[:], float(CAP), None, ALU.is_lt))
                s(nc.vector.tensor_scalar(slot[:], rank[:], float(CAP - 1), float(E * CAPP), ALU.min, ALU.add))
                s.wait()
                s(nc.vector.scalar_tensor_tensor(slot[:], which[:], float(CAPP), slot[:], ALU.mult, ALU.add))
                s(nc.vector.tensor_tensor(keep[:], keep[:], over_pair(valid[:, tiles]), ALU.mult))
                s.wait()
                own = pair[:, tiles, :].rearrange("p t j -> p j t")
                s(nc.vector.tensor_tensor(k.prob[:, :, tiles], k.prob[:, :, tiles], keep[:], ALU.mult))
                s(nc.vector.tensor_tensor(trash[:], slot[:], own, ALU.subtract))
                s(nc.vector.tensor_copy(k.source[:, tiles, :].rearrange("p t j -> p j t"), slot[:]))
                s.wait()
                s(nc.vector.tensor_tensor(trash[:], trash[:], keep[:], ALU.mult))
                s.wait()
                nc.vector.tensor_tensor(to[:, p].rearrange("p t j -> p j t"), trash[:], own, ALU.add).then_inc(to_ready, 1)
                s.end()

            pipelined(dve, NCH, 2, front, back)
            dve.wait_ge(w1_in, 16)
            nc.vector.tensor_copy(k.w1_high[:], k.w1[:]).then_inc(w1_high, 1)

        @block.gpsimd
        def _(pool):
            def front(i, p):
                pool.wait_ge(var, 2 * i + p + 1)
                nc.gpsimd.tensor_tensor(rs[:], ve[:], k.mhalf[:, 0:TC], ALU.pow).then_inc(rstd, 1)

            def back(i, p):
                pool.wait_ge(to_ready, 2 * i + p + 1)
                k.passed(nc.gpsimd)
                for t in range(TC):
                    for j in range(2):
                        nc.gpsimd.indirect_dma_start(
                            k.slots_dram, bass.IndirectOffsetOnAxis(ap=to[:, p, t, j:j + 1], axis=0),
                            xs[:, p, t, :], None).then_inc(scattered[p], 16)

            pool.wait_ge(k.zero_filled, 16 * k.fills)
            pipelined(pool, NCH, 2, front, back)
            pool.wait_ge(w1_high, 1)
            nc.gpsimd.tensor_tensor(k.w1_low[:], k.w1[:], k.w1_high[:].bitcast(F32), ALU.subtract)
            for n in range(2):
                pool.wait_ge(scattered[n], 32 * TC * (NCH // 2))

        @block.tensor
        def _(pe):
            pe.wait_ge(init, 4)
            nc.tensor.sem_inc(xT_ready, DM)
            nc.tensor.sem_inc(logits_out, 2)

            def front(i, p):
                u = 2 * i + p
                pe.wait_ge(xT_ready, DM * u + DM)
                for j in range(TC):
                    pe.wait_ge(xs_ready, TC * u + j + 1)
                    for m in range(DM):
                        last = nc.tensor.transpose(ps[:, m, j * P:j * P + P], xs[:, p, j, m * P:m * P + P], k.ident[:])
                last.then_inc(turned, 1)
                pe.wait_ge(xT_ready, DM * u + 2 * DM)
                pe.wait_ge(logits_out, u + 1)
                for j in range(TC):
                    for q in range(DM):
                        last = nc.tensor.matmul(ps[:, 2 + p, j * E:j * E + E], xT[:, q, j * P:j * P + P],
                                                k.weights["router"][:, q, :], start=(j == 0 and q == 0),
                                                stop=(q == DM - 1), skip_group_check=True)
                last.then_inc(logits_ready, 1)

            def back(i, p):
                pe.wait_ge(both_ready, 2 * i + p + 1)
                nc.tensor.matmul(ps[:, 4, 0:TC * E], triub[:], bothb[:].rearrange("p t e -> p (t e)"), start=True, stop=False)
                nc.tensor.matmul(ps[:, 4, 0:TC * E], onesb[:], totalb[:].rearrange("p t e -> p (t e)"), start=False,
                                 stop=True).then_inc(rank_ready, 1)

            pipelined(pe, NCH, 2, front, back)

        @block.scalar
        def _(act):
            def front(i, p):
                u = 2 * i + p
                act.wait_ge(turned, u + 1)
                for m in range(DM):
                    nc.scalar.activation(xT[:, m, :], ps[:, m, 0:CW], ACT.Copy).then_inc(xT_ready, 1)

            def back(i, p):
                act.wait_ge(diff_ready, 2 * i + p + 1)
                nc.scalar.activation(ex[:], diff[:], ACT.Exp).then_inc(exp_ready, 1)

            pipelined(act, NCH, 2, front, back)


def split_products(nc, out, left, right, first, final):
    for r, (x, y) in enumerate(((0, 0), (0, 1), (1, 0))):
        last = nc.tensor.matmul(out, left[x], right[y], start=(first and r == 0), stop=(final and r == 2))
    return last


def experts(k, ps):
    nc = k.nc
    with stage(k) as c:
        w1, w2, w1h, w1l = k.w1, k.w2, k.w1_high, k.w1_low
        w2h, w2l = (k.sb(c, f"s10_w2_{n}", [P, FM, D], F32R) for n in ("high", "low"))
        rows = k.sb(c, "s10_rows", [CR, 2, CT, D])
        xTh, xTl = (k.sb(c, f"s10_xT_{n}", [P, 2, DM, CAPP], F32R) for n in ("high", "low"))
        hidh, hidl = (k.sb(c, f"s10_hidden_{n}", [P, FM, CAPP], F32R) for n in ("high", "low"))
        out = k.sb(c, "s10_out", [CR, CT, D])
        HC = CAPP // 2
        RING = 4
        hid = k.sb(c, "s10_hidden", [P, RING, HC])
        r_in = [k.sem(f"s10_rows_in{n}") for n in range(2)]
        names = ("w1_in", "w2_in", "turned", "xT", "h", "hid", "w1_high", "w1_low", "w2_high", "w2_low", "y", "out")
        (w1_in, w2_in, turned, xT_ready, h_ready, hid_ready, w1_high, w1_low, w2_high, w2_low, y_ready,
         out_ready) = (k.sem("s10_" + n) for n in names)
        low_ready = [k.sem(f"s10_hidden_low{n}") for n in range(2)]
        stored = [k.sem(f"s10_stored{n}") for n in range(2)]
        block = c.enter_context(nc.Block())
        NH = 2 * FM
        TURNS = {5: 0, 7: 1, 9: 2, 11: 3}

        def group(r):
            return r % FM, slice(r // FM * HC, r // FM * HC + HC)

        def hidden_low(eng, raw, e, r):
            f, cols = group(r)
            eng.wait_ge(hid_ready, NH * e + r + 3)
            raw.tensor_tensor(hidl[:, f, cols], hid[:, r % RING, :], hidh[:, f, cols].bitcast(F32),
                              ALU.subtract).then_inc(low_ready[r % 2], 1)

        @block.sync
        def _(sp):
            def load_rows(e, n):
                src = k.slots_dram[ds(CAPP * e, CAPP), :].rearrange("(t r) d -> r t d", r=CR)
                sp.dma_start(rows[:, n], src).then_inc(r_in[n], 16)

            def period(e, n, weights, more_rows):
                if more_rows:
                    sp.wait_ge(turned, 4 * e + 4)
                    load_rows(e + 2, n)
                if weights:
                    sp.wait_ge(w1_low, e + 1)
                    sp.dma_start(w1[:], k.dram["w1"][:, ds(e + 1, 1)]).then_inc(w1_in, 16)
                    sp.wait_ge(w2_low, e + 1)
                    sp.dma_start(w2[:], k.dram["w2"][:, ds(e + 1, 1)]).then_inc(w2_in, 16)
                for half in range(2):
                    sp.wait_ge(out_ready, CT * e + 3 * half + 3 + 2)
                    dst = k.outs_dram[ds(CAPP * e + 3 * CR * half, 3 * CR), :].rearrange("(t r) d -> r t d", r=CR)
                    sp.dma_start(dst, out[:, 3 * half:3 * half + 3]).then_inc(stored[half], 16)

            for n in range(2):
                load_rows(n, n)
            with sp.Fori(0, E // 2 - 1) as i:
                for n in range(2):
                    period(2 * i + n, n, True, True)
            period(E - 2, 0, True, False)
            period(E - 1, 1, False, False)
            for half in range(2):
                sp.wait_ge(stored[half], 16 * E + 16)

        @block.tensor
        def _(pe):
            nc.tensor.sem_inc(xT_ready, 4)
            nc.tensor.sem_inc(hid_ready, 2)
            nc.tensor.sem_inc(out_ready, 2)

            def turn(i, n, b):
                m, e = b // 2, 2 * i + n
                if b == 0:
                    pe.wait_ge(r_in[n], 16 * i + 16)
                pe.wait_ge(xT_ready, 8 * e + 2 * b + 2)
                for j in range(3):
                    t = 3 * (b % 2) + j
                    last = nc.tensor.transpose(ps[:, b % 2, j * CR:j * CR + CR], rows[:, n, t, m * P:m * P + P],
                                               k.ident[0:CR, 0:CR])
                last.then_inc(turned, 1)

            def step(new, old):
                if not old:
                    for b in range(4):
                        turn(*new, b)
                    return
                n, e = old[1], 2 * old[0] + old[1]
                pe.wait_ge(w1_low, e + 1)
                pe.wait_ge(xT_ready, 8 * e + 12)
                for r in range(NH):
                    f, sl = group(r)
                    pe.wait_ge(hid_ready, NH * e + r + 1)
                    for q in range(DM):
                        cols = slice(f * P, f * P + P)
                        last = split_products(nc, ps[:, 2 + r % 2, 0:HC], (w1h[:, q, cols], w1l[:, q, cols]),
                                              (xTh[:, n, q, sl], xTl[:, n, q, sl]), q == 0, q == DM - 1)
                    last.then_inc(h_ready, 1)
                    if new and r in TURNS:
                        turn(*new, TURNS[r])
                pe.wait_ge(w2_low, e + 1)
                for t in range(CT):
                    if t % 3 == 0:
                        for low in low_ready:
                            pe.wait_ge(low, FM * e + FM // 2 * (t // 3 + 1) + 2)
                    pe.wait_ge(out_ready, CT * e + t + 1)
                    for f in range(FM):
                        sl = slice(t * CR, t * CR + CR)
                        last = split_products(nc, ps[0:CR, 4 + t % 2, 0:D], (hidh[:, f, sl], hidl[:, f, sl]),
                                              (w2h[:, f, :], w2l[:, f, :]), f == 0, f == FM - 1)
                    last.then_inc(y_ready, 1)

            overlapped(pe, E, 2, step)

        @block.scalar
        def _(act):
            nc.scalar.sem_inc(y_ready, CT)
            for low in low_ready:
                nc.scalar.sem_inc(low, 2)
            nc.scalar.sem_inc(w2_in, 16)

            def step(new, old):
                if not old:
                    return
                e = 2 * old[0] + old[1]
                for r in range(NH):
                    f, cols = group(r)
                    if f == 0:
                        act.wait_ge(y_ready, CT * e + 3 * (r // FM) + 3)
                    act.wait_ge(low_ready[r % 2], FM * e + r // 2 + 1)
                    act.wait_ge(h_ready, NH * e + r + 1)
                    nc.scalar.activation(hid[:, r % RING, :], ps[:, 2 + r % 2, 0:HC], ACT.Silu)
                    nc.scalar.activation(hidh[:, f, cols], ps[:, 2 + r % 2, 0:HC], ACT.Silu).then_inc(hid_ready, 1)
                    if r == 2:
                        act.wait_ge(y_ready, CT * e + CT)
                        act.wait_ge(w2_in, 16 * e + 16)
                        nc.scalar.activation(w2h[:], w2[:], ACT.Copy).then_inc(w2_high, 1)
                if new:
                    act.wait_ge(h_ready, NH * e + NH)
                    act.wait_ge(w1_in, 16 * e + 16)
                    nc.scalar.activation(w1h[:], w1[:], ACT.Copy).then_inc(w1_high, 1)

            overlapped(act, E, 2, step)

        @block.vector
        def _(dve):
            for n in range(2):
                nc.vector.sem_inc(stored[n], 16)

            def turned_rows(i, n, b):
                e, m = 2 * i + n, b // 2
                cols = slice((b % 2) * HC, (b % 2) * HC + HC)
                dve.wait_ge(turned, 4 * e + b + 1)
                nc.vector.tensor_copy(xTh[:, n, m, cols], ps[:, b % 2, 0:HC]).then_inc(xT_ready, 1)
                dve.wait_ge(xT_ready, 8 * e + 2 * b + 5)
                nc.vector.tensor_tensor(xTl[:, n, m, cols], ps[:, b % 2, 0:HC], xTh[:, n, m, cols].bitcast(F32),
                                        ALU.subtract).then_inc(xT_ready, 1)

            def step(new, old):
                if not old:
                    for b in range(4):
                        turned_rows(*new, b)
                    return
                e = 2 * old[0] + old[1]
                for r in range(NH):
                    if r % 2 == 1:
                        hidden_low(dve, nc.vector, e, r)
                    if new and r in TURNS:
                        turned_rows(*new, TURNS[r])
                    if r == 3:
                        dve.wait_ge(w2_high, e + 1)
                        nc.vector.tensor_tensor(w2l[:], w2[:], w2h[:].bitcast(F32), ALU.subtract).then_inc(w2_low, 1)
                for t in range(CT):
                    if t % 3 == 0:
                        dve.wait_ge(stored[t // 3], 16 * e + 16)
                    dve.wait_ge(y_ready, CT * e + CT + t + 1)
                    nc.vector.tensor_copy(out[:, t, :], ps[0:CR, 4 + t % 2, 0:D]).then_inc(out_ready, 1)

            overlapped(dve, E, 2, step)

        @block.gpsimd
        def _(pool):
            nc.gpsimd.sem_inc(w1_low, 1)

            def step(new, old):
                if not old:
                    return
                e = 2 * old[0] + old[1]
                for r in range(0, NH, 2):
                    hidden_low(pool, nc.gpsimd, e, r)
                if new:
                    pool.wait_ge(w1_high, e + 1)
                    nc.gpsimd.tensor_tensor(w1l[:], w1[:], w1h[:].bitcast(F32), ALU.subtract).then_inc(w1_low, 1)

            overlapped(pool, E, 2, step)


def combine(k):
    nc = k.nc
    with stage(k) as c:
        idx = k.sb(c, "s11_index", [P, 2, 2], I32)
        g = k.sb(c, "s11_rows", [P, 2, 2, D])
        y = k.sb(c, "s11_y", [P, 2, D])
        idx_ready, mixed, done = k.sem("s11_index"), k.sem("s11_mixed"), k.sem("s11_done")
        got = [k.sem(f"s11_got{n}") for n in range(2)]
        stored = [k.sem(f"s11_stored{n}") for n in range(2)]
        block = c.enter_context(nc.Block())

        @block.gpsimd
        def _(pool):
            nc.gpsimd.sem_inc(done, 2)
            with pool.Fori(0, NT // 2) as i:
                for n in range(2):
                    t = 2 * i + n
                    pool.wait_ge(done, t + 1)
                    nc.gpsimd.tensor_copy(idx[:, n, :], k.source[:, ds(t, 1), :]).then_inc(idx_ready, 1)
                    pool.wait_ge(idx_ready, t + 1)
                    k.passed(nc.gpsimd)
                    for j in range(2):
                        nc.gpsimd.indirect_dma_start(
                            g[:, n, j, :], None, k.outs_dram,
                            bass.IndirectOffsetOnAxis(ap=idx[:, n, j:j + 1], axis=0)).then_inc(got[n], 16)

        @block.vector
        def _(dve):
            for n in range(2):
                nc.vector.sem_inc(stored[n], 16)
            with dve.Fori(0, NT // 2) as i:
                for n in range(2):
                    t = 2 * i + n
                    dve.wait_ge(got[n], 32 * i + 32)
                    dve.wait_ge(stored[n], 16 * i + 16)
                    nc.vector.scalar_tensor_tensor(y[:, n, :], g[:, n, 0, :], k.prob[:, 0, ds(t, 1)], k.H[:, ds(t, 1), :],
                                                   ALU.mult, ALU.add).then_inc(mixed, 1)
                    dve.wait_ge(mixed, t + 1)
                    nc.vector.scalar_tensor_tensor(y[:, n, :], g[:, n, 1, :], k.prob[:, 1, ds(t, 1)], y[:, n, :],
                                                   ALU.mult, ALU.add).then_inc(done, 1)

        @block.sync
        def _(sp):
            out = k.out.rearrange("(t p) d -> p t d", p=P)
            with sp.Fori(0, NT // 2) as i:
                for n in range(2):
                    t = 2 * i + n
                    sp.wait_ge(done, t + 3)
                    sp.dma_start(out[:, ds(t, 1), :], y[:, n, :]).then_inc(stored[n], 16)
            for n in range(2):
                sp.wait_ge(stored[n], 16 * (NT // 2) + 16)


WEIGHTS = {"in_W": (DM, 2 * D), "dt_W": (DM, D), "b_W": (DM, D), "c_W": (DM, D), "out_W": (DM, D),
           "f1_W": (DM, F1), "f2_W": (F1 // P, D), "Wq": (DM, D), "Wk": (DM, D), "Wv": (DM, D), "Wo": (DM, D),
           "router": (DM, E)}


LATE = ("Wq", "Wk", "Wv", "Wo", "router")


def program(nc, dram, out):
    with ExitStack() as ctx:
        k = Core(nc, dram, ctx)
        k.out = out
        k.H = k.sb(ctx, "H", [P, NT, D])
        k.X = k.sb(ctx, "X", [P, NT, D])
        k.vecs = k.sb(ctx, "vecs_sb", [P, NV])
        k.rows = k.sb(ctx, "rows_sb", [P, len(ROWS), D])
        k.ident = k.sb(ctx, "ident_sb", [P, P])
        k.identb = k.sb(ctx, "ident_bf16", [P, P], BF16)
        k.triu = k.sb(ctx, "triu_sb", [P, P])
        k.half_gate_b = k.sb(ctx, "half_gate_b", [P, DM])
        k.quarter_bq = k.sb(ctx, "quarter_bq", [P, DM])
        k.slots_dram = nc.dram_tensor("expert_rows", (SLOTS + 2 * NP, D), F32, kind="Internal").ap()
        k.outs_dram = nc.dram_tensor("expert_outputs", (SLOTS, D), F32, kind="Internal").ap()
        k.zero_filled, k.fills = k.sem("zero_filled"), E
        k.v_dram = nc.dram_tensor("values", (NP, D), F32, kind="Internal").ap()
        k.mhalf = k.sb(ctx, "minus_half", [P, 2 * TC])
        k.wmean = k.sb(ctx, "mean_abs_w", [P, 3])
        k.weights = {n: k.sb(ctx, n + "_sb", [P, *WEIGHTS[n]]) for n in LATE}
        early = ctx.enter_context(ExitStack())
        k.weights |= {n: k.sb(early, n + "_sb", [P, *s]) for n, s in WEIGHTS.items() if n not in LATE}
        k.wq = {n: k.sb(early, n + "_ternary", [P, *s], BF16)
                for n, s in (("w_gate", (DM, INNER)), ("w_up", (DM, INNER)), ("w_down", (FM, D)))}
        k.const_in, k.weights_in = k.sem("const_in"), k.sem("weights_in")
        k.waits_passed = k.sem("waits_passed")
        k.row = lambda name: k.rows[:, ROWS.index(name), :]
        k.tile_out = lambda ps, j: ps[:, j // 2, (j % 2) * D:(j % 2) * D + D]
        ps = ctx.enter_context(nc.psum_tensor("ps", [P, 8, 512], F32))
        embed(k, ps)
        with ExitStack() as c:
            nxT = k.sb(c, "nxT", [P, DM, NP])
            yT = k.sb(c, "yT", [P, DM, NP])
            scan_norms(k, ps, nxT)
            with nc.Block() as block:
                @block.tensor
                def _(pe):
                    pe.wait_ge(k.weights_in, 16 * len(WEIGHTS))

                @block.gpsimd
                def _(pool):
                    nc.gpsimd.memset(yT[:, :, N:NP], 0.0)
            selective_scan(k, ps, nxT, yT)
            scan_output(k, ps, yT)
        with ExitStack() as c:
            xqT = k.sb(c, "xqT", [P, DM, NP], BF16)
            dq = k.sb(c, "row_scale", [P, NT])
            quant_rows(k, ps, xqT, dq)
            ternary_ffn(k, ps, xqT, dq)
        with ExitStack() as c:
            early.close()
            fT = k.sb(c, "fT", [P, DM, NP])
            with ExitStack() as c2:
                qT = k.sb(c2, "qT", [P, DM, NP])
                kT = k.sb(c2, "kT", [P, DM, NP])
                with nc.Block() as block:
                    @block.gpsimd
                    def _(pool):
                        nc.gpsimd.memset(fT[:, :, N:NP], 0.0)

                    @block.vector
                    def _(dve):
                        at = VEC["bq"][0]
                        nc.vector.tensor_scalar(k.quarter_bq[:], k.vecs[:, at:at + 2], 0.25, None, ALU.mult)
                attention_inputs(k, ps, qT, kT)
                attention(k, ps, qT, kT, fT)
            attention_output(k, ps, fT)
        with ExitStack() as c:
            k.prob = k.sb(c, "pair_weights", [P, 2, NT])
            k.source = k.sb(c, "pair_rows", [P, NT, 2], I32)
            with ExitStack() as c2:
                k.w1, k.w2 = k.sb(c2, "expert_w1", [P, DM, INNER]), k.sb(c2, "expert_w2", [P, FM, D])
                k.w1_high, k.w1_low = (k.sb(c2, f"expert_w1_{n}", [P, DM, INNER], F32R) for n in ("high", "low"))
                route(k, ps)
                experts(k, ps)
            combine(k)


def columns(v):
    import numpy as np
    return np.ascontiguousarray(v.reshape(-1, P).T)


def folded(w):
    import numpy as np
    return np.ascontiguousarray(w.reshape(-1, P, w.shape[1]).transpose(1, 0, 2))


def layout(a):
    import numpy as np
    g = {}
    x = a["x"].reshape(B, 3, 8, 16, 8, 16).transpose(1, 3, 5, 0, 2, 4).reshape(768, B * IMG)
    g["patches"] = folded(x)
    g["tok_W1"], g["tok_W2"] = folded(a["L0_tok_W1"]), folded(a["L0_tok_W2"])
    g["tok_b2"] = a["L0_tok_b2"].reshape(1, D)
    ids = np.zeros((NP,), np.int32)
    ids[:N].reshape(B, L)[:, IMG:] = a["x_txt"]
    g["tokens"] = np.ascontiguousarray(ids.reshape(NT, P).T)
    g["table"] = a["L0_txt_weight"]
    is_text = np.zeros((NP,), np.float32)
    is_text[:N].reshape(B, L)[:, IMG:] = 1.0
    is_image = np.zeros((NP,), np.float32)
    is_image[:N].reshape(B, L)[:, :IMG] = 1.0
    g["tmask"] = np.ascontiguousarray(is_text.reshape(NT, P).T)
    g["imask"] = is_image.reshape(1, NP)
    g["ident"] = np.eye(P, dtype=np.float32)
    g["triu"] = np.triu(np.ones((P, P), np.float32), 1)
    h = np.arange(P) // DH
    g["head_rows"] = (np.arange(HG)[:, None] == h[None, :]).astype(np.float32)
    same = (h[:, None] == h[None, :]).astype(np.float32)
    g["head_sum"] = np.stack([same, same * (np.arange(P) % DH >= DUP)[:, None].astype(np.float32)], 1)
    g["iota"] = np.ascontiguousarray(np.broadcast_to(np.arange(E, dtype=np.float32), (P, E)))
    token = np.arange(NP, dtype=np.float32).reshape(NT, P).T
    g["pair"] = np.ascontiguousarray(np.stack([TRASH + 2 * token, TRASH + 2 * token + 1], 2))
    g["valid"] = (token < N).astype(np.float32)
    g["w1"] = np.ascontiguousarray(a["L1_ffn_w1"].reshape(E, DM, P, INNER).transpose(2, 0, 1, 3))
    g["w2"] = np.ascontiguousarray(a["L1_ffn_w2"].reshape(E, FM, P, D).transpose(2, 0, 1, 3))
    s = "L0_attn_"
    vec = {"in_b": a[s + "in_b"], "dw0": a[s + "dw_W"][:, 0, 0], "dw1": a[s + "dw_W"][:, 0, 1],
           "dw2": a[s + "dw_W"][:, 0, 2], "tb1": a["L0_tok_b1"], "bq": a["L1_attn_bq"], "bk": a["L1_attn_bk"],
           "beta": np.repeat(a["L1_attn_beta"], DH), "t": np.repeat(a["L1_attn_t"], DH)}
    for n in ("dw_b", "dt_b", "b_b", "c_b", "a_log", "d_skip", "ln1_g", "ln1_b", "ln2_g", "ln2_b", "f1_b"):
        vec[n] = a[s + n]
    g["vecs"] = np.concatenate([columns(vec[n]) for n in VEC], 1)
    row = {"out_b": a[s + "out_b"], "f2_b": a[s + "f2_b"], "bv": a["L1_attn_bv"], "bo": a["L1_attn_bo"],
           "ln_w": a["L1_attn_ln_w"], "ln_b": a["L1_attn_ln_b"]}
    g["rows"] = np.ascontiguousarray(np.broadcast_to(np.stack([row[n] for n in ROWS]), (P, len(ROWS), D)))
    for n in ("in_W", "dt_W", "b_W", "c_W", "out_W", "f1_W", "f2_W"):
        g[n] = folded(a[s + n])
    for n in ("Wq", "Wk", "Wv", "Wo"):
        g[n] = folded(a["L1_attn_" + n].T)
    for n in FFN_WEIGHTS:
        g[n] = folded(a["L0_ffn_" + n].T)
    g["router"] = folded(a["L1_ffn_router_w"].T)
    return g


def kernel(**inputs):
    import numpy as np
    import concourse.bacc as bacc
    from concourse.bass_utils import run_bass_kernel_spmd as run

    nc = bacc.Bacc("TRN2", target_bir_lowering=False, num_devices=1)
    arrays, dram = {}, {}
    for name, a in layout({n: np.asarray(v) for n, v in inputs.items()}).items():
        a = np.ascontiguousarray(a)
        arrays[f"in_{name}_dram"] = a
        dram[name] = nc.dram_tensor(f"in_{name}_dram", a.shape, mybir.dt.from_np(a.dtype), kind="ExternalInput").ap()
    out = nc.dram_tensor("out_0_dram", (NP, D), F32, kind="ExternalOutput").ap()
    program(nc, dram, out)
    r = run(nc, [arrays], core_ids=[0])
    return r.results[0]["out_0_dram"][:N].reshape(B, L, D)
```

```python
from contextlib import ExitStack, contextmanager

import concourse.bass as bass
from concourse import mybir
from concourse.bass import ds

F32 = mybir.dt.float32
F32R = mybir.dt.float32r
BF16 = mybir.dt.bfloat16
I32 = mybir.dt.int32
U32 = mybir.dt.uint32
ALU = mybir.AluOpType
ACT = mybir.ActivationFunctionType
AX = mybir.AxisListType

P = 128
B, IMG, TXT = 16, 64, 77
L = IMG + TXT
N = B * L
NT = -(-N // P)
NP = NT * P
D = 256
DM = D // P
TC = 3
NCH = NT // TC
CW = TC * P
KP = 768 // P
BPI = 2
SW = BPI * L
F1 = 512
INNER = 1024
FM = INNER // P
HEADS, DH = 16, 16
HG = 8
NKC = -(-L // DH)
LAST0 = L - DH
DUP = (NKC - 1) * DH - LAST0
KB = 3
E = 8
CAP = int(1.25 * N * 2 / E) + 1
CT = 6
CR = -(-CAP // CT)
CAPP = CT * CR
SLOTS = E * CAPP
TRASH = SLOTS
EPS = 1e-5
MAGIC = 12582912.0

VEC = {}
for _name, _n in (("in_b", 4), ("dw0", 2), ("dw1", 2), ("dw2", 2), ("dw_b", 2), ("dt_b", 2), ("b_b", 2),
                  ("c_b", 2), ("a_log", 2), ("d_skip", 2), ("ln1_g", 2), ("ln1_b", 2), ("ln2_g", 2),
                  ("ln2_b", 2), ("f1_b", 4), ("tb1", 2), ("bq", 2), ("bk", 2), ("beta", 2), ("t", 2)):
    VEC[_name] = (sum(n for _, n in VEC.values()), _n)
NV = sum(n for _, n in VEC.values())
ROWS = ("out_b", "f2_b", "bv", "bo", "ln_w", "ln_b")


FFN_WEIGHTS = ("w_gate", "w_up", "w_down")


def pipelined(eng, n, u, front, back):
    front(0, 0)
    with eng.Fori(0, n // u - 1) as i:
        for p in range(u):
            front(i + (p + 1) // u, (p + 1) % u)
            back(i, p)
    for p in range(u):
        if p + 1 < u:
            front(n // u - 1, p + 1)
        back(n // u - 1, p)


def overlapped(eng, n, u, step):
    step((0, 0), None)
    with eng.Fori(0, n // u - 1) as i:
        for p in range(u):
            step((i + (p + 1) // u, (p + 1) % u), (i, p))
    for p in range(u):
        step((n // u - 1, p + 1) if p + 1 < u else None, (n // u - 1, p))


def overlapped_twice(eng, n, step):
    step((0, 0), None, None)
    step((0, 1), (0, 0), None)
    with eng.Fori(0, n // 2 - 1) as i:
        for p in range(2):
            step((i + 1, p), (i + p, 1 - p), (i, p))
    step(None, (n // 2 - 1, 1), (n // 2 - 1, 0))
    step(None, None, (n // 2 - 1, 1))


class Steps:

    def __init__(self, eng, sem, i=0, per=0):
        self.eng, self.sem, self.base, self.per, self.n = eng, sem, i * per, per, 0

    def __call__(self, ins):
        ins.then_inc(self.sem, 1)
        self.n += 1

    def wait(self):
        self.eng.wait_ge(self.sem, self.base + self.n)

    def end(self):
        assert self.n == self.per, (self.n, self.per)


class Core:

    def __init__(self, nc, dram, ctx):
        self.nc, self.dram, self.sems = nc, dram, []

    def sb(self, ctx, name, shape, dt=F32):
        return ctx.enter_context(self.nc.sbuf_tensor(name, shape, dt))

    def sem(self, name):
        self.sems.append(self.nc.alloc_semaphore(name=name))
        return self.sems[-1]

    def passed(self, eng):
        eng.sem_inc(self.waits_passed, 1)

    def vec(self, name, m):
        at, n = VEC[name]
        assert m < n
        return self.vecs[:, at + m:at + m + 1]


@contextmanager
def stage(k):
    k.sems = []
    with ExitStack() as c:
        yield c
    k.nc.clear_and_free_semaphores(k.sems)
    k.nc.all_engine_barrier()


def embed(k, ps):
    nc, dram = k.nc, k.dram
    with stage(k) as c:
        patches = k.sb(c, "patches", [P, KP, B * IMG])
        w1 = k.sb(c, "tok_w1", [P, KP, D])
        w2 = k.sb(c, "tok_w2", [P, DM, D])
        b2 = k.sb(c, "tok_b2", [1, D])
        imask = k.sb(c, "image_mask", [1, NP])
        tmask = k.sb(c, "text_mask", [P, NT])
        tok = k.sb(c, "token_ids", [P, NT], I32)
        h1 = k.sb(c, "h1", [P, DM, NP])
        rows = k.sb(c, "text_rows", [P, NT, D])
        vecs_in, small_in = k.sem("vecs_in"), k.sem("tok_small_in")
        patches_in = [k.sem(f"patches_in{n}") for n in range(2)]
        tok_in, gathered = k.sem("tok_in"), [k.sem(f"gathered{n}") for n in range(NCH)]
        cleared, hid, hid_out = k.sem("h1_cleared"), k.sem("hid_ready"), k.sem("hid_activated")
        emb, emb_out, half = k.sem("emb_ready"), k.sem("emb_out"), k.sem("half_bias")
        wf = {n: k.sb(c, n + "_f32", [P, DM * INNER]) for n in FFN_WEIGHTS}
        junk = k.sb(c, "abs_weights", [P, DM * INNER])
        asum = k.sb(c, "abs_sums", [P, 3])
        ones = k.sb(c, "ones", [P, P])
        wrec = k.sb(c, "inv_mean_abs", [P, 3])
        ffn_in = [k.sem(n + "_in") for n in FFN_WEIGHTS]
        zeros = k.sb(c, "zeros", [CR, CT, D])
        zeroed, inv_mean, scaled = k.sem("zeros_ready"), k.sem("inv_mean_ready"), k.sem("weights_scaled")
        st, stats = k.sb(c, "s1_stats", [P, NT, 6]), k.sem("s1_stats")
        summed, total, wq_steps = k.sem("abs_summed"), k.sem("abs_total"), k.sem("wq_steps")
        block = c.enter_context(nc.Block())

        @block.sync
        def _(sp):
            sp.dma_start(k.vecs[:], dram["vecs"]).then_inc(vecs_in, 16)
            sp.dma_start(w1[:], dram["tok_W1"]).then_inc(patches_in[0], 16)
            for n in range(2):
                sp.dma_start(patches[:, :, 512 * n:512 * n + 512],
                             dram["patches"][:, :, 512 * n:512 * n + 512]).then_inc(patches_in[n], 16)
            sp.dma_start(w2[:], dram["tok_W2"]).then_inc(small_in, 16)
            sp.dma_start(b2[:], dram["tok_b2"]).then_inc(small_in, 16)
            sp.dma_start(imask[:], dram["imask"]).then_inc(small_in, 16)
            sp.dma_start(tmask[:], dram["tmask"]).then_inc(small_in, 16)
            sp.dma_start(k.ident[:], dram["ident"]).then_inc(k.const_in, 16)
            sp.dma_start(k.triu[:], dram["triu"]).then_inc(k.const_in, 16)
            sp.dma_start(k.rows[:], dram["rows"]).then_inc(k.const_in, 16)
            for n, name in enumerate(FFN_WEIGHTS):
                sp.dma_start(wf[name][:], dram[name].rearrange("p a b -> p (a b)")).then_inc(ffn_in[n], 16)
            for name in WEIGHTS:
                sp.dma_start(k.weights[name][:], dram[name]).then_inc(k.weights_in, 16)
            sp.wait_ge(zeroed, 1)
            for e in range(E):
                sp.dma_start(k.slots_dram[CAPP * e:CAPP * e + CAPP, :].rearrange("(t r) d -> r t d", r=CR),
                             zeros[:]).then_inc(k.zero_filled, 16)

        @block.gpsimd
        def _(pool):
            pool.dma_start(tok[:], dram["tokens"]).then_inc(tok_in, 16)
            nc.gpsimd.memset(h1[:], 0.0).then_inc(cleared, 1)
            nc.gpsimd.memset(zeros[:], 0.0).then_inc(zeroed, 1)
            pool.wait_ge(tok_in, 16)
            for t in range(NT):
                nc.gpsimd.indirect_dma_start(
                    rows[:, t, :], None, dram["table"],
                    bass.IndirectOffsetOnAxis(ap=tok[:, t:t + 1], axis=0)).then_inc(gathered[t // TC], 16)

        @block.tensor
        def _(pe):
            for n in range(2):
                pe.wait_ge(patches_in[n], 16 * (2 - n))
                for m in range(DM):
                    for q in range(KP):
                        last = nc.tensor.matmul(ps[:, 2 * n + m, :], w1[:, q, m * P:m * P + P],
                                                patches[:, q, 512 * n:512 * n + 512],
                                                start=(q == 0), stop=(q == KP - 1))
                    last.then_inc(hid, 1)
            pe.wait_ge(hid_out, 2 * DM)
            pe.wait_ge(small_in, 64)
            for t in range(NT):
                if t == 8:
                    pe.wait_ge(half, 4)
                    pe.wait_ge(summed, 3)
                    nc.tensor.matmul(ps[:, 0, 0:3], ones[:], asum[:], start=True, stop=True).then_inc(total, 1)
                if t >= 4:
                    pe.wait_ge(emb_out, t - 3)
                out = ps[:, 4 + t % 4, 0:D]
                for m in range(DM):
                    nc.tensor.matmul(out, h1[:, m, t * P:t * P + P], w2[:, m, :], start=(m == 0), stop=False)
                nc.tensor.matmul(out, imask[:, t * P:t * P + P], b2[:], start=False, stop=True).then_inc(emb, 1)

        @block.scalar
        def _(act):
            act.wait_ge(vecs_in, 16)
            act.wait_ge(cleared, 1)
            for n in range(2):
                for m in range(DM):
                    act.wait_ge(hid, 2 * n + m + 1)
                    dst = h1[:, m, 0:N].rearrange("p (b l) -> p b l", b=B)[:, 8 * n:8 * n + 8, 0:IMG]
                    nc.scalar.activation(dst, ps[:, 2 * n + m, :].rearrange("p (b l) -> p b l", b=8),
                                         ACT.Silu, bias=k.vec("tb1", m)).then_inc(hid_out, 1)
            for n, name in enumerate(FFN_WEIGHTS):
                act.wait_ge(ffn_in[n], 16)
                if n:
                    act.wait_ge(summed, n)
                nc.scalar.activation(junk[:], wf[name][:], ACT.Abs, accum_out=asum[:, n:n + 1]).then_inc(summed, 1)
            act.wait_ge(inv_mean, 1)
            for n, name in enumerate(FFN_WEIGHTS):
                nc.scalar.activation(wf[name][:], wf[name][:], ACT.Copy, scale=wrec[:, n:n + 1]).then_inc(scaled, 1)

        @block.vector
        def _(dve):
            dve.wait_ge(vecs_in, 16)
            at = VEC["in_b"][0]
            nc.vector.tensor_scalar(k.half_gate_b[:], k.vecs[:, at + 2:at + 4], 0.5, None, ALU.mult).then_inc(half, 1)
            dve.wait_ge(k.const_in, 48)
            nc.vector.tensor_copy(k.identb[:], k.ident[:]).then_inc(half, 1)
            nc.vector.memset(k.mhalf[:], -0.5).then_inc(half, 1)
            nc.vector.memset(ones[:], 1.0).then_inc(half, 1)
            dve.wait_ge(small_in, 64)
            s, st_steps = Steps(dve, wq_steps), Steps(dve, stats)
            for t in range(NT):
                dve.wait_ge(gathered[t // TC], 16 * TC)
                dve.wait_ge(emb, t + 1)
                nc.vector.scalar_tensor_tensor(k.H[:, t, :], rows[:, t, :], tmask[:, t:t + 1], ps[:, 4 + t % 4, 0:D],
                                               ALU.mult, ALU.add).then_inc(emb_out, 1)
                if t % TC == TC - 1:
                    dve.wait_ge(emb_out, t + 1)
                    for j in range(t + 1 - TC, t + 1):
                        st_steps(nc.vector.bn_stats(st[:, j, :], k.H[:, j, :]))
                    st_steps.wait()
                    for j in range(t + 1 - TC, t + 1):
                        nc.vector.bn_aggr(k.meanvar[:, j, :], st[:, j, :])
                if t == 8:
                    dve.wait_ge(total, 1)
                    s(nc.vector.tensor_scalar(k.wmean[:], ps[:, 0, 0:3], 1.0 / (D * INNER), 1e-5, ALU.mult, ALU.max))
                    s.wait()
                    s(nc.vector.reciprocal(wrec[:], k.wmean[:]))
                    s.wait()
                    nc.vector.sem_inc(inv_mean, 1)
                if t in (11, 13, 15):
                    n = (t - 11) // 2
                    name = FFN_WEIGHTS[n]
                    dve.wait_ge(scaled, n + 1)
                    s(nc.vector.tensor_scalar(wf[name][:], wf[name][:], 1.0, -1.0, ALU.min, ALU.max))
                    s.wait()
                    nc.vector.tensor_scalar(k.wq[name][:].rearrange("p a b -> p (a b)"), wf[name][:], MAGIC, MAGIC,
                                            ALU.add, ALU.subtract)


def scan_norms(k, ps, nxT):
    nc = k.nc
    with stage(k) as c:
        ve = k.sb(c, "s2_var_eps", [P, 2, NT])
        rs = k.sb(c, "s2_rstd", [P, 2, NT])
        nx = k.sb(c, "s2_nx", [P, 2, TC, D])
        var, rstd = k.sem("s2_var"), k.sem("s2_rstd_ready")
        normed, turned, stored = k.sem("s2_normed"), k.sem("s2_turned"), k.sem("s2_stored")
        block = c.enter_context(nc.Block())

        @block.vector
        def _(dve):
            nc.vector.sem_inc(turned, 2)
            nc.vector.tensor_scalar(ve[:, 0, :], k.meanvar[:, :, 1], EPS, None, ALU.add).then_inc(var, 1)
            nc.vector.tensor_scalar(ve[:, 1, :], k.meanvar[:, :, 1], 1.0 + EPS, EPS * EPS, ALU.mult, ALU.add).then_inc(var, 1)
            dve.wait_ge(rstd, 1)
            with dve.Fori(0, NCH // 2) as i:
                for p in range(2):
                    dve.wait_ge(turned, 2 * i + p + 1)
                    for n in (1, 0):
                        for j in range(TC):
                            t = 2 * TC * i + TC * p + j
                            out = nx[:, p, j, :] if n else k.X[:, ds(t, 1), :]
                            last = nc.vector.tensor_scalar(out, k.H[:, ds(t, 1), :], k.meanvar[:, ds(t, 1), 0],
                                                           rs[:, n, ds(t, 1)], ALU.subtract, ALU.mult)
                            if n:
                                last.then_inc(normed, 1)

        @block.gpsimd
        def _(pool):
            pool.wait_ge(var, 2)
            nc.gpsimd.tensor_tensor(rs[:], ve[:], k.mhalf[:].rearrange("p (a b) -> p a b", a=2), ALU.pow).then_inc(rstd, 1)

        @block.tensor
        def _(pe):
            nc.tensor.sem_inc(stored, 2 * DM)
            with pe.Fori(0, NCH // 2) as i:
                for p in range(2):
                    u = 2 * i + p
                    pe.wait_ge(stored, DM * u + DM)
                    for j in range(TC):
                        pe.wait_ge(normed, TC * u + j + 1)
                        for m in range(DM):
                            last = nc.tensor.transpose(ps[:, 2 * p + m, j * P:j * P + P], nx[:, p, j, m * P:m * P + P],
                                                       k.ident[:])
                    last.then_inc(turned, 1)

        @block.scalar
        def _(act):
            with act.Fori(0, NCH // 2) as i:
                for p in range(2):
                    u = 2 * i + p
                    act.wait_ge(turned, u + 3)
                    for m in range(DM):
                        nc.scalar.activation(nxT[:, m, ds(CW * u, CW)], ps[:, 2 * p + m, 0:CW], ACT.Identity,
                                             bias=k.vec("ln1_b", m), scale=k.vec("ln1_g", m)).then_inc(stored, 1)


def selective_scan(k, ps, nxT, yT):
    nc = k.nc
    NS = N // SW
    W = k.weights
    with stage(k) as c:
        xp = k.sb(c, "s3_conv_in", [P, 2, DM, BPI, L + 2])
        mixed = k.sb(c, "s3_mixed", [P, 2, DM, SW])
        gate = k.sb(c, "s3_gate", [P, 2, DM, SW])
        az = k.sb(c, "s3_soft", [P, DM, SW])
        z = k.sb(c, "s3_z", [P, DM, SW])
        relu = k.sb(c, "s3_relu", [P, DM, SW])
        dt = k.sb(c, "s3_dt", [P, DM, SW])
        bt = k.sb(c, "s3_bt", [P, 2, DM, SW])
        ct = k.sb(c, "s3_ct", [P, 2, DM, SW])
        decay = k.sb(c, "s3_decay", [P, 2, DM, SW])
        state = k.sb(c, "s3_state", [P, DM, SW])
        nega = k.sb(c, "s3_neg_a", [P, DM])
        a0 = k.sb(c, "s3_exp_a", [P, DM])
        names = ("padded", "nega", "a0", "proj", "xp", "gate", "mix_steps", "mixed", "bcd", "z", "relu", "soft", "dt",
                 "decay", "bt", "ct", "asteps", "dsteps", "scanned")
        (padded, nega_ready, a0_ready, proj, xp_ready, gate_ready, mix_steps, mixed_ready, bcd, z_ready, relu_ready,
         soft_ready, dt_ready, decay_ready, bt_ready, ct_ready, asteps, dsteps, scanned) = (k.sem("s3_" + n) for n in names)
        block = c.enter_context(nc.Block())

        @block.gpsimd
        def _(pool):
            nc.gpsimd.memset(xp[:], 0.0).then_inc(padded, 1)

        @block.tensor
        def _(pe):
            def project(new, half, bank):
                i = 2 * new[0] + new[1]
                for m in range(DM):
                    col = (DM * half + m) * P
                    for q in range(DM):
                        last = nc.tensor.matmul(ps[:, bank + m, 0:SW], W["in_W"][:, q, col:col + P],
                                                nxT[:, q, ds(SW * i, SW)], start=(q == 0), stop=(q == DM - 1))
                    last.then_inc(proj, 1)

            def step(new, old):
                if new:
                    pe.wait_ge(xp_ready, DM * (2 * new[0] + new[1]) + DM)
                    project(new, 0, 2)
                if old:
                    i, p = 2 * old[0] + old[1], old[1]
                    pe.wait_ge(mixed_ready, DM * i + DM)
                    pe.wait_ge(ct_ready, DM * i + DM)
                    for w, bank in (("dt_W", 4), ("b_W", 6), ("c_W", 0)):
                        if w == "c_W":
                            pe.wait_ge(gate_ready, DM * i + DM)
                        for m in range(DM):
                            for q in range(DM):
                                last = nc.tensor.matmul(ps[:, bank + m, 0:SW], W[w][:, q, m * P:m * P + P],
                                                        mixed[:, p, q, :], start=(q == 0), stop=(q == DM - 1))
                            last.then_inc(bcd, 1)
                if new:
                    pe.wait_ge(ct_ready, DM * (2 * new[0] + new[1]) + DM)
                    project(new, 1, 0)

            overlapped(pe, NS, 2, step)

        @block.scalar
        def _(act):
            nc.scalar.sem_inc(ct_ready, DM)
            nc.scalar.sem_inc(xp_ready, DM)
            nc.scalar.activation(a0[:], k.vecs[:, VEC["a_log"][0]:VEC["a_log"][0] + DM], ACT.Exp).then_inc(a0_ready, 1)
            act.wait_ge(padded, 1)
            act.wait_ge(nega_ready, 1)

            def step(new, old):
                if new:
                    u = 2 * new[0] + new[1]
                    for m in range(DM):
                        act.wait_ge(proj, 4 * u + m + 1)
                        nc.scalar.activation(xp[:, new[1], m, :, 1:L + 1],
                                             ps[:, 2 + m, 0:SW].rearrange("p (b l) -> p b l", b=BPI),
                                             ACT.Identity, bias=k.vec("in_b", m)).then_inc(xp_ready, 1)
                if old:
                    i, p = 2 * old[0] + old[1], old[1]
                    s = Steps(act, asteps, i, 1 + DM)
                    for m in range(DM):
                        act.wait_ge(bcd, 6 * i + m + 1)
                        nc.scalar.activation(z[:, m, :], ps[:, 4 + m, 0:SW], ACT.Identity,
                                             bias=k.vec("dt_b", m)).then_inc(z_ready, 1)
                    act.wait_ge(scanned, i + 1)
                    for m in range(DM):
                        act.wait_ge(bcd, 6 * i + DM + m + 1)
                        nc.scalar.activation(bt[:, p, m, :], ps[:, 6 + m, 0:SW], ACT.Tanh,
                                             bias=k.vec("b_b", m)).then_inc(bt_ready, 1)
                    for m in range(DM):
                        act.wait_ge(bcd, 6 * i + 2 * DM + m + 1)
                        nc.scalar.activation(ct[:, p, m, :], ps[:, m, 0:SW], ACT.Tanh,
                                             bias=k.vec("c_b", m)).then_inc(ct_ready, 1)
                    act.wait_ge(z_ready, DM * i + DM)
                    s(nc.scalar.activation(az[:], z[:], ACT.Abs))
                    nc.scalar.preload_act_table_set("natural_log_exp_and_others")
                    s.wait()
                    for m in range(DM):
                        s(nc.scalar.activation(az[:, m, :], az[:, m, :], ACT.Exp, scale=-1.0))
                    s.wait()
                    nc.scalar.activation(az[:], az[:], ACT.Ln, bias=1.0).then_inc(soft_ready, 1)
                    s.end()
                if old:
                    for m in range(DM):
                        act.wait_ge(dt_ready, DM * i + m + 1)
                        nc.scalar.activation(decay[:, p, m, :], dt[:, m, :], ACT.Exp,
                                             scale=nega[:, m:m + 1]).then_inc(decay_ready, 1)
                if new:
                    for m in range(DM):
                        act.wait_ge(proj, 4 * u + DM + m + 1)
                        nc.scalar.activation(gate[:, new[1], m, :], ps[:, m, 0:SW], ACT.Tanh,
                                             bias=k.half_gate_b[:, m:m + 1], scale=0.5).then_inc(gate_ready, 1)

            overlapped(act, NS, 2, step)

        @block.vector
        def _(dve):
            nc.vector.sem_inc(scanned, 2)
            dve.wait_ge(a0_ready, 1)
            nc.vector.tensor_scalar(nega[:], a0[:], -1.0, None, ALU.mult).then_inc(nega_ready, 1)

            def softplus(i, p):
                i = 2 * i + p
                dve.wait_ge(z_ready, DM * i + DM)
                nc.vector.tensor_scalar(relu[:], z[:], 0.0, None, ALU.max).then_inc(relu_ready, 1)
                dve.wait_ge(relu_ready, i + 1)
                dve.wait_ge(soft_ready, i + 1)
                for m in range(DM):
                    nc.vector.tensor_tensor(dt[:, m, :], relu[:, m, :], az[:, m, :], ALU.add).then_inc(dt_ready, 1)

            def convolution(i, p):
                i = 2 * i + p
                mix = Steps(dve, mix_steps, i, 2 * DM)
                for tap in range(3):
                    for m in range(DM):
                        if tap == 0:
                            dve.wait_ge(xp_ready, DM * i + DM + m + 1)
                        x = xp[:, p, m, :, tap:tap + L]
                        out = mixed[:, p, m, :].rearrange("p (b l) -> p b l", b=BPI)
                        w = k.vec(f"dw{tap}", m)
                        if tap == 0:
                            mix(nc.vector.tensor_scalar(out, x, w, k.vec("dw_b", m), ALU.mult, ALU.add))
                        elif tap == 1:
                            mix(nc.vector.scalar_tensor_tensor(out, x, w, out, ALU.mult, ALU.add))
                        else:
                            nc.vector.scalar_tensor_tensor(out, x, w, out, ALU.mult, ALU.add).then_inc(mixed_ready, 1)
                    if tap < 2:
                        mix.wait()
                mix.end()

            def scan(i, p):
                i = 2 * i + p
                s = Steps(dve, dsteps, i, 5 + 2 * DM)
                dve.wait_ge(decay_ready, DM * i + DM)
                s(nc.vector.memset(decay[:, p].rearrange("p m (b l) -> p m b l", b=BPI)[:, :, :, 0:1], 0.0))
                s(nc.vector.tensor_tensor(dt[:], dt[:], mixed[:, p], ALU.mult))
                s.wait()
                dve.wait_ge(bt_ready, DM * i + DM)
                s(nc.vector.tensor_tensor(dt[:], dt[:], bt[:, p], ALU.mult))
                s.wait()
                for m in range(DM):
                    s(nc.vector.tensor_tensor_scan(state[:, m, :], decay[:, p, m, :], dt[:, m, :], 0.0, ALU.mult, ALU.add))
                s.wait()
                dve.wait_ge(ct_ready, DM * i + 2 * DM)
                s(nc.vector.tensor_tensor(state[:], state[:], ct[:, p], ALU.mult))
                s.wait()
                for m in range(DM):
                    s(nc.vector.scalar_tensor_tensor(state[:, m, :], mixed[:, p, m, :], k.vec("d_skip", m), state[:, m, :],
                                                     ALU.mult, ALU.add))
                s.wait()
                dve.wait_ge(gate_ready, DM * i + DM)
                s(nc.vector.scalar_tensor_tensor(yT[:, :, ds(SW * i, SW)], gate[:, p], 1.0, state[:], ALU.add, ALU.mult))
                s.wait()
                nc.vector.sem_inc(scanned, 1)
                s.end()

            def step(new, old):
                if new:
                    convolution(*new)
                if old:
                    softplus(*old)
                    scan(*old)

            overlapped(dve, NS, 2, step)


def scan_output(k, ps, yT):
    nc = k.nc
    W = k.weights
    with stage(k) as c:
        ys = k.sb(c, "s4_y", [P, DM, CW])
        xb = k.sb(c, "s4_xb", [P, TC, D])
        x2 = k.sb(c, "s4_x2", [P, 2, TC, D])
        hn = k.sb(c, "s4_hn", [P, TC, D])
        hx = k.sb(c, "s4_hx", [P, 2, TC, D])
        st = k.sb(c, "s4_stats", [P, TC, 6])
        mv = k.sb(c, "s4_meanvar", [P, TC, 2])
        ve = k.sb(c, "s4_var_eps", [P, TC])
        rs = k.sb(c, "s4_rstd", [P, TC])
        hT = k.sb(c, "s4_hT", [P, DM, CW])
        g = k.sb(c, "s4_gelu", [P, 4, CW])
        hst, hmv = k.sb(c, "s4_h_stats", [P, TC, 6]), k.sb(c, "s4_h_meanvar", [P, TC, 2])
        hsteps = k.sem("s4_hsteps")
        names = ("staged", "xb", "proj", "x2", "steps", "var", "rstd", "hn", "turned", "hT", "f1", "gelu", "hx1",
                 "hx", "f2", "done")
        (staged, xb_ready, proj, x2_ready, steps, var, rstd, hn_ready, turned, hT_ready, f1, gelu, hx1, hx_ready, f2,
         done) = (k.sem("s4_" + n) for n in names)
        block = c.enter_context(nc.Block())

        @block.gpsimd
        def _(pool):
            nc.gpsimd.sem_inc(done, 2 * TC)
            with pool.Fori(0, NCH // 2) as i:
                for p in range(2):
                    u = 2 * i + p
                    for j in range(TC):
                        nc.gpsimd.tensor_tensor(xb[:, j, :], k.X[:, ds(TC * u + j, 1), :], k.row("out_b"),
                                                ALU.add).then_inc(xb_ready, 1)
                    pool.wait_ge(var, u + 1)
                    nc.gpsimd.tensor_tensor(rs[:], ve[:], k.mhalf[:, 0:TC], ALU.pow).then_inc(rstd, 1)
                    pool.wait_ge(done, TC * u + TC)
                    for j in range(TC):
                        nc.gpsimd.tensor_tensor(hx[:, p, j, :], x2[:, p, j, :], k.row("f2_b"), ALU.add).then_inc(hx1, 1)
                    pool.wait_ge(hx1, TC * u + TC)
                    for j in range(TC):
                        nc.gpsimd.tensor_tensor(hx[:, p, j, :], hx[:, p, j, :], k.H[:, ds(TC * u + j, 1), :],
                                                ALU.add).then_inc(hx_ready, 1)

        @block.tensor
        def _(pe):
            def step(new, old):
                if old:
                    u = 2 * old[0] + old[1]
                    for j in range(TC):
                        pe.wait_ge(hn_ready, TC * u + j + 1)
                        for m in range(DM):
                            last = nc.tensor.transpose(ps[:, 2 + m, j * P:j * P + P], hn[:, j, m * P:m * P + P], k.ident[:])
                    last.then_inc(turned, 1)
                if new:
                    v = 2 * new[0] + new[1]
                    pe.wait_ge(staged, v + 1)
                    for j in range(TC):
                        for q in range(DM):
                            last = nc.tensor.matmul(k.tile_out(ps[:, 6:8], j), ys[:, q, j * P:j * P + P], W["out_W"][:, q, :],
                                                    start=(q == 0 and j != 1), stop=(q == DM - 1), skip_group_check=True)
                        last.then_inc(proj, 1)
                if old:
                    pe.wait_ge(hT_ready, DM * u + DM)
                    for m in range(4):
                        if new and m == 2:
                            pe.wait_ge(x2_ready, TC * v + TC)
                        for q in range(DM):
                            last = nc.tensor.matmul(ps[:, 4 + m, 0:CW], W["f1_W"][:, q, m * P:m * P + P], hT[:, q, :],
                                                    start=(q == 0), stop=(q == DM - 1))
                        last.then_inc(f1, 1)
                    pe.wait_ge(done, TC * u + 2 * TC)
                    pe.wait_ge(gelu, 4 * u + 4)
                    for j in range(TC):
                        for q in range(4):
                            last = nc.tensor.matmul(k.tile_out(ps, j), g[:, q, j * P:j * P + P], W["f2_W"][:, q, :],
                                                    start=(q == 0 and j != 1), stop=(q == 3), skip_group_check=True)
                        last.then_inc(f2, 1)

            overlapped(pe, NCH, 2, step)

        @block.scalar
        def _(act):
            nc.scalar.sem_inc(proj, TC)
            nc.scalar.sem_inc(f2, TC)

            def step(new, old):
                if new:
                    v = 2 * new[0] + new[1]
                    act.wait_ge(proj, TC * v + TC)
                    nc.scalar.activation(ys[:], yT[:, :, ds(CW * v, CW)], ACT.Copy).then_inc(staged, 1)
                if old:
                    u = 2 * old[0] + old[1]
                    act.wait_ge(f2, TC * u + TC)
                    for m in range(4):
                        act.wait_ge(f1, 4 * u + m + 1)
                        nc.scalar.activation(g[:, m, :], ps[:, 4 + m, 0:CW], ACT.Gelu, bias=k.vec("f1_b", m)).then_inc(gelu, 1)

            overlapped(act, NCH, 2, step)

        @block.vector
        def _(dve):
            nc.vector.sem_inc(turned, 1)

            def statistics(u):
                s = Steps(dve, hsteps, u, 2 * TC + 1)
                dve.wait_ge(done, TC * u + 3 * TC)
                k.passed(nc.vector)
                for j in range(TC):
                    s(nc.vector.bn_stats(hst[:, j, :], k.H[:, ds(TC * u + j, 1), :]))
                s.wait()
                k.passed(nc.vector)
                for j in range(TC):
                    s(nc.vector.bn_aggr(hmv[:, j, :], hst[:, j, :]))
                s.wait()
                s(nc.vector.tensor_copy(k.meanvar[:, ds(TC * u, TC), :], hmv[:]))
                s.wait()
                s.end()

            def step(new, old):
                if old:
                    u = 2 * old[0] + old[1]
                    dve.wait_ge(turned, u + 2)
                    for m in range(DM):
                        nc.vector.tensor_scalar(hT[:, m, :], ps[:, 2 + m, 0:CW], k.vec("ln2_g", m), k.vec("ln2_b", m),
                                                ALU.mult, ALU.add).then_inc(hT_ready, 1)
                if new:
                    v, p = 2 * new[0] + new[1], new[1]
                    for j in range(TC):
                        dve.wait_ge(xb_ready, TC * v + j + 1)
                        dve.wait_ge(proj, TC * v + TC + max(j, 1) + 1)
                        nc.vector.scalar_tensor_tensor(x2[:, p, j, :], k.tile_out(ps[:, 6:8], j), 0.5, xb[:, j, :],
                                                       ALU.mult, ALU.add).then_inc(x2_ready, 1)
                    s = Steps(dve, steps, v, 2 * TC)
                    dve.wait_ge(x2_ready, TC * v + TC)
                    for j in range(TC):
                        s(nc.vector.bn_stats(st[:, j, :], x2[:, p, j, :]))
                    s.wait()
                    k.passed(nc.vector)
                    for j in range(TC):
                        s(nc.vector.bn_aggr(mv[:, j, :], st[:, j, :]))
                    s.wait()
                    s.end()
                    nc.vector.tensor_scalar(ve[:], mv[:, :, 1], EPS, None, ALU.add).then_inc(var, 1)
                    dve.wait_ge(rstd, v + 1)
                    dve.wait_ge(turned, v + 1)
                    for j in range(TC):
                        nc.vector.tensor_scalar(hn[:, j, :], x2[:, p, j, :], mv[:, j, 0:1], rs[:, j:j + 1],
                                                ALU.subtract, ALU.mult).then_inc(hn_ready, 1)
                if old:
                    if old[1] == 1:
                        statistics(u - 1)
                    for j in range(TC):
                        dve.wait_ge(hx_ready, TC * u + j + 1)
                        dve.wait_ge(f2, TC * u + TC + max(j, 1) + 1)
                        nc.vector.tensor_tensor(k.H[:, ds(TC * u + j, 1), :], k.tile_out(ps, j), hx[:, old[1], j, :],
                                                ALU.add).then_inc(done, 1)
                    if old[1] == 1:
                        statistics(u)

            overlapped(dve, NCH, 2, step)


def quant_rows(k, ps, xqT, dq):
    nc = k.nc
    with stage(k) as c:
        ve = k.sb(c, "s5_var_eps", [P, NT])
        rs = k.sb(c, "s5_rstd", [P, NT])
        xs = k.sb(c, "s5_x", [P, TC, D])
        am = k.sb(c, "s5_absmax", [P, TC])
        rec = k.sb(c, "s5_inv_absmax", [P, TC])
        xq = k.sb(c, "s5_xq", [P, TC, D], BF16)
        steps, var, rstd = k.sem("s5_steps"), k.sem("s5_var"), k.sem("s5_rstd_ready")
        quant, turned, stored = k.sem("s5_quant"), k.sem("s5_turned"), k.sem("s5_stored")
        block = c.enter_context(nc.Block())
        tp = ps[:, 0, :].bitcast(BF16)[:, 0:DM * CW].rearrange("p (m t) -> p m t", m=DM)

        @block.vector
        def _(dve):
            nc.vector.sem_inc(turned, 1)
            nc.vector.sem_inc(quant, 1)
            nc.vector.tensor_scalar(ve[:], k.meanvar[:, :, 1], EPS, None, ALU.add).then_inc(var, 1)
            dve.wait_ge(rstd, 1)
            with dve.Fori(0, NCH) as i:
                s = Steps(dve, steps, i, 2 * TC + 5)
                dve.wait_ge(quant, i + 1)
                for j in range(TC):
                    t = TC * i + j
                    s(nc.vector.tensor_scalar(xs[:, j, :], k.H[:, ds(t, 1), :], k.meanvar[:, ds(t, 1), 0],
                                              rs[:, ds(t, 1)], ALU.subtract, ALU.mult))
                s.wait()
                s(nc.vector.tensor_reduce(am[:], xs[:], AX.X, ALU.max, apply_absolute_value=True))
                s.wait()
                s(nc.vector.tensor_scalar(am[:], am[:], 1e-5, None, ALU.max))
                s.wait()
                s(nc.vector.reciprocal(rec[:], am[:]))
                s(nc.vector.tensor_scalar(dq[:, ds(TC * i, TC)], am[:], 1.0 / 127.0, None, ALU.mult))
                s.wait()
                s(nc.vector.tensor_scalar(rec[:], rec[:], 127.0, None, ALU.mult))
                s.wait()
                for j in range(TC):
                    s(nc.vector.tensor_scalar(xs[:, j, :], xs[:, j, :], rec[:, j:j + 1], MAGIC, ALU.mult, ALU.add))
                s.wait()
                dve.wait_ge(turned, i + 1)
                nc.vector.tensor_scalar(xq[:], xs[:], MAGIC, 127.0, ALU.subtract, ALU.min).then_inc(quant, 1)
                s.end()

        @block.gpsimd
        def _(pool):
            pool.wait_ge(var, 1)
            nc.gpsimd.tensor_tensor(rs[:], ve[:], k.mhalf[:, 0:NT], ALU.pow).then_inc(rstd, 1)

        @block.tensor
        def _(pe):
            nc.tensor.sem_inc(stored, 1)
            with pe.Fori(0, NCH) as i:
                pe.wait_ge(stored, i + 1)
                pe.wait_ge(quant, i + 2)
                for j in range(TC):
                    for m in range(DM):
                        last = nc.tensor.transpose(tp[:, m, j * P:j * P + P], xq[:, j, m * P:m * P + P], k.identb[:])
                last.then_inc(turned, 1)

        @block.scalar
        def _(act):
            with act.Fori(0, NCH) as i:
                act.wait_ge(turned, i + 2)
                nc.scalar.activation(xqT[:, :, ds(CW * i, CW)], tp, ACT.Copy).then_inc(stored, 1)


def ternary_ffn(k, ps, xqT, dq):
    nc = k.nc
    with stage(k) as c:
        dqg = k.sb(c, "s5_gate_scale", [P, NT])
        dqu = k.sb(c, "s5_up_scale", [P, NT])
        sg = k.sb(c, "s5_silu", [P, 2, INNER])
        g = k.sb(c, "s5_g", [P, 2, INNER])
        gq = k.sb(c, "s5_gq", [P, 2, INNER], BF16)
        gqT = k.sb(c, "s5_gqT", [P, 2, FM, P], BF16)
        am = k.sb(c, "s5_g_absmax", [P, 2])
        rec = k.sb(c, "s5_g_inv_absmax", [P, 2])
        dqd = k.sb(c, "s5_down_scale", [P, NT])
        names = ("scales", "gate", "up", "silu", "g", "steps", "rec", "scaled", "gq", "turned", "gqT", "down", "done")
        (scales, gate, up, silu, g_ready, steps, rec_ready, scaled, gq_ready, turned, gqT_ready, down,
         done) = (k.sem("s5b_" + n) for n in names)
        block = c.enter_context(nc.Block())
        tp = [ps[:, 4 + p, :].bitcast(BF16).rearrange("p (m t) -> p m t", m=FM) for p in range(2)]

        @block.tensor
        def _(pe):
            nc.tensor.sem_inc(silu, 2)
            nc.tensor.sem_inc(g_ready, 2)
            nc.tensor.sem_inc(done, 2)

            def front(i, p):
                t = 2 * i + p
                for h in range(2):
                    pe.wait_ge(silu, 2 * t + h + 1)
                    for q in range(DM):
                        last = nc.tensor.matmul(ps[:, 2 * h, :], xqT[:, q, ds(P * t, P)],
                                                k.wq["w_gate"][:, q, 512 * h:512 * h + 512],
                                                start=(q == 0), stop=(q == DM - 1))
                    last.then_inc(gate, 1)
                    pe.wait_ge(g_ready, 2 * t + h + 1)
                    for q in range(DM):
                        last = nc.tensor.matmul(ps[:, 2 * h + 1, :], xqT[:, q, ds(P * t, P)],
                                                k.wq["w_up"][:, q, 512 * h:512 * h + 512],
                                                start=(q == 0), stop=(q == DM - 1))
                    last.then_inc(up, 1)

            def back(i, p):
                t = 2 * i + p
                pe.wait_ge(gq_ready, t + 3)
                for m in range(FM):
                    last = nc.tensor.transpose(tp[p][:, m, :], gq[:, p, m * P:m * P + P], k.identb[:])
                last.then_inc(turned, 1)
                pe.wait_ge(gqT_ready, t + 1)
                pe.wait_ge(done, t + 1)
                for m in range(FM):
                    last = nc.tensor.matmul(ps[:, 6 + p, 0:D], gqT[:, p, m, :], k.wq["w_down"][:, m, :],
                                            start=(m == 0), stop=(m == FM - 1))
                last.then_inc(down, 1)

            def step(new, middle, old):
                if new:
                    front(*new)
                if old:
                    back(*old)

            overlapped_twice(pe, NT, step)

        @block.scalar
        def _(act):
            act.wait_ge(scales, 2)

            def front(i, p):
                t = 2 * i + p
                for h in range(2):
                    act.wait_ge(gate, 2 * t + h + 1)
                    act.wait_ge(g_ready, 2 * t + h + 1)
                    k.passed(nc.scalar)
                    nc.scalar.activation(sg[:, p, 512 * h:512 * h + 512], ps[:, 2 * h, :], ACT.Silu,
                                         scale=dqg[:, ds(t, 1)]).then_inc(silu, 1)

            def back(i, p):
                act.wait_ge(turned, 2 * i + p + 1)
                act.wait_ge(down, 2 * i + p + 1)
                nc.scalar.activation(gqT[:, p], tp[p], ACT.Copy).then_inc(gqT_ready, 1)

            def step(new, middle, old):
                if new:
                    front(*new)
                if old:
                    back(*old)
                if middle:
                    i, p = middle
                    act.wait_ge(rec_ready, 2 * i + p + 1)
                    k.passed(nc.scalar)
                    nc.scalar.activation(g[:, p, :], g[:, p, :], ACT.Copy, scale=rec[:, p:p + 1]).then_inc(scaled, 1)

            nc.scalar.sem_inc(down, 2)
            overlapped_twice(act, NT, step)

        @block.vector
        def _(dve):
            nc.vector.tensor_scalar(dqg[:], dq[:], k.wmean[:, 0:1], None, ALU.mult).then_inc(scales, 1)
            nc.vector.tensor_scalar(dqu[:], dq[:], k.wmean[:, 1:2], None, ALU.mult).then_inc(scales, 1)
            dve.wait_ge(scales, 2)

            nc.vector.sem_inc(gq_ready, 2)

            def front(i, p):
                t = 2 * i + p
                dve.wait_ge(gq_ready, t + 1)
                for h in range(2):
                    dve.wait_ge(silu, 2 * t + 2 + h + 1)
                    dve.wait_ge(up, 2 * t + h + 1)
                    cols = slice(512 * h, 512 * h + 512)
                    nc.vector.scalar_tensor_tensor(g[:, p, cols], ps[:, 2 * h + 1, :], dqu[:, ds(t, 1)], sg[:, p, cols],
                                                   ALU.mult, ALU.mult).then_inc(g_ready, 1)
                s = Steps(dve, steps, t, 4)
                dve.wait_ge(g_ready, 2 * t + 4)
                s(nc.vector.tensor_reduce(am[:, p:p + 1], g[:, p, :], AX.X, ALU.max, apply_absolute_value=True))
                s.wait()
                s(nc.vector.tensor_scalar(am[:, p:p + 1], am[:, p:p + 1], 1e-5, None, ALU.max))
                s.wait()
                s(nc.vector.reciprocal(rec[:, p:p + 1], am[:, p:p + 1]))
                s(nc.vector.tensor_scalar(dqd[:, ds(t, 1)], am[:, p:p + 1], k.wmean[:, 2:3], 1.0 / 127.0,
                                          ALU.mult, ALU.mult))
                s.wait()
                s.end()
                nc.vector.tensor_scalar(rec[:, p:p + 1], rec[:, p:p + 1], 127.0, None, ALU.mult).then_inc(rec_ready, 1)

            def rounded(i, p):
                dve.wait_ge(scaled, 2 * i + p + 1)
                nc.vector.tensor_scalar(gq[:, p, :], g[:, p, :], MAGIC, MAGIC, ALU.add, ALU.subtract).then_inc(gq_ready, 1)

            def back(i, p):
                t = 2 * i + p
                dve.wait_ge(down, t + 3)
                nc.vector.scalar_tensor_tensor(k.H[:, ds(t, 1), :], ps[:, 6 + p, 0:D], dqd[:, ds(t, 1)],
                                               k.H[:, ds(t, 1), :], ALU.mult, ALU.add).then_inc(done, 1)

            def step(new, middle, old):
                if new:
                    front(*new)
                if middle:
                    rounded(*middle)
                if old:
                    back(*old)

            overlapped_twice(dve, NT, step)


def attention_inputs(k, ps, qT, kT):
    nc = k.nc
    W = k.weights
    with stage(k) as c:
        st = k.sb(c, "s6_stats", [P, TC, 6])
        mv = k.sb(c, "s6_meanvar", [P, TC, 2])
        ve = k.sb(c, "s6_var_eps", [P, TC])
        rs = k.sb(c, "s6_rstd", [P, TC])
        xs = k.sb(c, "s6_x", [P, TC, D])
        xT = k.sb(c, "s6_xT", [P, 2, DM, CW])
        vs = k.sb(c, "s6_v", [P, 2, TC, D])
        names = ("steps", "var", "rstd", "normed", "turned", "xT", "qk", "qk_out", "v", "v_out", "kept")
        (steps, var, rstd, normed, turned, xT_ready, qk, qk_out, v_ready, v_out, kept) = (k.sem("s6_" + n) for n in names)
        v_stored = [k.sem(f"s6_v_stored{n}") for n in range(2)]
        block = c.enter_context(nc.Block())

        @block.vector
        def _(dve):
            nc.vector.sem_inc(turned, 1)
            nc.vector.sem_inc(kept, 1)
            for n in range(2):
                nc.vector.sem_inc(v_stored[n], 16)

            def step(new, old):
                if new:
                    v = 2 * new[0] + new[1]
                    s = Steps(dve, steps, v, 2 * TC)
                    for j in range(TC):
                        s(nc.vector.bn_stats(st[:, j, :], k.H[:, ds(TC * v + j, 1), :]))
                    s.wait()
                    k.passed(nc.vector)
                    for j in range(TC):
                        s(nc.vector.bn_aggr(mv[:, j, :], st[:, j, :]))
                    s.wait()
                    s.end()
                    nc.vector.tensor_scalar(ve[:], mv[:, :, 1], EPS, None, ALU.add).then_inc(var, 1)
                    dve.wait_ge(rstd, v + 1)
                    dve.wait_ge(turned, v + 1)
                    dve.wait_ge(kept, v + 1)
                    for j in range(TC):
                        nc.vector.tensor_scalar(xs[:, j, :], k.H[:, ds(TC * v + j, 1), :],
                                                mv[:, j, 0:1], rs[:, j:j + 1], ALU.subtract, ALU.mult).then_inc(normed, 1)
                if old:
                    u, n = 2 * old[0] + old[1], old[1]
                    dve.wait_ge(v_stored[n], 16 * old[0] + 16)
                    for j in range(TC):
                        dve.wait_ge(v_ready, TC * u + max(j, 1) + 1)
                        nc.vector.tensor_tensor(vs[:, n, j, :], k.tile_out(ps[:, 6:8], j), k.row("bv"),
                                                ALU.add).then_inc(v_out, 1)

            overlapped(dve, NCH, 2, step)

        @block.gpsimd
        def _(pool):
            with pool.Fori(0, NCH) as i:
                pool.wait_ge(var, i + 1)
                nc.gpsimd.tensor_tensor(rs[:], ve[:], k.mhalf[:, 0:TC], ALU.pow).then_inc(rstd, 1)
                pool.wait_ge(normed, TC * i + TC)
                nc.gpsimd.tensor_copy(k.X[:, ds(TC * i, TC), :], xs[:]).then_inc(kept, 1)

        @block.tensor
        def _(pe):
            nc.tensor.sem_inc(v_out, TC)
            nc.tensor.sem_inc(qk_out, 4)
            nc.tensor.sem_inc(xT_ready, DM)

            def step(new, old):
                if old:
                    u = 2 * old[0] + old[1]
                    pe.wait_ge(qk_out, 4 * u + 4)
                    for n, w in enumerate(("Wq", "Wk")):
                        for m in range(DM):
                            for q in range(DM):
                                last = nc.tensor.matmul(ps[:, 2 + 2 * n + m, 0:CW], W[w][:, q, m * P:m * P + P],
                                                        xT[:, old[1], q, :], start=(q == 0), stop=(q == DM - 1))
                            last.then_inc(qk, 1)
                if new:
                    v = 2 * new[0] + new[1]
                    pe.wait_ge(xT_ready, DM * v + DM)
                    for j in range(TC):
                        pe.wait_ge(normed, TC * v + j + 1)
                        for m in range(DM):
                            last = nc.tensor.transpose(ps[:, m, j * P:j * P + P], xs[:, j, m * P:m * P + P], k.ident[:])
                    last.then_inc(turned, 1)
                if old:
                    pe.wait_ge(v_out, TC * u + TC)
                    for j in range(TC):
                        for q in range(DM):
                            last = nc.tensor.matmul(k.tile_out(ps[:, 6:8], j), xT[:, old[1], q, j * P:j * P + P],
                                                    W["Wv"][:, q, :], start=(q == 0 and j != 1), stop=(q == DM - 1),
                                                    skip_group_check=True)
                        last.then_inc(v_ready, 1)
                if new:
                    pe.wait_ge(xT_ready, DM * v + 2 * DM)

            overlapped(pe, NCH, 2, step)

        @block.scalar
        def _(act):
            def step(new, old):
                if old:
                    u = 2 * old[0] + old[1]
                    for m in range(DM):
                        act.wait_ge(qk, 4 * u + m + 1)
                        nc.scalar.activation(qT[:, m, ds(CW * u, CW)], ps[:, 2 + m, 0:CW], ACT.Identity, scale=0.25,
                                             bias=k.quarter_bq[:, m:m + 1]).then_inc(qk_out, 1)
                    for m in range(DM):
                        act.wait_ge(qk, 4 * u + DM + m + 1)
                        nc.scalar.activation(kT[:, m, ds(CW * u, CW)], ps[:, 4 + m, 0:CW], ACT.Identity,
                                             bias=k.vec("bk", m)).then_inc(qk_out, 1)
                if new:
                    act.wait_ge(turned, 2 * new[0] + new[1] + 2)
                    for m in range(DM):
                        nc.scalar.activation(xT[:, new[1], m, :], ps[:, m, 0:CW], ACT.Copy).then_inc(xT_ready, 1)

            overlapped(act, NCH, 2, step)

        @block.sync
        def _(sp):
            with sp.Fori(0, NCH // 2) as i:
                for n in range(2):
                    sp.wait_ge(v_out, 2 * TC * i + TC * n + 2 * TC)
                    sp.dma_start(k.v_dram.rearrange("(t p) d -> p t d", p=P)[:, ds(2 * TC * i + TC * n, TC), :],
                                 vs[:, n]).then_inc(v_stored[n], 16)
            for n in range(2):
                sp.wait_ge(v_stored[n], 16 * (NCH // 2) + 16)


def attention(k, ps, qT, kT, fT):
    nc = k.nc
    NU = 2 * B
    NV8 = HG + HG
    with stage(k) as c:
        kb = k.sb(c, "s7_key_blocks", [P, 2, NKC, P])
        vb = k.sb(c, "s7_value_blocks", [P, 2, NKC, P])
        v8 = k.sb(c, "s7_values", [P, 2, NKC, D])
        a = k.sb(c, "s7_abs", [P, 2, NKC, L])
        w = k.sb(c, "s7_ln_cauchy", [P, NKC, L])
        pw = k.sb(c, "s7_exp_and_cauchy", [P, 2, NKC, 2 * L])
        zs = k.sb(c, "s7_chunk_sums", [P, 2, 2 * L])
        mx = k.sb(c, "s7_max", [P, L])
        cm = k.sb(c, "s7_head_max", [P, 2, HG])
        nm = k.sb(c, "s7_neg_max", [HG, L], BF16)
        lz = k.sb(c, "s7_ln_sums", [P, 2 * L])
        rz = k.sb(c, "s7_inv_sums", [P, 2 * L])
        t1 = k.sb(c, "s7_softmax_part", [P, L])
        t2 = k.sb(c, "s7_cauchy_part", [P, L])
        hsel = k.sb(c, "s7_head_rows", [HG, P], BF16)
        hself = k.sb(c, "s7_head_rows_f32", [HG, P])
        hsum = k.sb(c, "s7_head_sum", [P, 2, P])
        tb = k.sb(c, "s7_tb2", [P, 2])
        tbb = k.sb(c, "s7_tb", [P, 2])
        names = ("const", "tb1", "hsel", "kb", "vb", "scores", "max", "abs", "t1", "cm", "t2", "nm", "shifted", "exp",
                 "sq", "ln", "cauchy", "exp_summed", "cauchy_summed", "sums", "lz", "rz", "parts")
        (const, tb1, hsel_ready, kb_ready, vb_ready, scores, max_ready, abs_ready, t1_ready, cm_ready, t2_ready,
         nm_ready, shifted, exp_ready, sq_ready, ln_ready, cauchy, exp_summed, cauchy_summed, sums, lz_ready, rz_ready,
         parts) = (k.sem("s7_" + n) for n in names)
        v_in = [k.sem(f"s7_v_in{n}") for n in range(2)]
        block = c.enter_context(nc.Block())

        def bank(n, j):
            return ps[:, 3 * n + j // KB, (j % KB) * L:(j % KB) * L + L]

        def banks(n):
            return ps[:, 3 * n:3 * n + 3, 0:KB * L]

        o_pw, z_p = ps[:, 6, 0:2 * L], ps[:, 6, 2 * L:3 * L]
        tr1, tr2, z_w = ps[:, 7, 0:P], ps[0:L - P, 7, P:2 * P], ps[:, 7, 2 * P:2 * P + L]
        cm_t = ps[0:HG, 7, 0:L]

        @block.sync
        def _(sp):
            sp.dma_start(hself[:], k.dram["head_rows"]).then_inc(const, 16)
            sp.dma_start(hsum[:], k.dram["head_sum"]).then_inc(const, 16)
            with sp.Fori(0, B // 2) as i:
                for n in range(2):
                    b = 2 * i + n
                    sp.wait_ge(vb_ready, 8 * i + 4 * n + 4)
                    for h in range(HG):
                        rows = slice(DH * h, DH * h + DH)
                        src = k.v_dram[ds(L * b, (NKC - 1) * DH), :].rearrange("(j m) d -> m j d", m=DH)
                        sp.dma_start(v8[rows, n, 0:NKC - 1, :], src).then_inc(v_in[n], 16)
                        sp.dma_start(v8[rows, n, NKC - 1, :],
                                     k.v_dram[ds(L * b + LAST0, DH), :]).then_inc(v_in[n], 16)

        @block.gpsimd
        def _(pool):
            nc.gpsimd.sem_inc(vb_ready, 8)
            pool.wait_ge(const, 32)
            same_head = hsum[:, 0:1, :].to_broadcast([P, NKC - 1, P])

            def over_heads(keys):
                return keys.rearrange("p (j h m) -> p j h m", h=1, m=DH)

            def keys(i, p):
                u, n, b = 4 * i + p, p % 2, 2 * i + p // 2
                pool.wait_ge(scores, u + 1)
                k.passed(nc.gpsimd)
                out = kb[:, n].rearrange("p j (h m) -> p j h m", h=HG)
                mask = hsum[:, 0:1, :].rearrange("p j (h m) -> p j h m", h=HG)
                nk = NKC - 1
                nc.gpsimd.tensor_tensor(out[:, 0:nk], over_heads(kT[:, n, ds(L * b, nk * DH)]).to_broadcast([P, nk, HG, DH]),
                                        mask.to_broadcast([P, nk, HG, DH]), ALU.mult).then_inc(kb_ready, 1)
                nc.gpsimd.tensor_tensor(out[:, nk], over_heads(kT[:, n, ds(L * b + LAST0, DH)])[:, 0].to_broadcast([P, HG, DH]),
                                        mask[:, 0], ALU.mult).then_inc(kb_ready, 1)

            def values(i, p):
                u, n, slot = 4 * i + p, p % 2, p // 2
                if n == 0:
                    pool.wait_ge(v_in[slot], 16 * NV8 * (i + 1))
                pool.wait_ge(sums, u + 1)
                cols = slice(P * n, P * n + P)
                nc.gpsimd.tensor_tensor(vb[:, n, 0:NKC - 1, :], v8[:, slot, 0:NKC - 1, cols], same_head,
                                        ALU.mult).then_inc(vb_ready, 1)
                nc.gpsimd.tensor_tensor(vb[:, n, NKC - 1, :], v8[:, slot, NKC - 1, cols], hsum[:, 1, :],
                                        ALU.mult).then_inc(vb_ready, 1)

            pipelined(pool, NU, 4, keys, values)

        @block.tensor
        def _(pe):
            nc.tensor.sem_inc(scores, 2)
            nc.tensor.sem_inc(sums, 2)
            pe.wait_ge(const, 32)
            pe.wait_ge(hsel_ready, 1)

            def score(i, p):
                u, n, b = 4 * i + p, p % 2, 2 * i + p // 2
                pe.wait_ge(kb_ready, 2 * u + 2)
                pe.wait_ge(exp_ready, u + 1)
                for j in range(NKC):
                    last = nc.tensor.matmul(bank(n, j), kb[:, n, j, :], qT[:, n, ds(L * b, L)],
                                            start=(j % KB == 0), stop=False, skip_group_check=True)
                last.then_inc(scores, 1)

            def outputs(i, p, chunks):
                u, n = 4 * i + p, p % 2
                if 0 in chunks:
                    pe.wait_ge(vb_ready, 2 * u + 10)
                    pe.wait_ge(parts, 3 * u + 3)
                    pe.wait_ge(exp_ready, u + 3)
                    pe.wait_ge(cauchy, u + 2)
                for j in chunks:
                    nc.tensor.matmul(o_pw, vb[:, n, j, :], pw[:, n, j, :], start=(j == 0), stop=(j == NKC - 1),
                                     skip_group_check=True)

            def turn_maxima(i, p):
                pe.wait_ge(max_ready, 4 * i + p + 1)
                nc.tensor.transpose(tr1, mx[:, 0:P], k.ident[:])
                nc.tensor.transpose(tr2, mx[:, P:L], k.ident[:]).then_inc(t1_ready, 1)

            def turn_head_maxima(i, p):
                pe.wait_ge(cm_ready, 2 * (4 * i + p) + 2)
                nc.tensor.transpose(cm_t[:, 0:P], cm[:, 0, :], k.ident[:])
                nc.tensor.transpose(cm_t[:, P:L], cm[0:L - P, 1, :], k.ident[0:L - P, 0:L - P]).then_inc(t2_ready, 1)

            def shift(i, p):
                u, n = 4 * i + p, p % 2
                pe.wait_ge(nm_ready, u + 1)
                pe.wait_ge(abs_ready, u + 1)
                for r in range(3):
                    last = nc.tensor.matmul(ps[:, 3 * n + r, 0:KB * L].rearrange("p (j l) -> p j l", j=KB), hsel[:],
                                            nm[:].rearrange("h (o l) -> h o l", o=1).to_broadcast([HG, KB, L]),
                                            start=False, stop=True, skip_group_check=True)
                last.then_inc(shifted, 1)

            def head_sums(i, p):
                u, n = 4 * i + p, p % 2
                pe.wait_ge(exp_summed, u + 1)
                pe.wait_ge(cauchy_summed, u + 1)
                for dst, cols in ((z_p, slice(0, L)), (z_w, slice(L, 2 * L))):
                    nc.tensor.matmul(dst, hsum[:, 0, :], zs[:, n, cols], start=(dst is z_w), stop=False,
                                     skip_group_check=True)
                    last = nc.tensor.matmul(dst, hsum[:, 1, :], pw[:, n, NKC - 1, cols], start=False, stop=True,
                                            skip_group_check=True)
                last.then_inc(sums, 1)

            def step(new, old):
                if new:
                    score(*new)
                if old:
                    outputs(*old, range(0, 4))
                if new:
                    turn_maxima(*new)
                if old:
                    outputs(*old, range(4, 7))
                if new:
                    turn_head_maxima(*new)
                if old:
                    outputs(*old, range(7, NKC))
                if new:
                    shift(*new)
                if old:
                    head_sums(*old)

            overlapped(pe, NU, 4, step)

        @block.scalar
        def _(act):
            nc.scalar.sem_inc(exp_ready, 2)
            nc.scalar.sem_inc(sq_ready, 2)
            nc.scalar.sem_inc(cauchy, 1)
            act.wait_ge(const, 32)
            nc.scalar.preload_act_table_set("natural_log_exp_and_others")
            nc.scalar.activation(hsel[:], hself[:], ACT.Copy).then_inc(hsel_ready, 1)
            act.wait_ge(tb1, 2)

            def step(new, old):
                if new:
                    u, n = 4 * new[0] + new[1], new[1] % 2
                    act.wait_ge(abs_ready, u + 1)
                    act.wait_ge(cauchy, u + 1)
                    nc.scalar.activation(w[:], a[:, n], ACT.Square, bias=k.vec("beta", n)).then_inc(sq_ready, 1)
                    act.wait_ge(sq_ready, u + 3)
                    nc.scalar.activation(w[:], w[:], ACT.Ln, bias=tb[:, n:n + 1]).then_inc(ln_ready, 1)
                    act.wait_ge(shifted, u + 1)
                    act.wait_ge(sums, u + 1)
                    nc.scalar.activation(pw[:, n, :, 0:L].rearrange("p (r j) l -> p r j l", r=3),
                                         banks(n).rearrange("p r (j l) -> p r j l", j=KB), ACT.Exp).then_inc(exp_ready, 1)
                if old:
                    u = 4 * old[0] + old[1]
                    act.wait_ge(sums, u + 3)
                    act.wait_ge(parts, 3 * u + 3)
                    nc.scalar.activation(lz[:, 0:L], z_p, ACT.Ln).then_inc(lz_ready, 1)
                    nc.scalar.activation(lz[:, L:2 * L], z_w, ACT.Ln).then_inc(lz_ready, 1)
                    act.wait_ge(lz_ready, 2 * u + 2)
                    nc.scalar.activation(rz[:], lz[:], ACT.Exp, scale=-1.0).then_inc(rz_ready, 1)
                if new:
                    u, n = 4 * new[0] + new[1], new[1] % 2
                    act.wait_ge(ln_ready, u + 1)
                    nc.scalar.activation(pw[:, n, :, L:2 * L], w[:], ACT.Exp, scale=-1.0).then_inc(cauchy, 1)

            overlapped(act, NU, 4, step)

        @block.vector
        def _(dve):
            at, bt = VEC["t"][0], VEC["beta"][0]
            nc.vector.sem_inc(parts, 3)
            nc.vector.tensor_tensor(tbb[:], k.vecs[:, at:at + 2], k.vecs[:, bt:bt + 2], ALU.mult).then_inc(tb1, 1)
            dve.wait_ge(tb1, 1)
            nc.vector.tensor_tensor(tb[:], tbb[:], tbb[:], ALU.mult).then_inc(tb1, 1)

            def chunk_sums(n, cols):
                return nc.vector.tensor_reduce(zs[:, n, cols], pw[:, n, 0:NKC - 1, cols].rearrange("p j l -> p l j"),
                                               AX.X, ALU.add)

            def step(new, old):
                if new:
                    u, n = 4 * new[0] + new[1], new[1] % 2
                    dve.wait_ge(scores, u + 3)
                    src = banks(n).rearrange("p r (j l) -> p l r j", j=KB)
                    nc.vector.tensor_reduce(mx[:], src, AX.XY, ALU.max).then_inc(max_ready, 1)
                    dve.wait_ge(sq_ready, u + 1)
                    nc.vector.tensor_scalar(a[:, n].bitcast(I32).rearrange("p (r j) l -> p r (j l)", r=3),
                                            banks(n).bitcast(I32), 0x7FFFFFFF, None, ALU.bitwise_and).then_inc(abs_ready, 1)
                    dve.wait_ge(t1_ready, u + 1)
                    nc.vector.tensor_reduce(cm[:, 0, :], tr1.rearrange("p (h m) -> p h m", h=HG), AX.X,
                                            ALU.max).then_inc(cm_ready, 1)
                    nc.vector.tensor_reduce(cm[0:L - P, 1, :], tr2.rearrange("p (h m) -> p h m", h=HG), AX.X,
                                            ALU.max).then_inc(cm_ready, 1)
                if old:
                    u, n = 4 * old[0] + old[1], old[1] % 2
                    dve.wait_ge(cauchy, u + 2)
                    chunk_sums(n, slice(L, 2 * L)).then_inc(cauchy_summed, 1)
                if new:
                    u, n = 4 * new[0] + new[1], new[1] % 2
                    dve.wait_ge(t2_ready, u + 1)
                    nc.vector.tensor_scalar(nm[:], cm_t, -1.0, None, ALU.mult).then_inc(nm_ready, 1)
                    dve.wait_ge(exp_ready, u + 3)
                    chunk_sums(n, slice(0, L)).then_inc(exp_summed, 1)
                if old:
                    u, n, b = 4 * old[0] + old[1], old[1] % 2, 2 * old[0] + old[1] // 2
                    dve.wait_ge(rz_ready, u + 1)
                    dve.wait_ge(parts, 3 * u + 3)
                    nc.vector.scalar_tensor_tensor(t1[:], o_pw[:, 0:L], 0.5, rz[:, 0:L], ALU.mult, ALU.mult).then_inc(parts, 1)
                    nc.vector.scalar_tensor_tensor(t2[:], o_pw[:, L:2 * L], 0.5, rz[:, L:2 * L], ALU.mult,
                                                   ALU.mult).then_inc(parts, 1)
                    dve.wait_ge(parts, 3 * u + 5)
                    nc.vector.tensor_tensor(fT[:, n, ds(L * b, L)], t1[:], t2[:], ALU.add).then_inc(parts, 1)

            overlapped(dve, NU, 4, step)


def attention_output(k, ps, fT):
    nc = k.nc
    W = k.weights
    with stage(k) as c:
        fs = k.sb(c, "s8_f", [P, DM, CW])
        hx = k.sb(c, "s8_hx", [P, 2, TC, D])
        y = k.sb(c, "s8_y", [P, 2, TC, D])
        st, hst = k.sb(c, "s8_stats", [P, TC, 6]), k.sb(c, "s8_h_stats", [P, TC, 6])
        mv, hmv = k.sb(c, "s8_meanvar", [P, 2, TC, 2]), k.sb(c, "s8_h_meanvar", [P, TC, 2])
        ve = k.sb(c, "s8_var_eps", [P, 2, TC])
        rs = k.sb(c, "s8_rstd", [P, 2, TC])
        names = ("staged", "hx1", "hx", "proj", "y", "steps", "hsteps", "var", "rstd", "done")
        staged, hx1, hx_ready, proj, y_ready, steps, hsteps, var, rstd, done = (k.sem("s8_" + n) for n in names)
        block = c.enter_context(nc.Block())

        @block.gpsimd
        def _(pool):
            nc.gpsimd.sem_inc(done, 2 * TC)
            with pool.Fori(0, NCH // 2) as i:
                for p in range(2):
                    u = 2 * i + p
                    pool.wait_ge(var, u + 1)
                    nc.gpsimd.tensor_tensor(rs[:, p], ve[:, p], k.mhalf[:, 0:TC], ALU.pow).then_inc(rstd, 1)
                    pool.wait_ge(done, TC * u + TC)
                    nc.gpsimd.tensor_tensor(hx[:, p], k.H[:, ds(TC * u, TC), :], k.X[:, ds(TC * u, TC), :],
                                            ALU.add).then_inc(hx1, 1)
                    pool.wait_ge(hx1, u + 1)
                    for j in range(TC):
                        nc.gpsimd.tensor_tensor(hx[:, p, j, :], hx[:, p, j, :], k.row("ln_b"), ALU.add).then_inc(hx_ready, 1)

        @block.scalar
        def _(act):
            nc.scalar.sem_inc(proj, TC)
            with act.Fori(0, NCH) as u:
                act.wait_ge(proj, TC * u + TC)
                nc.scalar.activation(fs[:], fT[:, :, ds(CW * u, CW)], ACT.Copy).then_inc(staged, 1)

        @block.tensor
        def _(pe):
            nc.tensor.sem_inc(y_ready, 2 * TC)
            with pe.Fori(0, NCH // 2) as i:
                for p in range(2):
                    u = 2 * i + p
                    pe.wait_ge(staged, u + 1)
                    pe.wait_ge(y_ready, TC * u + TC)
                    for j in range(TC):
                        for q in range(DM):
                            last = nc.tensor.matmul(k.tile_out(ps[:, 2 * p:2 * p + 2], j), fs[:, q, j * P:j * P + P],
                                                    W["Wo"][:, q, :], start=(q == 0 and j != 1), stop=(q == DM - 1),
                                                    skip_group_check=True)
                        last.then_inc(proj, 1)

        @block.vector
        def _(dve):
            def step(new, old):
                if new:
                    v, p = 2 * new[0] + new[1], new[1]
                    dve.wait_ge(done, TC * v + TC)
                    for j in range(TC):
                        dve.wait_ge(proj, TC * v + TC + max(j, 1) + 1)
                        nc.vector.tensor_tensor(y[:, p, j, :], k.tile_out(ps[:, 2 * p:2 * p + 2], j), k.row("bo"),
                                                ALU.add).then_inc(y_ready, 1)
                    s = Steps(dve, steps, v, 2 * TC)
                    dve.wait_ge(y_ready, TC * v + 3 * TC)
                    for j in range(TC):
                        s(nc.vector.bn_stats(st[:, j, :], y[:, p, j, :]))
                    s.wait()
                    k.passed(nc.vector)
                    for j in range(TC):
                        s(nc.vector.bn_aggr(mv[:, p, j, :], st[:, j, :]))
                    s.wait()
                    s.end()
                    nc.vector.tensor_scalar(ve[:, p], mv[:, p, :, 1], EPS, None, ALU.add).then_inc(var, 1)
                if old:
                    u, p = 2 * old[0] + old[1], old[1]
                    s = Steps(dve, hsteps, u, 3 * TC + 1)
                    for j in range(TC):
                        s(nc.vector.scalar_tensor_tensor(y[:, p, j, :], y[:, p, j, :], mv[:, p, j, 0:1], k.row("ln_w"),
                                                         ALU.subtract, ALU.mult))
                    s.wait()
                    dve.wait_ge(rstd, u + 1)
                    for j in range(TC):
                        dve.wait_ge(hx_ready, TC * u + j + 1)
                        nc.vector.scalar_tensor_tensor(k.H[:, ds(TC * u + j, 1), :], y[:, p, j, :], rs[:, p, j:j + 1],
                                                       hx[:, p, j, :], ALU.mult, ALU.add).then_inc(done, 1)
                    dve.wait_ge(done, TC * u + 3 * TC)
                    k.passed(nc.vector)
                    for j in range(TC):
                        s(nc.vector.bn_stats(hst[:, j, :], k.H[:, ds(TC * u + j, 1), :]))
                    s.wait()
                    k.passed(nc.vector)
                    for j in range(TC):
                        s(nc.vector.bn_aggr(hmv[:, j, :], hst[:, j, :]))
                    s.wait()
                    s(nc.vector.tensor_copy(k.meanvar[:, ds(TC * u, TC), :], hmv[:]))
                    s.wait()
                    s.end()

            overlapped(dve, NCH, 2, step)


def route(k, ps):
    nc = k.nc
    RS = 3
    with stage(k) as c:
        sb = lambda name, shape, dt=F32: k.sb(c, "s9_" + name, shape, dt)
        ve, rs = sb("var_eps", [P, NT]), sb("rstd", [P, NT])
        mean = sb("mean", [P, RS, TC])
        rstd_of = sb("rstd_of_chunk", [P, RS, TC])
        xs = sb("x", [P, RS, TC, D])
        xT = sb("xT", [P, DM, CW])
        logits, rest, found = sb("logits", [P, TC, E]), sb("logits_rest", [P, TC, E]), sb("found", [P, TC, E])
        top, which = sb("top2", [P, 2, TC]), sb("top2_index_less_8", [P, 2, TC])
        ex, den, diff = sb("exp", [P, TC]), sb("den", [P, TC]), sb("diff", [P, TC])
        oh = sb("one_hot", [P, 2, TC, E])
        both, before = sb("both", [P, TC, E]), sb("before", [P, TC, E])
        bothb = sb("both_bf16", [P, TC, E], BF16)
        total = sb("total", [P, TC + 1, E])
        totalb = sb("total_bf16", [P, TC, E], BF16)
        triub, onesb = sb("triu_bf16", [P, P], BF16), sb("ones_bf16", [P, P], BF16)
        junk = sb("junk", [P, 2, TC, E])
        rank, keep, slot, trash = (sb(n, [P, 2, TC]) for n in ("rank", "keep", "slot", "trash"))
        iota, iota8, pair = sb("iota", [P, E]), sb("iota_less_8", [P, E]), sb("pair", [P, NT, 2])
        valid = sb("valid", [P, NT])
        to = sb("scatter_index", [P, RS, TC, 2], I32)
        names = ("consts", "init", "steps", "bsteps", "rstd", "xs", "turned", "xT", "logits", "logits_out",
                 "diff", "exp", "both", "rank", "to", "xs_free")
        (consts, init, steps, bsteps, rstd, xs_ready, turned, xT_ready, logits_ready, logits_out, diff_ready,
         exp_ready, both_ready, rank_ready, to_ready, xs_free) = (k.sem("s9_" + n) for n in names)
        scattered = [k.sem(f"s9_scattered{n}") for n in range(RS)]
        w1_in, w2_in, w1_high = k.sem("s9_w1_in"), k.sem("s9_w2_in"), k.sem("s9_w1_high")
        block = c.enter_context(nc.Block())

        def over_experts(x):
            return x.rearrange("p (t e) -> p t e", e=1).to_broadcast([P, TC, E])

        def over_tiles(x):
            return x.rearrange("p (t e) -> p t e", t=1).to_broadcast([P, TC, E])

        def over_pair(x):
            return x.rearrange("p (j t) -> p j t", j=1).to_broadcast([P, 2, TC])

        @block.sync
        def _(sp):
            sp.dma_start(iota[:], k.dram["iota"]).then_inc(consts, 16)
            sp.dma_start(pair[:], k.dram["pair"]).then_inc(consts, 16)
            sp.dma_start(valid[:], k.dram["valid"]).then_inc(consts, 16)
            sp.dma_start(k.w1[:], k.dram["w1"][:, 0:1]).then_inc(w1_in, 16)
            sp.dma_start(k.w2[:], k.dram["w2"][:, 0:1]).then_inc(w2_in, 16)
            sp.sem_inc(xs_free, RS)
            with sp.Fori(0, NCH // RS) as i:
                for p in range(RS):
                    sp.wait_ge(scattered[p], 32 * TC * i + 32 * TC)
                    sp.sem_inc(xs_free, 1)
            sp.wait_ge(w2_in, 16)

        @block.vector
        def _(dve):
            s = Steps(dve, init)
            dve.wait_ge(consts, 48)
            s(nc.vector.tensor_copy(triub[:], k.triu[:]))
            s(nc.vector.memset(onesb[:], 1.0))
            s(nc.vector.memset(total[:], 0.0))
            s(nc.vector.tensor_scalar(iota8[:], iota[:], float(-E), None, ALU.add))
            s(nc.vector.tensor_scalar(ve[:], k.meanvar[:, :, 1], EPS, None, ALU.add))
            s.wait()
            dve.wait_ge(rstd, 1)

            def front(i, p):
                u = RS * i + p
                h = k.H[:, ds(TC * u, TC), :]
                s = Steps(dve, steps, u, 3)
                s(nc.vector.tensor_copy(mean[:, p], k.meanvar[:, ds(TC * u, TC), 0]))
                s(nc.vector.tensor_copy(rstd_of[:, p], rs[:, ds(TC * u, TC)]))
                s.wait()
                dve.wait_ge(xs_free, u + 1)
                for j in range(TC):
                    nc.vector.tensor_scalar(xs[:, p, j, :], k.H[:, ds(TC * u + j, 1), :], mean[:, p, j:j + 1],
                                            rstd_of[:, p, j:j + 1], ALU.subtract, ALU.mult).then_inc(xs_ready, 1)
                dve.wait_ge(xs_ready, TC * u + TC)
                s(nc.vector.tensor_tensor(h, h, xs[:, p], ALU.add))
                s.end()

            def back(i, p):
                u = RS * i + p
                tiles = ds(TC * u, TC)
                s = Steps(dve, bsteps, u, 34)
                dve.wait_ge(logits_ready, u + 1)
                nc.vector.tensor_copy(logits[:], ps[:, 2 + p, 0:TC * E]).then_inc(logits_out, 1)
                dve.wait_ge(logits_out, u + 3)
                for j, x in enumerate((logits, rest)):
                    s(nc.vector.tensor_reduce(top[:, j, :], x[:], AX.X, ALU.max))
                    s.wait()
                    s(nc.vector.tensor_tensor(found[:], x[:], over_experts(top[:, j, :]), ALU.is_equal))
                    s.wait()
                    s(nc.vector.scalar_tensor_tensor(found[:], found[:], float(-E), over_tiles(iota[:]), ALU.mult, ALU.add))
                    s.wait()
                    s(nc.vector.tensor_reduce(which[:, j, :], found[:], AX.X, ALU.min))
                    s.wait()
                    s(nc.vector.tensor_tensor(oh[:, j], over_tiles(iota8[:]), over_experts(which[:, j, :]), ALU.is_equal))
                    s.wait()
                    if j == 0:
                        s(nc.vector.scalar_tensor_tensor(rest[:], oh[:, 0], -3e38, logits[:], ALU.mult, ALU.add))
                        s.wait()
                nc.vector.tensor_tensor(diff[:], top[:, 1, :], top[:, 0, :], ALU.subtract).then_inc(diff_ready, 1)
                for j in range(2):
                    s(nc.vector.tensor_tensor(oh[:, j], oh[:, j], valid[:, tiles].rearrange("p (t e) -> p t e", e=1)
                                              .to_broadcast([P, TC, E]), ALU.mult))
                s.wait()
                s(nc.vector.tensor_tensor(both[:], oh[:, 0], oh[:, 1], ALU.add))
                s.wait()
                s(nc.vector.tensor_copy(bothb[:], both[:]))
                for j in range(TC):
                    s(nc.vector.tensor_tensor(total[:, j + 1, :], total[:, j, :], both[:, j, :], ALU.add))
                    s.wait()
                nc.vector.tensor_copy(totalb[:], total[:, 0:TC, :]).then_inc(both_ready, 1)
                dve.wait_ge(both_ready, u + 1)
                s(nc.vector.tensor_copy(total[:, 0, :], total[:, TC, :]))
                dve.wait_ge(exp_ready, u + 1)
                s(nc.vector.tensor_scalar(den[:], ex[:], 1.0, None, ALU.add))
                s.wait()
                s(nc.vector.reciprocal(k.prob[:, 0, tiles], den[:]))
                s.wait()
                s(nc.vector.tensor_tensor(k.prob[:, 1, tiles], k.prob[:, 0, tiles], ex[:], ALU.mult))
                dve.wait_ge(rank_ready, u + 1)
                s(nc.vector.tensor_copy(before[:], ps[:, 5, 0:TC * E]))
                s.wait()
                for j in range(2):
                    s(nc.vector.tensor_tensor(junk[:, j], before[:], oh[:, j], ALU.mult))
                s.wait()
                s(nc.vector.tensor_reduce(rank[:], junk[:], AX.X, ALU.add))
                s.wait()
                s(nc.vector.tensor_scalar(keep[:], rank[:], float(CAP), None, ALU.is_lt))
                s(nc.vector.tensor_scalar(slot[:], rank[:], float(CAP - 1), float(E * CAPP), ALU.min, ALU.add))
                s.wait()
                s(nc.vector.scalar_tensor_tensor(slot[:], which[:], float(CAPP), slot[:], ALU.mult, ALU.add))
                s(nc.vector.tensor_tensor(keep[:], keep[:], over_pair(valid[:, tiles]), ALU.mult))
                s.wait()
                own = pair[:, tiles, :].rearrange("p t j -> p j t")
                s(nc.vector.tensor_tensor(k.prob[:, :, tiles], k.prob[:, :, tiles], keep[:], ALU.mult))
                s(nc.vector.tensor_tensor(trash[:], slot[:], own, ALU.subtract))
                s(nc.vector.tensor_copy(k.source[:, tiles, :].rearrange("p t j -> p j t"), slot[:]))
                s.wait()
                s(nc.vector.tensor_tensor(trash[:], trash[:], keep[:], ALU.mult))
                s.wait()
                nc.vector.tensor_tensor(to[:, p].rearrange("p t j -> p j t"), trash[:], own, ALU.add).then_inc(to_ready, 1)
                s.end()

            pipelined(dve, NCH, RS, front, back)
            dve.wait_ge(w1_in, 16)
            nc.vector.tensor_copy(k.w1_high[:], k.w1[:]).then_inc(w1_high, 1)
            dve.wait_ge(w1_high, 1)
            nc.vector.tensor_tensor(k.w1_low[:], k.w1[:], k.w1_high[:].bitcast(F32), ALU.subtract)

        @block.gpsimd
        def _(pool):
            pool.wait_ge(init, 5)
            nc.gpsimd.tensor_tensor(rs[:], ve[:], k.mhalf[:, 0:NT], ALU.pow).then_inc(rstd, 1)
            pool.wait_ge(k.zero_filled, 16 * k.fills)
            with pool.Fori(0, NCH // RS) as i:
                for p in range(RS):
                    pool.wait_ge(to_ready, RS * i + p + 1)
                    k.passed(nc.gpsimd)
                    for t in range(TC):
                        for j in range(2):
                            nc.gpsimd.indirect_dma_start(
                                k.slots_dram, bass.IndirectOffsetOnAxis(ap=to[:, p, t, j:j + 1], axis=0),
                                xs[:, p, t, :], None).then_inc(scattered[p], 16)
            for n in range(RS):
                pool.wait_ge(scattered[n], 32 * TC * (NCH // RS))

        @block.tensor
        def _(pe):
            pe.wait_ge(init, 4)
            nc.tensor.sem_inc(xT_ready, DM)
            nc.tensor.sem_inc(logits_out, 2)

            def front(i, p):
                u = RS * i + p
                pe.wait_ge(xT_ready, DM * u + DM)
                for j in range(TC):
                    pe.wait_ge(xs_ready, TC * u + j + 1)
                    for m in range(DM):
                        last = nc.tensor.transpose(ps[:, m, j * P:j * P + P], xs[:, p, j, m * P:m * P + P], k.ident[:])
                last.then_inc(turned, 1)
                pe.wait_ge(xT_ready, DM * u + 2 * DM)
                pe.wait_ge(logits_out, u + 1)
                for j in range(TC):
                    for q in range(DM):
                        last = nc.tensor.matmul(ps[:, 2 + p, j * E:j * E + E], xT[:, q, j * P:j * P + P],
                                                k.weights["router"][:, q, :], start=(j == 0 and q == 0),
                                                stop=(q == DM - 1), skip_group_check=True)
                last.then_inc(logits_ready, 1)

            def back(i, p):
                pe.wait_ge(both_ready, RS * i + p + 1)
                nc.tensor.matmul(ps[:, 5, 0:TC * E], triub[:], bothb[:].rearrange("p t e -> p (t e)"), start=True, stop=False)
                nc.tensor.matmul(ps[:, 5, 0:TC * E], onesb[:], totalb[:].rearrange("p t e -> p (t e)"), start=False,
                                 stop=True).then_inc(rank_ready, 1)

            pipelined(pe, NCH, RS, front, back)

        @block.scalar
        def _(act):
            def front(i, p):
                u = RS * i + p
                act.wait_ge(turned, u + 1)
                for m in range(DM):
                    nc.scalar.activation(xT[:, m, :], ps[:, m, 0:CW], ACT.Copy).then_inc(xT_ready, 1)

            def back(i, p):
                act.wait_ge(diff_ready, RS * i + p + 1)
                nc.scalar.activation(ex[:], diff[:], ACT.Exp).then_inc(exp_ready, 1)

            pipelined(act, NCH, RS, front, back)


def split_products(nc, out, left, right, first, final):
    for r, (x, y) in enumerate(((0, 0), (0, 1), (1, 0))):
        last = nc.tensor.matmul(out, left[x], right[y], start=(first and r == 0), stop=(final and r == 2))
    return last


def experts(k, ps):
    nc = k.nc
    with stage(k) as c:
        w1, w2, w1h, w1l = k.w1, k.w2, k.w1_high, k.w1_low
        w2h, w2l = (k.sb(c, f"s10_w2_{n}", [P, FM, D], F32R) for n in ("high", "low"))
        rows = k.sb(c, "s10_rows", [CR, 2, CT, D])
        xTh, xTl = (k.sb(c, f"s10_xT_{n}", [P, 2, DM, CAPP], F32R) for n in ("high", "low"))
        hidh, hidl = (k.sb(c, f"s10_hidden_{n}", [P, FM, CAPP], F32R) for n in ("high", "low"))
        out = k.sb(c, "s10_out", [CR, CT, D])
        HC = CAPP // 2
        RING = 4
        hid = k.sb(c, "s10_hidden", [P, RING, HC])
        r_in = [k.sem(f"s10_rows_in{n}") for n in range(2)]
        names = ("w1_in", "w2_in", "turned", "xT", "h", "hid", "w1_high", "w1_low", "w2_high", "w2_low", "y", "out")
        (w1_in, w2_in, turned, xT_ready, h_ready, hid_ready, w1_high, w1_low, w2_high, w2_low, y_ready,
         out_ready) = (k.sem("s10_" + n) for n in names)
        low_ready = [k.sem(f"s10_hidden_low{n}") for n in range(2)]
        stored = [k.sem(f"s10_stored{n}") for n in range(2)]
        block = c.enter_context(nc.Block())
        NH = 2 * FM
        TURNS = {5: 0, 7: 1, 9: 2, 11: 3}

        def group(r):
            return r % FM, slice(r // FM * HC, r // FM * HC + HC)

        def hidden_low(eng, raw, e, r):
            f, cols = group(r)
            eng.wait_ge(hid_ready, NH * e + r + 3)
            raw.tensor_tensor(hidl[:, f, cols], hid[:, r % RING, :], hidh[:, f, cols].bitcast(F32),
                              ALU.subtract).then_inc(low_ready[r % 2], 1)

        @block.sync
        def _(sp):
            def load_rows(e, n):
                src = k.slots_dram[ds(CAPP * e, CAPP), :].rearrange("(t r) d -> r t d", r=CR)
                sp.dma_start(rows[:, n], src).then_inc(r_in[n], 16)

            def period(e, n, weights, more_rows):
                if more_rows:
                    sp.wait_ge(turned, 4 * e + 4)
                    load_rows(e + 2, n)
                if weights:
                    sp.wait_ge(w1_low, e + 1)
                    sp.dma_start(w1[:], k.dram["w1"][:, ds(e + 1, 1)]).then_inc(w1_in, 16)
                    sp.wait_ge(w2_low, e + 1)
                    sp.dma_start(w2[:], k.dram["w2"][:, ds(e + 1, 1)]).then_inc(w2_in, 16)
                for half in range(2):
                    sp.wait_ge(out_ready, CT * e + 3 * half + 3 + 2)
                    dst = k.outs_dram[ds(CAPP * e + 3 * CR * half, 3 * CR), :].rearrange("(t r) d -> r t d", r=CR)
                    sp.dma_start(dst, out[:, 3 * half:3 * half + 3]).then_inc(stored[half], 16)

            for n in range(2):
                load_rows(n, n)
            with sp.Fori(0, E // 2 - 1) as i:
                for n in range(2):
                    period(2 * i + n, n, True, True)
            period(E - 2, 0, True, False)
            period(E - 1, 1, False, False)
            for half in range(2):
                sp.wait_ge(stored[half], 16 * E + 16)

        @block.tensor
        def _(pe):
            nc.tensor.sem_inc(xT_ready, 4)
            nc.tensor.sem_inc(hid_ready, 2)
            nc.tensor.sem_inc(out_ready, 2)

            def turn(i, n, b):
                m, e = b // 2, 2 * i + n
                if b == 0:
                    pe.wait_ge(r_in[n], 16 * i + 16)
                pe.wait_ge(xT_ready, 8 * e + 2 * b + 2)
                for j in range(3):
                    t = 3 * (b % 2) + j
                    last = nc.tensor.transpose(ps[:, b % 2, j * CR:j * CR + CR], rows[:, n, t, m * P:m * P + P],
                                               k.ident[0:CR, 0:CR])
                last.then_inc(turned, 1)

            def step(new, old):
                if not old:
                    for b in range(4):
                        turn(*new, b)
                    return
                n, e = old[1], 2 * old[0] + old[1]
                pe.wait_ge(w1_low, e + 1)
                pe.wait_ge(xT_ready, 8 * e + 12)
                for r in range(NH):
                    f, sl = group(r)
                    pe.wait_ge(hid_ready, NH * e + r + 1)
                    for q in range(DM):
                        cols = slice(f * P, f * P + P)
                        last = split_products(nc, ps[:, 2 + r % 2, 0:HC], (w1h[:, q, cols], w1l[:, q, cols]),
                                              (xTh[:, n, q, sl], xTl[:, n, q, sl]), q == 0, q == DM - 1)
                    last.then_inc(h_ready, 1)
                    if new and r in TURNS:
                        turn(*new, TURNS[r])
                pe.wait_ge(w2_low, e + 1)
                for t in range(CT):
                    if t % 3 == 0:
                        for low in low_ready:
                            pe.wait_ge(low, FM * e + FM // 2 * (t // 3 + 1) + 2)
                    pe.wait_ge(out_ready, CT * e + t + 1)
                    for f in range(FM):
                        sl = slice(t * CR, t * CR + CR)
                        last = split_products(nc, ps[0:CR, 4 + t % 2, 0:D], (hidh[:, f, sl], hidl[:, f, sl]),
                                              (w2h[:, f, :], w2l[:, f, :]), f == 0, f == FM - 1)
                    last.then_inc(y_ready, 1)

            overlapped(pe, E, 2, step)

        @block.scalar
        def _(act):
            nc.scalar.sem_inc(y_ready, CT)
            for low in low_ready:
                nc.scalar.sem_inc(low, 2)
            nc.scalar.sem_inc(w2_in, 16)

            def step(new, old):
                if not old:
                    return
                e = 2 * old[0] + old[1]
                for r in range(NH):
                    f, cols = group(r)
                    if f == 0:
                        act.wait_ge(y_ready, CT * e + 3 * (r // FM) + 3)
                    act.wait_ge(low_ready[r % 2], FM * e + r // 2 + 1)
                    act.wait_ge(h_ready, NH * e + r + 1)
                    nc.scalar.activation(hid[:, r % RING, :], ps[:, 2 + r % 2, 0:HC], ACT.Silu)
                    nc.scalar.activation(hidh[:, f, cols], ps[:, 2 + r % 2, 0:HC], ACT.Silu).then_inc(hid_ready, 1)
                    if r == 2:
                        act.wait_ge(y_ready, CT * e + CT)
                        act.wait_ge(w2_in, 16 * e + 16)
                        nc.scalar.activation(w2h[:], w2[:], ACT.Copy).then_inc(w2_high, 1)
                if new:
                    act.wait_ge(h_ready, NH * e + NH)
                    act.wait_ge(w1_in, 16 * e + 16)
                    nc.scalar.activation(w1h[:], w1[:], ACT.Copy).then_inc(w1_high, 1)

            overlapped(act, E, 2, step)

        @block.vector
        def _(dve):
            for n in range(2):
                nc.vector.sem_inc(stored[n], 16)

            def turned_rows(i, n, b):
                e, m = 2 * i + n, b // 2
                cols = slice((b % 2) * HC, (b % 2) * HC + HC)
                dve.wait_ge(turned, 4 * e + b + 1)
                nc.vector.tensor_copy(xTh[:, n, m, cols], ps[:, b % 2, 0:HC]).then_inc(xT_ready, 1)
                dve.wait_ge(xT_ready, 8 * e + 2 * b + 5)
                nc.vector.tensor_tensor(xTl[:, n, m, cols], ps[:, b % 2, 0:HC], xTh[:, n, m, cols].bitcast(F32),
                                        ALU.subtract).then_inc(xT_ready, 1)

            def step(new, old):
                if not old:
                    for b in range(4):
                        turned_rows(*new, b)
                    return
                e = 2 * old[0] + old[1]
                for r in range(NH):
                    if r % 2 == 1:
                        hidden_low(dve, nc.vector, e, r)
                    if new and r in TURNS:
                        turned_rows(*new, TURNS[r])
                    if r == 3:
                        dve.wait_ge(w2_high, e + 1)
                        nc.vector.tensor_tensor(w2l[:], w2[:], w2h[:].bitcast(F32), ALU.subtract).then_inc(w2_low, 1)
                for t in range(CT):
                    if t % 3 == 0:
                        dve.wait_ge(stored[t // 3], 16 * e + 16)
                    dve.wait_ge(y_ready, CT * e + CT + t + 1)
                    nc.vector.tensor_copy(out[:, t, :], ps[0:CR, 4 + t % 2, 0:D]).then_inc(out_ready, 1)

            overlapped(dve, E, 2, step)

        @block.gpsimd
        def _(pool):
            nc.gpsimd.sem_inc(w1_low, 1)

            def step(new, old):
                if not old:
                    return
                e = 2 * old[0] + old[1]
                for r in range(0, NH, 2):
                    hidden_low(pool, nc.gpsimd, e, r)
                if new:
                    pool.wait_ge(w1_high, e + 1)
                    nc.gpsimd.tensor_tensor(w1l[:], w1[:], w1h[:].bitcast(F32), ALU.subtract).then_inc(w1_low, 1)

            overlapped(pool, E, 2, step)


def combine(k):
    nc = k.nc
    with stage(k) as c:
        g = k.sb(c, "s11_rows", [P, NCH, TC, 2, D])
        y = k.sb(c, "s11_y", [P, 2, TC, D])
        mixed, done = k.sem("s11_mixed"), k.sem("s11_done")
        got = [k.sem(f"s11_got{n}") for n in range(NCH)]
        stored = [k.sem(f"s11_stored{n}") for n in range(2)]
        block = c.enter_context(nc.Block())

        @block.gpsimd
        def _(pool):
            for n in range(NCH):
                for t in range(TC):
                    for j in range(2):
                        at = TC * n + t
                        nc.gpsimd.indirect_dma_start(
                            g[:, n, t, j, :], None, k.outs_dram,
                            bass.IndirectOffsetOnAxis(ap=k.source[:, at, j:j + 1], axis=0)).then_inc(got[n], 16)

        @block.vector
        def _(dve):
            for n in range(NCH):
                dve.wait_ge(got[n], 32 * TC)
                if n >= 2:
                    dve.wait_ge(stored[n % 2], 16 * (n // 2))
                for j in range(TC):
                    t = TC * n + j
                    nc.vector.scalar_tensor_tensor(y[:, n % 2, j, :], g[:, n, j, 0, :], k.prob[:, 0, t:t + 1],
                                                   k.H[:, t, :], ALU.mult, ALU.add).then_inc(mixed, 1)
                dve.wait_ge(mixed, TC * n + TC)
                for j in range(TC):
                    t = TC * n + j
                    nc.vector.scalar_tensor_tensor(y[:, n % 2, j, :], g[:, n, j, 1, :], k.prob[:, 1, t:t + 1],
                                                   y[:, n % 2, j, :], ALU.mult, ALU.add).then_inc(done, 1)

        @block.sync
        def _(sp):
            out = k.out.rearrange("(t p) d -> p t d", p=P)
            for n in range(NCH):
                sp.wait_ge(done, TC * n + TC)
                sp.dma_start(out[:, TC * n:TC * n + TC, :], y[:, n % 2]).then_inc(stored[n % 2], 16)
            for n in range(2):
                sp.wait_ge(stored[n], 16 * (NCH // 2))


WEIGHTS = {"in_W": (DM, 2 * D), "dt_W": (DM, D), "b_W": (DM, D), "c_W": (DM, D), "out_W": (DM, D),
           "f1_W": (DM, F1), "f2_W": (F1 // P, D), "Wq": (DM, D), "Wk": (DM, D), "Wv": (DM, D), "Wo": (DM, D),
           "router": (DM, E)}


LATE = ("Wq", "Wk", "Wv", "Wo", "router")


def program(nc, dram, out):
    with ExitStack() as ctx:
        k = Core(nc, dram, ctx)
        k.out = out
        k.H = k.sb(ctx, "H", [P, NT, D])
        k.X = k.sb(ctx, "X", [P, NT, D])
        k.vecs = k.sb(ctx, "vecs_sb", [P, NV])
        k.rows = k.sb(ctx, "rows_sb", [P, len(ROWS), D])
        k.ident = k.sb(ctx, "ident_sb", [P, P])
        k.identb = k.sb(ctx, "ident_bf16", [P, P], BF16)
        k.triu = k.sb(ctx, "triu_sb", [P, P])
        k.half_gate_b = k.sb(ctx, "half_gate_b", [P, DM])
        k.quarter_bq = k.sb(ctx, "quarter_bq", [P, DM])
        k.slots_dram = nc.dram_tensor("expert_rows", (SLOTS + 2 * NP, D), F32, kind="Internal").ap()
        k.outs_dram = nc.dram_tensor("expert_outputs", (SLOTS, D), F32, kind="Internal").ap()
        k.zero_filled, k.fills = k.sem("zero_filled"), E
        k.v_dram = nc.dram_tensor("values", (NP, D), F32, kind="Internal").ap()
        k.mhalf = k.sb(ctx, "minus_half", [P, 2 * NT])
        k.meanvar = k.sb(ctx, "row_meanvar", [P, NT, 2])
        k.wmean = k.sb(ctx, "mean_abs_w", [P, 3])
        k.weights = {n: k.sb(ctx, n + "_sb", [P, *WEIGHTS[n]]) for n in LATE}
        early = ctx.enter_context(ExitStack())
        k.weights |= {n: k.sb(early, n + "_sb", [P, *s]) for n, s in WEIGHTS.items() if n not in LATE}
        k.wq = {n: k.sb(early, n + "_ternary", [P, *s], BF16)
                for n, s in (("w_gate", (DM, INNER)), ("w_up", (DM, INNER)), ("w_down", (FM, D)))}
        k.const_in, k.weights_in = k.sem("const_in"), k.sem("weights_in")
        k.waits_passed = k.sem("waits_passed")
        k.row = lambda name: k.rows[:, ROWS.index(name), :]
        k.tile_out = lambda ps, j: ps[:, j // 2, (j % 2) * D:(j % 2) * D + D]
        ps = ctx.enter_context(nc.psum_tensor("ps", [P, 8, 512], F32))
        embed(k, ps)
        with ExitStack() as c:
            nxT = k.sb(c, "nxT", [P, DM, NP])
            yT = k.sb(c, "yT", [P, DM, NP])
            scan_norms(k, ps, nxT)
            with nc.Block() as block:
                @block.tensor
                def _(pe):
                    pe.wait_ge(k.weights_in, 16 * len(WEIGHTS))

                @block.gpsimd
                def _(pool):
                    nc.gpsimd.memset(yT[:, :, N:NP], 0.0)
            selective_scan(k, ps, nxT, yT)
            scan_output(k, ps, yT)
        with ExitStack() as c:
            xqT = k.sb(c, "xqT", [P, DM, NP], BF16)
            dq = k.sb(c, "row_scale", [P, NT])
            quant_rows(k, ps, xqT, dq)
            ternary_ffn(k, ps, xqT, dq)
        with ExitStack() as c:
            early.close()
            cf = c.enter_context(ExitStack())
            fT = k.sb(cf, "fT", [P, DM, NP])
            with ExitStack() as c2:
                qT = k.sb(c2, "qT", [P, DM, NP])
                kT = k.sb(c2, "kT", [P, DM, NP])
                with nc.Block() as block:
                    @block.gpsimd
                    def _(pool):
                        nc.gpsimd.memset(fT[:, :, N:NP], 0.0)

                    @block.vector
                    def _(dve):
                        at = VEC["bq"][0]
                        nc.vector.tensor_scalar(k.quarter_bq[:], k.vecs[:, at:at + 2], 0.25, None, ALU.mult)
                attention_inputs(k, ps, qT, kT)
                attention(k, ps, qT, kT, fT)
            attention_output(k, ps, fT)
            cf.close()
            k.prob = k.sb(c, "pair_weights", [P, 2, NT])
            k.source = k.sb(c, "pair_rows", [P, NT, 2], I32)
            with ExitStack() as c2:
                k.w1, k.w2 = k.sb(c2, "expert_w1", [P, DM, INNER]), k.sb(c2, "expert_w2", [P, FM, D])
                k.w1_high, k.w1_low = (k.sb(c2, f"expert_w1_{n}", [P, DM, INNER], F32R) for n in ("high", "low"))
                route(k, ps)
                experts(k, ps)
            combine(k)


def columns(v):
    import numpy as np
    return np.ascontiguousarray(v.reshape(-1, P).T)


def folded(w):
    import numpy as np
    return np.ascontiguousarray(w.reshape(-1, P, w.shape[1]).transpose(1, 0, 2))


def layout(a):
    import numpy as np
    g = {}
    x = a["x"].reshape(B, 3, 8, 16, 8, 16).transpose(1, 3, 5, 0, 2, 4).reshape(768, B * IMG)
    g["patches"] = folded(x)
    g["tok_W1"], g["tok_W2"] = folded(a["L0_tok_W1"]), folded(a["L0_tok_W2"])
    g["tok_b2"] = a["L0_tok_b2"].reshape(1, D)
    ids = np.zeros((NP,), np.int32)
    ids[:N].reshape(B, L)[:, IMG:] = a["x_txt"]
    g["tokens"] = np.ascontiguousarray(ids.reshape(NT, P).T)
    g["table"] = a["L0_txt_weight"]
    is_text = np.zeros((NP,), np.float32)
    is_text[:N].reshape(B, L)[:, IMG:] = 1.0
    is_image = np.zeros((NP,), np.float32)
    is_image[:N].reshape(B, L)[:, :IMG] = 1.0
    g["tmask"] = np.ascontiguousarray(is_text.reshape(NT, P).T)
    g["imask"] = is_image.reshape(1, NP)
    g["ident"] = np.eye(P, dtype=np.float32)
    g["triu"] = np.triu(np.ones((P, P), np.float32), 1)
    h = np.arange(P) // DH
    g["head_rows"] = (np.arange(HG)[:, None] == h[None, :]).astype(np.float32)
    same = (h[:, None] == h[None, :]).astype(np.float32)
    g["head_sum"] = np.stack([same, same * (np.arange(P) % DH >= DUP)[:, None].astype(np.float32)], 1)
    g["iota"] = np.ascontiguousarray(np.broadcast_to(np.arange(E, dtype=np.float32), (P, E)))
    token = np.arange(NP, dtype=np.float32).reshape(NT, P).T
    g["pair"] = np.ascontiguousarray(np.stack([TRASH + 2 * token, TRASH + 2 * token + 1], 2))
    g["valid"] = (token < N).astype(np.float32)
    g["w1"] = np.ascontiguousarray(a["L1_ffn_w1"].reshape(E, DM, P, INNER).transpose(2, 0, 1, 3))
    g["w2"] = np.ascontiguousarray(a["L1_ffn_w2"].reshape(E, FM, P, D).transpose(2, 0, 1, 3))
    s = "L0_attn_"
    vec = {"in_b": a[s + "in_b"], "dw0": a[s + "dw_W"][:, 0, 0], "dw1": a[s + "dw_W"][:, 0, 1],
           "dw2": a[s + "dw_W"][:, 0, 2], "tb1": a["L0_tok_b1"], "bq": a["L1_attn_bq"], "bk": a["L1_attn_bk"],
           "beta": np.repeat(a["L1_attn_beta"], DH), "t": np.repeat(a["L1_attn_t"], DH)}
    for n in ("dw_b", "dt_b", "b_b", "c_b", "a_log", "d_skip", "ln1_g", "ln1_b", "ln2_g", "ln2_b", "f1_b"):
        vec[n] = a[s + n]
    g["vecs"] = np.concatenate([columns(vec[n]) for n in VEC], 1)
    row = {"out_b": a[s + "out_b"], "f2_b": a[s + "f2_b"], "bv": a["L1_attn_bv"], "bo": a["L1_attn_bo"],
           "ln_w": a["L1_attn_ln_w"], "ln_b": a["L1_attn_ln_b"]}
    g["rows"] = np.ascontiguousarray(np.broadcast_to(np.stack([row[n] for n in ROWS]), (P, len(ROWS), D)))
    for n in ("in_W", "dt_W", "b_W", "c_W", "out_W", "f1_W", "f2_W"):
        g[n] = folded(a[s + n])
    for n in ("Wq", "Wk", "Wv", "Wo"):
        g[n] = folded(a["L1_attn_" + n].T)
    for n in FFN_WEIGHTS:
        g[n] = folded(a["L0_ffn_" + n].T)
    g["router"] = folded(a["L1_ffn_router_w"].T)
    return g


def kernel(**inputs):
    import numpy as np
    import concourse.bacc as bacc
    from concourse.bass_utils import run_bass_kernel_spmd as run

    nc = bacc.Bacc("TRN2", target_bir_lowering=False, num_devices=1)
    arrays, dram = {}, {}
    for name, a in layout({n: np.asarray(v) for n, v in inputs.items()}).items():
        a = np.ascontiguousarray(a)
        arrays[f"in_{name}_dram"] = a
        dram[name] = nc.dram_tensor(f"in_{name}_dram", a.shape, mybir.dt.from_np(a.dtype), kind="ExternalInput").ap()
    out = nc.dram_tensor("out_0_dram", (NP, D), F32, kind="ExternalOutput").ap()
    program(nc, dram, out)
    r = run(nc, [arrays], core_ids=[0])
    return r.results[0]["out_0_dram"][:N].reshape(B, L, D)
```
